# Optimizing a Trainium2 kernel written in Bass

```python
import numpy as np
import jax
import jax.numpy as jnp

def _softmax(x, axis=-1):
    return jax.nn.softmax(x, axis=axis)

def _gelu(x):
    return jax.nn.gelu(x, approximate=True)

def _silu(x):
    return jax.nn.silu(x)

def _sigmoid(x):
    return jax.nn.sigmoid(x)

def _layernorm(x, axis=-1, eps=1e-05):
    m = jnp.mean(x, axis=axis, keepdims=True)
    v = jnp.var(x, axis=axis, keepdims=True)
    return (x - m) / jnp.sqrt(v + eps)

def _scatter_add(tgt, idx, src, axis=0):
    return tgt.at[idx].add(src)

def _segment_sum(src, seg, n):
    return jax.ops.segment_sum(src, seg, n)
kernel_name = 'mk_gnn_preln_d2_gnn_r8_6b074a'

def setup_inputs(seed: int=0):
    np.random.seed(seed)
    _w = jnp.asarray

    def _rec_inputs():
        import jax
        import jax.numpy as jnp
        _gk = jax.random.key(seed)
        x = -8.776e-05 + 1 * jax.random.normal(jax.random.fold_in(_gk, 1), (1250, 512), jnp.float32)
        _s = jax.random.randint(jax.random.fold_in(_gk, 2), (10000,), 0, 1250, jnp.int32)
        _d = jax.random.randint(jax.random.fold_in(_gk, 3), (10000,), 0, 1250, jnp.int32)
        _loop = jnp.arange(1250, dtype=jnp.int32)
        src = jnp.concatenate([_s, _d, _loop])
        dst = jnp.concatenate([_d, _s, _loop])
        _o = jnp.argsort(dst, stable=True)
        src = src[_o]
        dst = dst[_o]
        edge_attr_128 = 0.000283511 + 1.00007 * jax.random.normal(jax.random.fold_in(_gk, 11), (21250, 128), jnp.float32)
        return (x, src, dst, edge_attr_128)
    x, src, dst, edge_attr_128 = _rec_inputs()

    def _L0_gnn_setup():
        import jax, jax.numpy as jnp
        import numpy as np
        N_NODES = 1250

        def sage_conv(x, src, dst, Wl, bl, Wr):
            msg = x[src]
            summed = jax.ops.segment_sum(msg, dst, num_segments=N_NODES)
            cnt = jax.ops.segment_sum(jnp.ones((src.shape[0],), x.dtype), dst, num_segments=N_NODES)
            mean = summed / jnp.maximum(cnt, 1.0)[:, None]
            return mean @ Wl.T + bl + x @ Wr.T
        key = jax.random.key(seed)
        ks = jax.random.split(key, 7)
        d = 512
        E = 20000
        x = jax.random.normal(ks[0], (N_NODES, d), jnp.float32)
        edge_index = jax.random.randint(ks[1], (2, E), 0, N_NODES, jnp.int64)
        s = 1.0 / np.sqrt(d)
        Wl0 = jax.random.normal(ks[2], (d, d), jnp.float32) * s
        bl0 = jnp.zeros((d,), jnp.float32)
        Wr0 = jax.random.normal(ks[3], (d, d), jnp.float32) * s
        Wl1 = jax.random.normal(ks[4], (d, d), jnp.float32) * s
        bl1 = jnp.zeros((d,), jnp.float32)
        Wr1 = jax.random.normal(ks[5], (d, d), jnp.float32) * s
        return {'x': x, 'edge_index': edge_index, 'Wl0': Wl0, 'bl0': bl0, 'Wr0': Wr0, 'Wl1': Wl1, 'bl1': bl1, 'Wr1': Wr1}
    _L0_gnn_all = _L0_gnn_setup()
    _L0_gnn_in = {k: v for k, v in _L0_gnn_all.items() if k in ('Wl0', 'bl0', 'Wr0', 'Wl1', 'bl1', 'Wr1')}
    del _L0_gnn_all

    def _L1_gnn_setup():
        import jax, jax.numpy as jnp
        import numpy as np
        N, E = (1250, 18750)
        HD, ED = (512, 128)
        BN_EPS = 1e-05
        key = jax.random.key(seed)
        ks = jax.random.split(key, 16)
        s = 0.02
        return {'h': jax.random.normal(ks[0], (N, HD), jnp.float32), 'edge_index': jax.random.randint(ks[1], (2, E), 0, N, jnp.int32), 'edge_attr': jax.random.normal(ks[2], (E, ED), jnp.float32), 'W1': jax.random.normal(ks[3], (HD, HD + ED), jnp.float32) * s, 'b1': jnp.zeros((HD,), jnp.float32), 'W2': jax.random.normal(ks[4], (HD, HD), jnp.float32) * s, 'b2': jnp.zeros((HD,), jnp.float32), 'W_ih': jax.random.normal(ks[5], (3 * HD, HD), jnp.float32) * s, 'W_hh': jax.random.normal(ks[6], (3 * HD, HD), jnp.float32) * s, 'b_ih': jnp.zeros((3 * HD,), jnp.float32), 'b_hh': jnp.zeros((3 * HD,), jnp.float32), 'gamma': jnp.ones((HD,), jnp.float32), 'beta': jnp.zeros((HD,), jnp.float32), 'run_mean': jnp.zeros((HD,), jnp.float32), 'run_var': jnp.ones((HD,), jnp.float32)}
    _L1_gnn_all = _L1_gnn_setup()
    _L1_gnn_in = {k: v for k, v in _L1_gnn_all.items() if k in ('W1', 'b1', 'W2', 'b2', 'W_ih', 'W_hh', 'b_ih', 'b_hh', 'gamma', 'beta', 'run_mean', 'run_var')}
    del _L1_gnn_all
    return {'x': x, 'src': src, 'dst': dst, 'edge_attr_128': edge_attr_128, 'L0_gnn_Wl0': _L0_gnn_in['Wl0'], 'L0_gnn_bl0': _L0_gnn_in['bl0'], 'L0_gnn_Wr0': _L0_gnn_in['Wr0'], 'L0_gnn_Wl1': _L0_gnn_in['Wl1'], 'L0_gnn_bl1': _L0_gnn_in['bl1'], 'L0_gnn_Wr1': _L0_gnn_in['Wr1'], 'L1_gnn_W1': _L1_gnn_in['W1'], 'L1_gnn_b1': _L1_gnn_in['b1'], 'L1_gnn_W2': _L1_gnn_in['W2'], 'L1_gnn_b2': _L1_gnn_in['b2'], 'L1_gnn_W_ih': _L1_gnn_in['W_ih'], 'L1_gnn_W_hh': _L1_gnn_in['W_hh'], 'L1_gnn_b_ih': _L1_gnn_in['b_ih'], 'L1_gnn_b_hh': _L1_gnn_in['b_hh'], 'L1_gnn_gamma': _L1_gnn_in['gamma'], 'L1_gnn_beta': _L1_gnn_in['beta'], 'L1_gnn_run_mean': _L1_gnn_in['run_mean'], 'L1_gnn_run_var': _L1_gnn_in['run_var']}

def reference(x, src, dst, edge_attr_128, L0_gnn_Wl0, L0_gnn_bl0, L0_gnn_Wr0, L0_gnn_Wl1, L0_gnn_bl1, L0_gnn_Wr1, L1_gnn_W1, L1_gnn_b1, L1_gnn_W2, L1_gnn_b2, L1_gnn_W_ih, L1_gnn_W_hh, L1_gnn_b_ih, L1_gnn_b_hh, L1_gnn_gamma, L1_gnn_beta, L1_gnn_run_mean, L1_gnn_run_var):
    import jax
    import jax.numpy as jnp

    def _L0_gnn_ref(x, edge_index, Wl0, bl0, Wr0, Wl1, bl1, Wr1):
        import jax, jax.numpy as jnp
        import numpy as np
        N_NODES = 1250

        def sage_conv(x, src, dst, Wl, bl, Wr):
            msg = x[src]
            summed = jax.ops.segment_sum(msg, dst, num_segments=N_NODES)
            cnt = jax.ops.segment_sum(jnp.ones((src.shape[0],), x.dtype), dst, num_segments=N_NODES)
            mean = summed / jnp.maximum(cnt, 1.0)[:, None]
            return mean @ Wl.T + bl + x @ Wr.T
        src, dst = (edge_index[0], edge_index[1])
        h = jax.nn.relu(sage_conv(x, src, dst, Wl0, bl0, Wr0))
        h = jax.nn.relu(sage_conv(h, src, dst, Wl1, bl1, Wr1))
        return h

    def _L1_gnn_ref(h, edge_index, edge_attr, W1, b1, W2, b2, W_ih, W_hh, b_ih, b_hh, gamma, beta, run_mean, run_var):
        import jax, jax.numpy as jnp
        import numpy as np
        N, E = (1250, 18750)
        HD, ED = (512, 128)
        BN_EPS = 1e-05
        src, dst = (edge_index[0], edge_index[1])
        m_in = jnp.concatenate([h[src], edge_attr], axis=1)
        m = jax.nn.relu(m_in @ W1.T + b1) @ W2.T + b2
        agg = jax.ops.segment_sum(m, dst, num_segments=h.shape[0])
        gi = agg @ W_ih.T + b_ih
        gh = h @ W_hh.T + b_hh
        i_r, i_z, i_n = jnp.split(gi, 3, axis=1)
        h_r, h_z, h_n = jnp.split(gh, 3, axis=1)
        r = jax.nn.sigmoid(i_r + h_r)
        z = jax.nn.sigmoid(i_z + h_z)
        n = jnp.tanh(i_n + r * h_n)
        h_new = (1.0 - z) * n + z * h
        bn = gamma * (h_new - run_mean) * jax.lax.rsqrt(run_var + BN_EPS) + beta
        return h + bn
    edge_index = jnp.stack([src, dst])
    h = jnp.maximum(_layernorm(x, axis=-1), 0.0)
    x = x + _L0_gnn_ref(h, edge_index, L0_gnn_Wl0, L0_gnn_bl0, L0_gnn_Wr0, L0_gnn_Wl1, L0_gnn_bl1, L0_gnn_Wr1)
    h = jnp.maximum(_layernorm(x, axis=-1), 0.0)
    x = x + _L1_gnn_ref(h, edge_index, edge_attr_128, L1_gnn_W1, L1_gnn_b1, L1_gnn_W2, L1_gnn_b2, L1_gnn_W_ih, L1_gnn_W_hh, L1_gnn_b_ih, L1_gnn_b_hh, L1_gnn_gamma, L1_gnn_beta, L1_gnn_run_mean, L1_gnn_run_var)
    return x

_drawn_inputs = setup_inputs


def setup_inputs(seed=0):
    import zlib

    import numpy as np

    out = dict(_drawn_inputs(seed))
    spreads = {'L0_gnn_bl0': (0.0, 0.1),
     'L0_gnn_bl1': (0.0, 0.1),
     'L1_gnn_b1': (0.0, 0.1),
     'L1_gnn_b2': (0.0, 0.1),
     'L1_gnn_b_ih': (0.0, 0.4),
     'L1_gnn_b_hh': (0.0, 0.562),
     'L1_gnn_gamma': (1.0, 0.2),
     'L1_gnn_beta': (0.0, 0.1),
     'L1_gnn_run_mean': (0.0, 0.1),
     'L1_gnn_run_var': (1.0, 0.6)}
    factors = {}
    for name, (base, spread) in spreads.items():
        noise = np.random.default_rng([zlib.crc32(name.encode()), seed]).standard_normal(out[name].shape)
        drawn = base * np.exp(spread * noise) if base else spread * noise
        out[name] = jnp.asarray(drawn.astype(out[name].dtype))
    for name, factor in factors.items():
        out[name] = (out[name] * factor).astype(out[name].dtype)
    return out
```

```python
import concourse.bass as bass
from concourse import mybir
from contextlib import ExitStack

P = 128
N = 1250
D = 512
ED = 128
E = 21250
NT = -(-N // P)
NP = NT * P
LAST = N - (NT - 1) * P
KC = D // P
ET = -(-E // P)
FULL = E // P
TAIL = E - FULL * P
U = 3
TC = 172
ROWS2 = ET - P
EPS = 1e-5

JOBS = []
for _c in range(NT):
    JOBS.append(("h", _c))
    if _c < 8:
        JOBS.append((("Wl0", "Wr0")[_c // KC], _c % KC))
for _n in range(NT):
    if _n < KC:
        JOBS.append(("Wl1", _n))
    if _n:
        JOBS.append(("g", _n - 1))
JOBS.append(("g", NT - 1))
JOBS += [("Wr1", k) for k in range(KC)]
JOBS += [("W1a", k) for k in range(KC)] + [("W1b", 0)]
JOBS += [("W2", k) for k in range(KC)]
JOBS += [("h2", n) for n in range(NT)]
JOBS += [("ih_r", k) for k in range(KC)]
JOBS += [("R", c) for c in range(NT)]
JOBS += [("hh_r", k) for k in range(KC)]
JOBS += [("ih_n", k) for k in range(KC)]
JOBS += [("hh_n", k) for k in range(KC)]
JOBS += [("ih_z", k) for k in range(KC)]
JOBS += [("hh_z", k) for k in range(KC)]
JOB = {name: i for i, name in enumerate(JOBS)}

STAGED = ["Wl0", "Wr0", "Wl1", "Wr1", "W1a", "W2", "ih_r", "hh_r", "ih_n", "hh_n", "ih_z", "hh_z"]
LAST_JOB = {w: JOB[(w, KC - 1)] for w in STAGED}
LAST_JOB["W1a"] = JOB[("W1b", 0)]
SLOT = {"Wl0": "A", "Wr0": "B", "Wl1": "A", "Wr1": "B", "W1a": "A", "W1b": "E", "W2": "B", "ih_r": "A",
        "hh_r": "C", "ih_n": "B", "hh_n": "A", "ih_z": "C", "hh_z": "B"}


def build_gnn(nc, x, src, dst, edge_attr, Wl0, bl0, Wr0, Wl1, bl1, Wr1, W1, b1, W2, b2, W_ih, W_hh,
              b_ih, b_hh, gamma, beta, run_mean, run_var, out, p_table, h_stash, xh_stash):
    f32, f32r, f16, i32 = mybir.dt.float32, mybir.dt.float32r, mybir.dt.float16, mybir.dt.int32
    ALU, ACT, AX = mybir.AluOpType, mybir.ActivationFunctionType, mybir.AxisListType

    weight_rows = {"Wl0": Wl0, "Wr0": Wr0, "Wl1": Wl1, "Wr1": Wr1, "W1a": W1, "W2": W2}
    for g, gate in enumerate("rzn"):
        weight_rows["ih_" + gate] = W_ih[g * D:(g + 1) * D, :]
        weight_rows["hh_" + gate] = W_hh[g * D:(g + 1) * D, :]

    with ExitStack() as ctx:
        KB = 1024
        top = [nc.sbuf_base + (-nc.sbuf_base) % 32]

        def region(nbytes):
            at = top[0]
            top[0] += nbytes
            assert top[0] <= nc.sbuf_usable_end, (top[0], nc.sbuf_usable_end)
            return at

        class Part:
            def __init__(self, start, nbytes):
                self.at, self.end = start, start + nbytes

            def __call__(self, name, shape, dt):
                size = mybir.dt.size(dt)
                for s in shape[1:]:
                    size *= s
                size += (-size) % 32
                t = nc.alloc_sbuf_tensor_at(name, shape, dt, offset=self.at)
                self.at += size
                assert self.at <= self.end, (name, self.at - self.end)
                return t

        def part(nbytes):
            return Part(region(nbytes), nbytes)

        misc = part(13 * KB + KB // 4)
        ident = misc("ident", [P, P], f32)
        cntb = Part(misc.at, 5 * KB)("cntb", [P, NP], f32)
        iota = misc("iota", [P, NP], f32)
        srcI = misc("srcI", [P, TC], i32)
        dstF = misc("dstF", [P, TC], f32)
        tab = misc("tab", [1, 32], i32)
        ea_row = misc("ea_row", [1, TC], i32)
        cnt = misc("cnt", [P, NT], f32)
        rcnt = misc("rcnt", [P, NT], f32)
        bn6 = misc("bn6", [P, NT, 6], f32)
        mv = misc("mv", [P, NT, 2], f32)
        ln = misc("ln", [P, 6, NT], f32)
        rstd = misc("rstd", [P, NT], f32)
        shift = misc("shift", [P, NT], f32)
        w1b_at = misc.at
        W1b_hi = misc("W1b_hi", [P, D], f32r)
        W1b_lo = misc("W1b_lo", [P, D], f32r)
        W1b_done = Part(w1b_at, 4 * KB)
        bin_b = W1b_done("bin_b", [P, D], f32)
        bhn_b = W1b_done("bhn_b", [P, D], f32)
        b2col = misc("b2col", [P, KC], f32)
        idx = [misc(f"idx{j}", [P, 1], i32) for j in range(U)]

        feat = part(40 * KB)
        hT_hi = feat("hT_hi", [P, KC, NP], f32r)
        hT_lo = feat("hT_lo", [P, KC, NP], f32r)

        slots = part(32 * KB)
        slot = {s: (slots(f"slot{s}_hi", [P, KC, D], f32r), slots(f"slot{s}_lo", [P, KC, D], f32r))
                for s in "AB"}
        slot["E"] = (W1b_hi, W1b_lo)
        stage = part(10 * KB)("stage", [P, KC, D + ED], f32)

        big = region(70 * KB)
        sage = Part(big, 70 * KB)
        AT = sage("AT", [P, NT, NP], f32)
        u_at = sage.at
        u = sage("u", [P, NT, D], f32)
        hots = Part(u_at, 20 * KB)
        hot_src = [hots(f"hot_src{j}", [P, NP], f16) for j in range(U)]
        hot_dst = [hots(f"hot_dst{j}", [P, P], f16) for j in range(U)]
        iota16 = hots("iota16", [P, NP], f16)
        srcF = hots("srcF", [P, TC], f32)
        ones16 = hots("ones16", [P, 1], f16)
        zeros16 = hots("zeros16", [P, D], f16)
        rows = Part(big, 50 * KB)
        dst_i = rows("dst_i", [P, 2, P], i32)
        src_i = rows("src_i", [P, 2, P], i32)
        real_i = rows("real_i", [P, P], i32)
        dst_f = rows("dst_f", [P, 2, P], f32)
        src_f = rows("src_f", [P, 2, P], f32)
        real_f = rows("real_f", [P, P], f32)
        ends = rows("ends", [P, 4], f32)
        ends16 = rows("ends16", [P, 4, 16], f32)
        span = rows("span", [16, 8, ET], f32)
        tile_no = rows("tile_no", [16, ET], f32)
        tile_up = rows("tile_up", [16, ET], f32)
        chunk_lo = rows("chunk_lo", [16, 1], f32)
        chunk_hi = rows("chunk_hi", [16, 1], f32)
        reach = rows("reach", [16, 4], f32)
        line = rows("line", [1, 8, 32], f32)
        line_i = rows("line_i", [1, 2, 32], i32)

        late = Part(big, 70 * KB)
        RT_hi = late("RT_hi", [P, KC, NP], f32r)
        RT_lo = late("RT_lo", [P, KC, NP], f32r)
        late_at = late.at
        edge = Part(late_at, 30 * KB)
        gathered = [edge(f"gathered{j}", [P, D], f32) for j in range(U)]
        msg = [edge(f"msg{j}", [P, D], f32) for j in range(U)]
        ea = [edge(f"ea{j}", [P, ED], f32) for j in range(U)]
        eaT_hi = edge("eaT_hi", [P, U, P], f32r)
        eaT_lo = edge("eaT_lo", [P, U, P], f32r)
        hot = [edge(f"hot{j}", [P, P], f32) for j in range(U)]
        Rtmp = [edge(f"Rtmp{j}", [P, D], f32) for j in range(2)]
        zeros = edge("zeros", [P, D], f16)
        before = Part(big, 20 * KB)
        h2 = before("h2", [P, NT, D], f32)
        gru = Part(late_at, 30 * KB)
        slot["C"] = (gru("slotC_hi", [P, KC, D], f32r), gru("slotC_lo", [P, KC, D], f32r))
        ta = [gru(f"ta{j}", [P, D], f32) for j in range(2)]
        tb = [gru(f"tb{j}", [P, D], f32) for j in range(2)]
        tc = [gru(f"tc{j}", [P, D], f32) for j in range(2)]

        xs = part(20 * KB)
        x_at = xs.at
        xt = xs("xt", [P, NT, D], f32)
        rn = Part(x_at, 20 * KB)("rn", [P, NT, D], f32)

        tmps = part(12 * KB)
        tmp_at = tmps.at
        ht = [tmps(f"ht{j}", [P, D], f32) for j in range(2)]
        va = [tmps(f"va{j}", [P, D], f32) for j in range(2)]
        za = [tmps(f"za{j}", [P, D], f32) for j in range(2)]
        gates = Part(tmp_at, 12 * KB)
        td = [gates(f"td{j}", [P, D], f32) for j in range(2)]
        te = [gates(f"te{j}", [P, D], f32) for j in range(2)]
        tf = [gates(f"tf{j}", [P, D], f32) for j in range(2)]

        bias = part(10 * KB)
        bias_at = bias.at
        bl0_b = bias("bl0_b", [P, D], f32)
        bl1_b = bias("bl1_b", [P, D], f32)
        b1_b = bias("b1_b", [P, D], f32)
        G_b = bias("G_b", [P, D], f32)
        B_b = bias("B_b", [P, D], f32)
        sage_done = Part(bias_at, 4 * KB)
        br_b = sage_done("br_b", [P, D], f32)
        bz_b = sage_done("bz_b", [P, D], f32)

        psA = [ctx.enter_context(nc.psum_tensor(f"psA{q}", [P, 3 * D], f32)) for q in range(2)]
        psT = [ctx.enter_context(nc.psum_tensor(f"psT{q}", [P, D], f32)) for q in range(2)]
        bank = [psA[b // 3][:, (b % 3) * D:(b % 3 + 1) * D] for b in range(6)]

        names = """idx_zero idx_loaded x_loaded const rows_f ends_made tables ends_bcast tile_tables
            reach_made reach_T tab_ready hot_ready hot_used counts_done counts_out counts_in ln_stats ln_sqrt ln_ready
            h_made staged tr_pe tr_hi tr_lo u_done u_out sv_done sv_read z_made g_made x1_made
            h2_made p_done p_made xh_made h_stored xh_stored bias_loaded bias_sqrt bias_made
            ea_T ea_hi ea_lo q_done q_used msg_made hot_made summed gate idx_made
            R_done R_out diag_made cntb_done cntb_out agg_done agg_f agg_hi agg_lo
            r_done r_sum r_made n_done n_hn n_mul n_bias n_sum n_made z_done z_sum z_gate z_diff z_mul
            z_new z_scaled z_out dve_chain act_chain pool_chain sp_gate gate_bias n_bias_loaded""".split()
        S = {n: ctx.enter_context(nc.semaphore("s_" + n)) for n in names}
        p_stored = [ctx.enter_context(nc.semaphore(f"s_p_stored{j}")) for j in range(2)]
        ea_loaded = [ctx.enter_context(nc.semaphore(f"s_ea_loaded{j}")) for j in range(U)]
        p_gathered = [ctx.enter_context(nc.semaphore(f"s_p_gathered{j}")) for j in range(U)]
        h_loaded = [ctx.enter_context(nc.semaphore(f"s_h_loaded{j}")) for j in range(2)]
        xh_loaded = [ctx.enter_context(nc.semaphore(f"s_xh_loaded{j}")) for j in range(2)]
        out_stored = [ctx.enter_context(nc.semaphore(f"s_out_stored{j}")) for j in range(2)]

        block = ctx.enter_context(nc.Block())

        def chunk_visits(eng, c):
            base = eng.value_load(tab[0:1, c:c + 1], min_val=-U * 700, max_val=ET)
            v0 = eng.value_load(tab[0:1, 16 + c:17 + c], min_val=1, max_val=700)
            v1 = eng.value_load(tab[0:1, 17 + c:18 + c], min_val=2, max_val=700)
            return base, v0, v1

        def first_tile(eng, v, base):
            return nc.s_assert_within(eng.snap(v * U + base), 0, TC - U,
                                      skip_runtime_bounds_check_because="the tile tables bound the visits")

        @block.sync
        def _(sp):
            sp.wait_ge(S["idx_zero"], 2)
            for t, a in ((dst_i, dst), (src_i, src)):
                sp.dma_start(t[:, 0, :], a[0:P * P].rearrange("(t p) -> t p", p=P)).then_inc(S["idx_loaded"], 16)
                sp.dma_start(t[0:FULL - P, 1, :], a[P * P:FULL * P].rearrange("(t p) -> t p", p=P))\
                  .then_inc(S["idx_loaded"], 16)
            sp.dma_start(dst_i[FULL - P:FULL - P + 1, 1, P - TAIL:P], dst[FULL * P:E].unsqueeze(0))\
              .then_inc(S["idx_loaded"], 16)
            sp.dma_start(src_i[FULL - P:FULL - P + 1, 1, :], src[E - P:E].unsqueeze(0)).then_inc(S["idx_loaded"], 16)
            sp.dma_start(real_i[0:FULL - P, :], dst[P * P:FULL * P].rearrange("(t p) -> t p", p=P))\
              .then_inc(S["idx_loaded"], 16)
            sp.dma_start(real_i[FULL - P:FULL - P + 1, :], dst[E - P:E].unsqueeze(0)).then_inc(S["idx_loaded"], 16)

            def stage_weights(w):
                if STAGED.index(w):
                    sp.wait_ge(S["tr_pe"], LAST_JOB[STAGED[STAGED.index(w) - 1]] + 1)
                rows_of = weight_rows[w]
                sp.dma_start(stage[:, :, 0:rows_of.shape[1]], rows_of.rearrange("(b p) k -> p b k", p=P))\
                  .then_inc(S["staged"], 16)

            stage_weights("Wl0")
            for t, a in ((bl0_b, bl0), (bl1_b, bl1), (b1_b, b1), (G_b, run_var), (B_b, beta),
                         (za[0], gamma), (za[1], run_mean)):
                sp.dma_start(t[:, :], a.partition_broadcast(P)).then_inc(S["bias_loaded"], 16)
            sp.dma_start(b2col[:, :], b2.rearrange("(k p) -> p k", p=P), allow_slow_non_contiguous=True)\
              .then_inc(S["bias_loaded"], 16)
            for w in STAGED[1:5]:
                stage_weights(w)
            stage_weights("W2")
            for n in range(NT):
                sp.wait_ge(S["p_made"], n + 1)
                sp.dma_start(p_table[n * P:(n + 1) * P, :], va[n % 2][:, :]).then_inc(p_stored[n % 2], 16)
            sp.wait_ge(S["h2_made"], NT)
            sp.dma_start(h_stash[:, :, :], h2[:, :, :]).then_inc(S["h_stored"], 16)
            sp.wait_ge(S["xh_made"], NT)
            sp.dma_start(xh_stash[:, :, :], xt[:, :, :]).then_inc(S["xh_stored"], 16)
            for j in range(2):
                sp.wait_ge(p_stored[j], 16 * (NT // 2))
            for t, a in ((br_b, b_ih[0:D]), (bz_b, b_ih[D:2 * D]), (va[0], b_hh[0:D]), (va[1], b_hh[D:2 * D])):
                sp.dma_start(t[:, :], a.partition_broadcast(P)).then_inc(S["gate_bias"], 16)
            stage_weights("ih_r")
            stage_weights("hh_r")
            sp.wait_ge(S["tab_ready"], 1)
            sp.wait_ge(S["h_stored"], 16)
            sp.wait_ge(S["counts_in"], 1)
            for c in range(NT):
                base, v0, v1 = chunk_visits(sp, c)
                with sp.Fori(v0, v1) as v:
                    t = first_tile(sp, v, base)
                    sp.wait_ge(S["ea_T"], v)
                    sp.sem_inc(S["sp_gate"], 1)
                    for j in range(U):
                        row = sp.value_load(ea_row[0:1, bass.ds(t + j, 1)], min_val=0, max_val=E - P)
                        sp.dma_start(ea[j][:, :], edge_attr[bass.ds(row, P), :]).then_inc(ea_loaded[j], 16)
            end = sp.value_load(tab[0:1, 16 + NT:17 + NT], min_val=2, max_val=700)
            for k in range(2):
                sp.wait_ge(S["ea_T"], end + k)
                sp.sem_inc(S["sp_gate"], 1)
                for j in range(U):
                    sp.dma_start(ea[j][:, :], edge_attr[0:P, :]).then_inc(ea_loaded[j], 16)
            sp.wait_ge(S["R_done"], NT)
            for t, a in ((bin_b, b_ih[2 * D:3 * D]), (bhn_b, b_hh[2 * D:3 * D])):
                sp.dma_start(t[:, :], a.partition_broadcast(P)).then_inc(S["n_bias_loaded"], 16)
            for w in ("ih_n", "hh_n", "ih_z", "hh_z"):
                stage_weights(w)
            for n in range(NT):
                size = P if n < NT - 1 else LAST
                if n >= 2:
                    sp.wait_ge(S["z_diff"], n - 1)
                else:
                    sp.wait_ge(S["n_made"], NT - 1 + n)
                sp.dma_start(te[n % 2][:, :], h_stash[:, n, :]).then_inc(h_loaded[n % 2], 16)
                if n >= 2:
                    sp.wait_ge(S["z_out"], n - 1)
                sp.dma_start(tf[n % 2][:, :], xh_stash[:, n, :]).then_inc(xh_loaded[n % 2], 16)
                if n >= 1:
                    sp.wait_ge(S["z_out"], n)
                    sp.dma_start(out[(n - 1) * P:n * P, :], tc[(n - 1) % 2][:, :])\
                      .then_inc(out_stored[(n - 1) % 2], 16)
            sp.wait_ge(S["z_out"], NT)
            sp.dma_start(out[(NT - 1) * P:N, :], tc[(NT - 1) % 2][0:LAST, :]).then_inc(out_stored[(NT - 1) % 2], 16)
            for j in range(2):
                sp.wait_ge(out_stored[j], 16 * (NT // 2))

        @block.gpsimd
        def _(pool):
            chain = [0]

            def link(ins):
                chain[0] += 1
                ins.then_inc(S["pool_chain"], 1)
                pool.wait_ge(S["pool_chain"], chain[0])

            pool.memset(dst_i[:, 1, :], -1).then_inc(S["idx_zero"], 1)
            pool.memset(src_i[:, 1, :], 0).then_inc(S["idx_zero"], 1)
            link(pool.memset(ident[:, :], 0.0))
            link(pool.affine_select(out=ident[:, :], in_=ident[:, :], compare_op=ALU.not_equal, fill=1.0,
                                    base=0, pattern=[[-1, P]], channel_multiplier=1))
            pool.iota(chunk_lo[:, :], pattern=[[0, 1]], base=0, channel_multiplier=P,
                      allow_small_or_imprecise_dtypes=True)
            pool.iota(chunk_hi[:, :], pattern=[[0, 1]], base=P - 1, channel_multiplier=P,
                      allow_small_or_imprecise_dtypes=True)
            pool.iota(tile_no[:, :], pattern=[[1, ET]], base=-1000, channel_multiplier=0,
                      allow_small_or_imprecise_dtypes=True)
            pool.iota(tile_up[:, :], pattern=[[1, ET]], base=1, channel_multiplier=0,
                      allow_small_or_imprecise_dtypes=True)
            pool.memset(line[:, :, :], 0.0)
            pool.memset(xt[:, NT - 1, :], 0.0).then_inc(S["const"], 1)
            pool.iota(iota16[:, :], pattern=[[1, NP]], base=0, channel_multiplier=0,
                      allow_small_or_imprecise_dtypes=True)
            pool.iota(iota[:, :], pattern=[[1, NP]], base=0, channel_multiplier=0,
                      allow_small_or_imprecise_dtypes=True)
            pool.memset(ones16[:, :], 1.0)
            pool.memset(zeros16[:, :], 0.0).then_inc(S["const"], 1)
            link(pool.iota(ea_row[:, :], pattern=[[P, TC]], base=0, channel_multiplier=0))
            link(pool.tensor_scalar(ea_row[:, :], ea_row[:, :], E - P, None, ALU.min))
            pool.memset(tab[0:1, 28:32], 0).then_inc(S["counts_in"], 1)

            pool.wait_ge(S["bias_made"], 1)
            for n in range(NT):
                pool.wait_ge(S["h2_made"], n + 1)
                link(pool.tensor_tensor(xt[:, n, :], xt[:, n, :], h2[:, n, :], ALU.add))
                pool.tensor_tensor(xt[:, n, :], xt[:, n, :], B_b[:, :], ALU.add).then_inc(S["xh_made"], 1)

            pool.wait_ge(p_stored[0], 16 * (NT // 2))
            pool.wait_ge(p_stored[1], 16 * (NT // 2))
            pool.wait_ge(S["h_stored"], 16)
            pool.memset(zeros[:, :], 0.0).then_inc(S["const"], 1)

            def gather(j):
                pool.indirect_dma_start(
                    out=gathered[j][:, :], out_offset=None, in_=p_table[:, :],
                    in_offset=bass.IndirectOffsetOnAxis(ap=idx[j][:, 0:1], axis=0)).then_inc(p_gathered[j], 16)

            for c in range(NT):
                base, v0, v1 = chunk_visits(pool, c)
                with pool.Fori(v0, v1) as v:
                    t = first_tile(pool, v, base)
                    for j in range(U):
                        pool.wait_ge(S["q_used"], v * U + (j + 1))
                        pool.sem_inc(S["gate"], 1)
                        pool.tensor_copy(idx[j][:, :], srcI[:, bass.ds(t + j, 1)]).then_inc(S["idx_made"], 1)
                        pool.wait_ge(S["idx_made"], v * U + (j + 1))
                        pool.sem_inc(S["gate"], 1)
                        gather(j)
            end = pool.value_load(tab[0:1, 16 + NT:17 + NT], min_val=2, max_val=700)
            for j in range(U):
                pool.wait_ge(S["q_used"], end * U + (j + 1))
                pool.sem_inc(S["gate"], 1)
                gather(j)

            pool.wait_ge(S["xh_stored"], 16)
            pool.wait_ge(S["n_bias_loaded"], 32)
            for n in range(NT):
                pool.wait_ge(S["n_hn"], n + 1)
                pool.tensor_tensor(ta[n % 2][:, :], ta[n % 2][:, :], rn[:, n, :], ALU.mult).then_inc(S["n_mul"], 1)
                pool.wait_ge(S["n_mul"], n + 1)
                pool.tensor_tensor(ta[n % 2][:, :], ta[n % 2][:, :], bin_b[:, :], ALU.add).then_inc(S["n_bias"], 1)
            for n in range(NT):
                pool.wait_ge(S["n_made"], n + 1)
                pool.wait_ge(h_loaded[n % 2], 16 * (n // 2 + 1))
                if n >= 2:
                    pool.wait_ge(S["z_mul"], n - 1)
                pool.tensor_tensor(td[n % 2][:, :], te[n % 2][:, :], rn[:, n, :], ALU.subtract)\
                    .then_inc(S["z_diff"], 1)

        @block.scalar
        def _(act):
            act.wait_ge(S["const"], 1)
            act.dma_start(xt[:, 0:NT - 1, :], x[0:(NT - 1) * P, :].rearrange("(n p) d -> p n d", p=P))\
               .then_inc(S["x_loaded"], 16)
            act.dma_start(xt[0:LAST, NT - 1, :], x[(NT - 1) * P:N, :]).then_inc(S["x_loaded"], 16)
            act.wait_ge(S["bias_sqrt"], 1)
            act.activation(G_b[:, :], G_b[:, :], ACT.Sqrt).then_inc(S["bias_sqrt"], 1)

            def ln_root(k):
                act.wait_ge(S["ln_stats"], k + 1)
                act.activation(ln[:, 1, :], ln[:, 0, :], ACT.Sqrt).then_inc(S["ln_sqrt"], 1)

            def hi_part(name, k):
                j = JOB[(name, k)]
                act.wait_ge(S["tr_pe"], j + 1)
                if name in ("h", "g", "h2"):
                    o = hT_hi[:, :, k * P:(k + 1) * P]
                elif name == "R":
                    o = RT_hi[:, :, k * P:(k + 1) * P]
                elif name == "W1b":
                    o = W1b_hi[:, :]
                else:
                    o = slot[SLOT[name]][0][:, k, :]
                i = psT[j % 2][:, :]
                if name in ("h", "g", "h2", "R"):
                    i = i.rearrange("p (k n) -> p k n", k=KC)
                act.activation(o, i, ACT.Copy).then_inc(S["tr_hi"], 1)

            ln_root(0)

            def make_h(c):
                if c < 2:
                    act.wait_ge(S["ln_ready"], 1)
                else:
                    act.wait_ge(S["tr_pe"], JOB[("h", c - 2)] + 1)
                act.activation(ht[c % 2][:, :], xt[:, c, :], ACT.Relu, bias=shift[:, c:c + 1],
                               scale=rstd[:, c:c + 1]).then_inc(S["h_made"], 1)

            make_h(0)
            make_h(1)
            for c in range(NT):
                act.wait_ge(S["counts_done"], c + 1)
                act.activation(AT[:, :, c * P:(c + 1) * P],
                               psA[c % 2][:, 0:NP].rearrange("p (s d) -> p s d", s=NT), ACT.Copy)
                act.activation(cnt[:, c:c + 1], psA[c % 2][:, NP:NP + 1], ACT.Copy).then_inc(S["counts_out"], 1)
                hi_part("h", c)
                if c < 8:
                    hi_part(("Wl0", "Wr0")[c // KC], c % KC)
                if c + 2 < NT:
                    make_h(c + 2)

            def u_out(layer, n):
                act.wait_ge(S["u_done"], layer * NT + n + 1)
                act.activation(u[:, n, :], bank[n % 2], ACT.Copy).then_inc(S["u_out"], 1)

            for n in range(NT):
                u_out(0, n)
            for n in range(NT):
                if n < KC:
                    hi_part("Wl1", n)
                act.wait_ge(S["z_made"], n + 1)
                if n >= 2:
                    act.wait_ge(S["tr_pe"], JOB[("g", n - 2)] + 1)
                act.activation(ht[n % 2][:, :], za[n % 2][:, :], ACT.Relu).then_inc(S["g_made"], 1)
                if n:
                    hi_part("g", n - 1)
            hi_part("g", NT - 1)
            for n in range(NT):
                if n < KC:
                    hi_part("Wr1", n)
                u_out(1, n)
            for n in range(KC):
                hi_part("W1a", n)
            hi_part("W1b", 0)
            for n in range(KC):
                hi_part("W2", n)
            ln_root(1)
            act.wait_ge(S["ln_ready"], 2)

            def make_h2(n):
                act.activation(h2[:, n, :], xt[:, n, :], ACT.Relu, bias=shift[:, n:n + 1],
                               scale=rstd[:, n:n + 1]).then_inc(S["h2_made"], 1)
            make_h2(0)
            make_h2(1)
            for n in range(NT):
                if n + 2 < NT:
                    make_h2(n + 2)
                hi_part("h2", n)
            for n in range(KC):
                hi_part("ih_r", n)

            def hi_of_edges(v):
                act.wait_ge(S["ea_T"], v + 1)
                act.wait_ge(S["q_done"], U * v)
                act.activation(eaT_hi[:, :, :], bank[5][:, 0:U * P].rearrange("p (j e) -> p j e", j=U),
                               ACT.Copy).then_inc(S["ea_hi"], 1)

            def relu_messages(v):
                for j in range(U):
                    act.wait_ge(S["q_used"], v * U + (U + j + 1))
                    act.activation(msg[j][:, :], msg[j][:, :], ACT.Relu).then_inc(S["msg_made"], 1)

            act.wait_ge(S["h_stored"], 16)
            hi_of_edges(1)
            hi_of_edges(2)
            relu_messages(1)
            for c in range(NT):
                base, v0, v1 = chunk_visits(act, c)
                with act.Fori(v0, v1) as v:
                    hi_of_edges(v + 2)
                    relu_messages(v + 1)
                act.wait_ge(S["R_done"], c + 1)
                if c >= 2:
                    act.wait_ge(S["tr_pe"], JOB[("R", c - 2)] + 1)
                act.activation(Rtmp[c % 2][:, :], bank[3 + c % 2], ACT.Copy).then_inc(S["R_out"], 1)
                if c:
                    hi_part("R", c - 1)
            hi_part("R", NT - 1)
            for n in range(KC):
                hi_part("hh_r", n)
            for i in range(3 * KC):
                nb, oc = i // KC, i % KC
                act.wait_ge(S["agg_f"], i + 1)
                act.wait_ge(S["agg_done"], KC * (nb + 1))
                w = min(D, NP - nb * D)
                act.activation(RT_hi[:, oc, nb * D:nb * D + w], ta[i % 2][:, 0:w], ACT.Copy).then_inc(S["agg_hi"], 1)
            act.wait_ge(S["xh_stored"], 16)
            for n in range(NT):
                act.wait_ge(S["r_sum"], n + 1)
                act.activation(rn[:, n, :], tb[n % 2][:, :], ACT.Sigmoid).then_inc(S["r_made"], 1)
                if n < KC:
                    hi_part("ih_n", n)
            for k in range(KC):
                hi_part("hh_n", k)
            for n in range(NT):
                act.wait_ge(S["n_sum"], n + 1)
                act.activation(rn[:, n, :], te[n % 2][:, :], ACT.Tanh).then_inc(S["n_made"], 1)
                if n < KC:
                    hi_part("ih_z", n)
            for k in range(KC):
                hi_part("hh_z", k)
            for n in range(NT):
                act.wait_ge(S["z_sum"], n + 1)
                act.activation(tb[n % 2][:, :], tb[n % 2][:, :], ACT.Sigmoid).then_inc(S["z_gate"], 1)

        @block.vector
        def _(dve):
            chain = [0]

            def link(ins):
                chain[0] += 1
                ins.then_inc(S["dve_chain"], 1)
                dve.wait_ge(S["dve_chain"], chain[0])

            dve.wait_ge(S["idx_loaded"], 16 * 8)
            dve.tensor_copy(real_f[0:ROWS2, :], real_i[0:ROWS2, :])
            dve.tensor_copy(src_f[:, :, :], src_i[:, :, :])
            link(dve.tensor_copy(dst_f[:, :, :], dst_i[:, :, :]))
            S_rows = S["rows_f"]
            dve.tensor_reduce(ends[:, 0:1], dst_f[:, 0, :], AX.X, ALU.min)
            dve.tensor_reduce(ends[:, 1:2], dst_f[:, 0, :], AX.X, ALU.max)
            dve.tensor_reduce(ends[0:ROWS2, 2:3], real_f[0:ROWS2, :], AX.X, ALU.min)
            link(dve.tensor_reduce(ends[0:ROWS2, 3:4], real_f[0:ROWS2, :], AX.X, ALU.max))
            dve.tensor_copy(ends16[:, 0:2, :], ends[:, 0:2].unsqueeze(2).to_broadcast([P, 2, 16]))
            dve.tensor_copy(ends16[0:ROWS2, 2:4, :], ends[0:ROWS2, 2:4].unsqueeze(2).to_broadcast([ROWS2, 2, 16]))\
               .then_inc(S["ends_made"], 1)
            dve.wait_ge(S["const"], 1)
            dve.wait_ge(S["ends_bcast"], 1)
            dve.tensor_copy(span[:, 0, :], psT[1][0:16, 0:ET])
            link(dve.tensor_copy(span[:, 1, :], psT[1][0:16, 256:256 + ET]))
            link(dve.tensor_scalar(span[:, 2, :], span[:, 0, :], chunk_hi[:, 0:1], None, ALU.is_le))
            link(dve.scalar_tensor_tensor(span[:, 3, :], span[:, 1, :], chunk_lo[:, 0:1], span[:, 2, :],
                                          ALU.is_ge, ALU.mult))
            dve.tensor_tensor(span[:, 4, :], span[:, 3, :], tile_no[:, :], ALU.mult)
            link(dve.tensor_tensor(span[:, 5, :], span[:, 3, :], tile_up[:, :], ALU.mult))
            dve.tensor_reduce(reach[:, 0:1], span[:, 4, :], AX.X, ALU.min)
            link(dve.tensor_reduce(reach[:, 1:2], span[:, 5, :], AX.X, ALU.max))
            link(dve.tensor_scalar(reach[:, 2:3], reach[:, 0:1], 1000.0, float(ET - 1), ALU.add, ALU.min))
            link(dve.scalar_tensor_tensor(reach[:, 3:4], reach[:, 2:3], 1.0, reach[:, 1:2], ALU.add, ALU.max))
            dve.tensor_copy(reach[:, 0:1], reach[:, 2:3]).then_inc(S["reach_made"], 1)
            dve.wait_ge(S["tables"], 1)
            dve.tensor_copy(dstF[:, :], psT[0][:, 0:TC])
            dve.tensor_copy(srcI[:, :], psT[0][:, 256:256 + TC])
            dve.tensor_copy(srcF[:, :], psT[0][:, 256:256 + TC]).then_inc(S["tile_tables"], 1)
            dve.wait_ge(S["reach_T"], 1)
            dve.tensor_copy(line[0:1, 0, 0:NT], psT[1][0:1, 0:NT])
            link(dve.tensor_copy(line[0:1, 1, 0:NT], psT[1][0:1, 16:16 + NT]))
            link(dve.tensor_tensor(line[0:1, 2, 0:NT], line[0:1, 1, 0:NT], line[0:1, 0, 0:NT], ALU.subtract))
            link(dve.tensor_scalar(line_i[0:1, 0, 0:NT], line[0:1, 2, 0:NT], float(U - 1), 43691.0, ALU.add, ALU.mult))
            link(dve.tensor_scalar(line_i[0:1, 1, 0:NT], line_i[0:1, 0, 0:NT], 17, None, ALU.logical_shift_right))
            link(dve.tensor_copy(line[0:1, 3, 16:16 + NT], line_i[0:1, 1, 0:NT]))
            for k in range(4):
                s = 1 << k
                link(dve.tensor_tensor(line[0:1, 4 + k, 16:16 + NT], line[0:1, 3 + k, 16:16 + NT],
                                       line[0:1, 3 + k, 16 - s:16 + NT - s], ALU.add))
            link(dve.tensor_scalar(line[0:1, 4, 15:16 + NT], line[0:1, 7, 15:16 + NT], 1.0, None, ALU.add))
            dve.tensor_copy(tab[0:1, 16:17 + NT], line[0:1, 4, 15:16 + NT])
            dve.scalar_tensor_tensor(tab[0:1, 0:NT], line[0:1, 4, 15:15 + NT], -float(U), line[0:1, 0, 0:NT],
                                     ALU.mult, ALU.add).then_inc(S["tab_ready"], 1)

            def ln_finish(k):
                dve.tensor_scalar(ln[:, 0, :], mv[:, :, 1], EPS, None, ALU.add).then_inc(S["ln_stats"], 1)
                dve.wait_ge(S["ln_sqrt"], k + 1)
                link(dve.reciprocal(ln[:, 2, :], ln[:, 1, :]))
                link(dve.tensor_tensor(ln[:, 3, :], ln[:, 2, :], ln[:, 2, :], ALU.mult))
                link(dve.tensor_tensor(ln[:, 4, :], ln[:, 3, :], ln[:, 0, :], ALU.mult))
                link(dve.tensor_scalar(ln[:, 5, :], ln[:, 4, :], -0.5, 1.5, ALU.mult, ALU.add))
                link(dve.tensor_tensor(rstd[:, :], ln[:, 5, :], ln[:, 2, :], ALU.mult))
                dve.scalar_tensor_tensor(shift[:, :], mv[:, :, 0], -1.0, rstd[:, :], ALU.mult, ALU.mult)\
                   .then_inc(S["ln_ready"], 1)

            dve.wait_ge(S["bias_loaded"], 16 * 8)
            link(dve.tensor_scalar(za[1][:, :], za[1][:, :], -1.0, None, ALU.mult))
            link(dve.tensor_scalar(G_b[:, :], G_b[:, :], EPS, None, ALU.add))
            dve.tensor_copy(va[0][:, :], G_b[:, :]).then_inc(S["bias_sqrt"], 1)
            dve.wait_ge(S["x_loaded"], 32)
            for n in range(NT):
                last = dve.bn_stats(bn6[:, n, :], xt[:, n, :])
            link(last)
            for n in range(NT):
                last = dve.bn_aggr(mv[:, n, :], bn6[:, n, :])
            link(last)
            dve.wait_ge(S["bias_sqrt"], 2)
            link(dve.reciprocal(va[1][:, :], G_b[:, :]))
            link(dve.tensor_tensor(G_b[:, :], va[1][:, :], va[1][:, :], ALU.mult))
            link(dve.tensor_tensor(G_b[:, :], G_b[:, :], va[0][:, :], ALU.mult))
            link(dve.tensor_scalar(G_b[:, :], G_b[:, :], -0.5, 1.5, ALU.mult, ALU.add))
            link(dve.tensor_tensor(G_b[:, :], G_b[:, :], va[1][:, :], ALU.mult))
            link(dve.tensor_tensor(G_b[:, :], G_b[:, :], za[0][:, :], ALU.mult))
            link(dve.tensor_tensor(za[1][:, :], za[1][:, :], G_b[:, :], ALU.mult))
            dve.tensor_tensor(B_b[:, :], B_b[:, :], za[1][:, :], ALU.add).then_inc(S["bias_made"], 1)
            ln_finish(0)

            def lo_part(name, k):
                j = JOB[(name, k)]
                dve.wait_ge(S["tr_hi"], j + 1)
                if name in ("h", "g", "h2"):
                    hi, lo = (t[:, :, k * P:(k + 1) * P] for t in (hT_hi, hT_lo))
                elif name == "R":
                    hi, lo = (t[:, :, k * P:(k + 1) * P] for t in (RT_hi, RT_lo))
                elif name == "W1b":
                    hi, lo = W1b_hi[:, :], W1b_lo[:, :]
                else:
                    hi, lo = (t[:, k, :] for t in slot[SLOT[name]])
                i = psT[j % 2][:, :]
                if name in ("h", "g", "h2", "R"):
                    i = i.rearrange("p (k n) -> p k n", k=KC)
                dve.tensor_tensor(lo, i, hi.bitcast(f32), ALU.subtract).then_inc(S["tr_lo"], 1)

            dve.wait_ge(S["const"], 2)
            dve.wait_ge(S["tab_ready"], 1)
            dve.wait_ge(S["tile_tables"], 1)
            for c in range(NT):
                base, v0, v1 = chunk_visits(dve, c)
                with dve.Fori(v0, v1) as v:
                    t = first_tile(dve, v, base)
                    for j in range(U):
                        dve.wait_ge(S["hot_used"], v * U + (j + 1))
                        dve.tensor_scalar(hot_dst[j][:, :], iota16[:, c * P:(c + 1) * P],
                                          dstF[:, bass.ds(t + j, 1)], None, ALU.is_equal)
                        dve.tensor_scalar(hot_src[j][:, :], iota16[:, :], srcF[:, bass.ds(t + j, 1)], None,
                                          ALU.is_equal).then_inc(S["hot_ready"], 1)
                if c:
                    lo_part("h", c - 1)
                    if c - 1 < 8:
                        lo_part(("Wl0", "Wr0")[(c - 1) // KC], (c - 1) % KC)
            lo_part("h", NT - 1)
            dve.wait_ge(S["counts_out"], NT)
            link(dve.tensor_scalar(rcnt[:, :], cnt[:, :], 1.0, None, ALU.max))
            link(dve.reciprocal(rcnt[:, :], rcnt[:, :]))

            def sage_sum(layer, n):
                dve.wait_ge(S["sv_done"], layer * NT + n + 1)
                if layer == 0 and n >= 2:
                    dve.wait_ge(S["g_made"], n - 1)
                link(dve.tensor_tensor(va[n % 2][:, :], bank[4 + n % 2], (bl0_b, bl1_b)[layer][:, :], ALU.add))
                dve.scalar_tensor_tensor(za[n % 2][:, :], bank[2 + n % 2], rcnt[:, n:n + 1], va[n % 2][:, :],
                                         ALU.mult, ALU.add).then_inc(S["z_made"], 1)

            for n in range(NT):
                if n < KC:
                    lo_part("Wl1", n)
                sage_sum(0, n)
                if n:
                    lo_part("g", n - 1)
            lo_part("g", NT - 1)
            for n in range(NT):
                if n < KC:
                    lo_part("Wr1", n)
            for n in range(NT):
                sage_sum(1, n)
                dve.wait_ge(S["z_made"], NT + n + 1)
                link(dve.scalar_tensor_tensor(xt[:, n, :], za[n % 2][:, :], 0.0, xt[:, n, :], ALU.max, ALU.add))
                if n < KC:
                    lo_part("W1a", n)
                if n == KC:
                    lo_part("W1b", 0)
                link(dve.bn_stats(bn6[:, n, :], xt[:, n, :]))
                last = dve.bn_aggr(mv[:, n, :], bn6[:, n, :])
            link(last)
            for k in range(KC):
                lo_part("W2", k)
            ln_finish(1)
            for n in range(NT + 1):
                if n < NT:
                    lo_part("h2", n)
                if n:
                    m = n - 1
                    dve.wait_ge(S["p_done"], m + 1)
                    if m >= 2:
                        dve.wait_ge(p_stored[m % 2], 16 * (m // 2))
                    dve.tensor_tensor(va[m % 2][:, :], bank[m % 2], b1_b[:, :], ALU.add).then_inc(S["p_made"], 1)
            for k in range(KC):
                lo_part("ih_r", k)

            def lo_of_edges(v):
                dve.wait_ge(S["ea_hi"], v)
                dve.tensor_tensor(eaT_lo[:, :, :], bank[5][:, 0:U * P].rearrange("p (j e) -> p j e", j=U),
                                  eaT_hi[:, :, :].bitcast(f32), ALU.subtract).then_inc(S["ea_lo"], 1)

            def add_gathered(v):
                for j in range(U):
                    dve.wait_ge(S["q_done"], v * U + (j + 1))
                    dve.wait_ge(S["summed"], v * U + (j + 1))
                    dve.wait_ge(p_gathered[j], v * 16)
                    dve.tensor_tensor(msg[j][:, :], bank[j], gathered[j][:, :], ALU.add).then_inc(S["q_used"], 1)

            dve.wait_ge(S["gate_bias"], 64)
            dve.tensor_tensor(br_b[:, :], br_b[:, :], va[0][:, :], ALU.add)
            link(dve.tensor_tensor(bz_b[:, :], bz_b[:, :], va[1][:, :], ALU.add))
            dve.wait_ge(S["h_stored"], 16)
            lo_of_edges(1)
            lo_of_edges(2)
            add_gathered(1)
            for c in range(NT):
                base, v0, v1 = chunk_visits(dve, c)
                with dve.Fori(v0, v1) as v:
                    t = first_tile(dve, v, base)
                    dve.wait_ge(S["summed"], v * U + U)
                    for j in range(U):
                        last = dve.tensor_scalar(hot[j][:, :], iota[:, c * P:(c + 1) * P],
                                                 dstF[:, bass.ds(t + j, 1)], None, ALU.is_equal)
                    last.then_inc(S["hot_made"], 1)
                    lo_of_edges(v + 2)
                    add_gathered(v + 1)
                if c:
                    lo_part("R", c - 1)
            lo_part("R", NT - 1)
            for c in range(NT):
                if c >= 2:
                    dve.wait_ge(S["cntb_done"], c - 1)
                dve.tensor_scalar(hot[c % 2][:, :], ident[:, :], cnt[:, c:c + 1], None, ALU.mult)\
                   .then_inc(S["diag_made"], 1)
                if c == 0:
                    dve.memset(hot[2][:, :], 1.0).then_inc(S["diag_made"], 1)
            for q in range(3):
                w = min(D, NP - q * D)
                dve.wait_ge(S["cntb_done"], min(NT, KC * (q + 1)))
                last = dve.tensor_copy(cntb[:, q * D:q * D + w], bank[q][:, 0:w])
            last.then_inc(S["cntb_out"], 1)
            dve.wait_ge(S["cntb_out"], 1)
            for k in range(KC):
                lo_part("hh_r", k)

            def agg_lo(i):
                nb, oc = i // KC, i % KC
                w = min(D, NP - nb * D)
                dve.wait_ge(S["agg_hi"], i + 1)
                dve.tensor_tensor(RT_lo[:, oc, nb * D:nb * D + w], ta[i % 2][:, 0:w],
                                  RT_hi[:, oc, nb * D:nb * D + w].bitcast(f32), ALU.subtract)\
                   .then_inc(S["agg_lo"], 1)

            for i in range(3 * KC):
                nb, oc = i // KC, i % KC
                w = min(D, NP - nb * D)
                dve.wait_ge(S["agg_done"], i + 1)
                if i >= 2:
                    dve.wait_ge(S["agg_lo"], i - 1)
                dve.scalar_tensor_tensor(ta[i % 2][:, 0:w], cntb[:, nb * D:nb * D + w], b2col[:, oc:oc + 1],
                                         bank[i % 6][:, 0:w], ALU.mult, ALU.add).then_inc(S["agg_f"], 1)
                if i:
                    agg_lo(i - 1)
            agg_lo(3 * KC - 1)

            for n in range(NT):
                dve.wait_ge(S["r_done"], n + 1)
                if n >= 2:
                    dve.wait_ge(S["r_made"], n - 1)
                dve.tensor_tensor(tb[n % 2][:, :], bank[n % 2], br_b[:, :], ALU.add).then_inc(S["r_sum"], 1)
                if n < KC:
                    lo_part("ih_n", n)
            for k in range(KC):
                lo_part("hh_n", k)

            dve.wait_ge(S["n_bias_loaded"], 32)
            def n_sum(n):
                dve.wait_ge(S["n_bias"], n + 1)
                if n >= 2:
                    dve.wait_ge(S["n_made"], n - 1)
                dve.tensor_tensor(te[n % 2][:, :], bank[2 + n % 2], ta[n % 2][:, :], ALU.add).then_inc(S["n_sum"], 1)

            for n in range(NT):
                dve.wait_ge(S["n_done"], n + 1)
                if n >= 2:
                    dve.wait_ge(S["n_sum"], n - 1)
                dve.tensor_tensor(ta[n % 2][:, :], bank[4 + n % 2], bhn_b[:, :], ALU.add).then_inc(S["n_hn"], 1)
                if n:
                    n_sum(n - 1)
                if 1 <= n <= KC:
                    lo_part("ih_z", n - 1)
            n_sum(NT - 1)
            for k in range(KC):
                lo_part("hh_z", k)

            def z_finish(n):
                dve.wait_ge(S["z_gate"], n + 1)
                dve.wait_ge(S["z_diff"], n + 1)
                dve.tensor_tensor(tb[n % 2][:, :], tb[n % 2][:, :], td[n % 2][:, :], ALU.mult)\
                   .then_inc(S["z_mul"], 1)
                dve.wait_ge(S["z_mul"], n + 1)
                link(dve.tensor_tensor(tb[n % 2][:, :], tb[n % 2][:, :], rn[:, n, :], ALU.add))
                link(dve.tensor_tensor(tb[n % 2][:, :], tb[n % 2][:, :], G_b[:, :], ALU.mult))
                dve.wait_ge(xh_loaded[n % 2], 16 * (n // 2 + 1))
                if n >= 2:
                    dve.wait_ge(out_stored[n % 2], 16 * (n // 2))
                dve.tensor_tensor(tc[n % 2][:, :], tb[n % 2][:, :], tf[n % 2][:, :], ALU.add)\
                   .then_inc(S["z_out"], 1)

            for n in range(NT):
                dve.wait_ge(S["z_done"], n + 1)
                if n >= 2:
                    dve.wait_ge(S["z_out"], n - 1)
                dve.tensor_tensor(tb[n % 2][:, :], bank[n % 2], bz_b[:, :], ALU.add).then_inc(S["z_sum"], 1)
                if n:
                    z_finish(n - 1)
            z_finish(NT - 1)

        @block.tensor
        def _(pe):
            pe.wait_ge(S["pool_chain"], 2)
            pe.wait_ge(S["ends_made"], 1)
            two = TC - P
            for q, (lo, hi) in enumerate(((0, 2), (1, 3))):
                pe.matmul(psT[1][0:16, q * 256:q * 256 + P], ends16[:, lo, :], ident[:, :], start=True, stop=True)
                last = pe.matmul(psT[1][0:16, q * 256 + P:q * 256 + ET], ends16[0:ROWS2, hi, :],
                                 ident[0:ROWS2, 0:ROWS2], start=True, stop=True)
            last.then_inc(S["ends_bcast"], 1)
            for q, rows_f in enumerate((dst_f, src_f)):
                pe.transpose(psT[0][:, q * 256:q * 256 + P], rows_f[:, 0, :], ident[:, :])
                last = pe.transpose(psT[0][:, q * 256 + P:q * 256 + TC], rows_f[0:two, 1, :], ident[0:two, 0:two])
            last.then_inc(S["tables"], 1)
            pe.wait_ge(S["reach_made"], 1)
            pe.transpose(psT[1][0:1, 0:16], reach[:, 0:1], ident[0:16, 0:16])
            pe.transpose(psT[1][0:1, 16:32], reach[:, 3:4], ident[0:16, 0:16]).then_inc(S["reach_T"], 1)

            def job(name, k):
                j = JOB[(name, k)]
                if j >= 2:
                    pe.wait_ge(S["tr_lo"], j - 1)
                if name in STAGED and k == 0:
                    pe.wait_ge(S["staged"], 16 * (STAGED.index(name) + 1))
                for b in range(KC):
                    if name == "h" or name == "g":
                        i = ht[k % 2][:, b * P:(b + 1) * P]
                    elif name == "h2":
                        i = h2[:, k, b * P:(b + 1) * P]
                    elif name == "R":
                        i = Rtmp[k % 2][:, b * P:(b + 1) * P]
                    elif name == "W1b":
                        i = stage[:, b, D:D + ED]
                    else:
                        i = stage[:, b, k * P:(k + 1) * P]
                    last = pe.transpose(psT[j % 2][:, b * P:(b + 1) * P], i, ident[:, :])
                last.then_inc(S["tr_pe"], 1)

            def product(o, lhs, rhs, start=True, stop=True):
                for kc in range(KC):
                    for p, (a, b) in enumerate(((0, 0), (0, 1), (1, 0))):
                        last = pe.matmul(o, lhs[a](kc), rhs[b](kc), start=start and kc == 0 and p == 0,
                                         stop=stop and kc == KC - 1 and p == 2)
                return last

            def nodes(t, n):
                return tuple((lambda kc, y=y: y[:, kc, n * P:(n + 1) * P]) for y in t)

            def weights(name):
                return tuple((lambda kc, y=y: y[:, kc, :]) for y in slot[SLOT[name]])

            hT, RT = (hT_hi, hT_lo), (RT_hi, RT_lo)

            pe.wait_ge(S["tab_ready"], 1)
            pe.wait_ge(S["const"], 2)
            pe.wait_ge(S["tile_tables"], 1)
            pe.sem_inc(S["hot_used"], 2 * U)
            pe.sem_inc(S["hot_ready"], U)
            for c in range(NT):
                if c >= 2:
                    pe.wait_ge(S["counts_out"], c - 1)
                A = psA[c % 2]
                for q in range(3):
                    pe.matmul(A[:, q * D:(q + 1) * D], zeros16[:, 0:P], zeros16[:, :], start=True, stop=False)
                base, v0, v1 = chunk_visits(pe, c)
                with pe.Fori(v0, v1) as v:
                    for j in range(U):
                        pe.wait_ge(S["hot_ready"], v * U + (j + 1))
                        for s in range(NT):
                            pe.matmul(A[:, s * P:(s + 1) * P], hot_src[j][:, s * P:(s + 1) * P], hot_dst[j][:, :],
                                      start=False, stop=False)
                        pe.matmul(A[:, NP:NP + 1], hot_dst[j][:, :], ones16[:, :], start=False, stop=False)\
                          .then_inc(S["hot_used"], 1)
                for q in range(3):
                    last = pe.matmul(A[:, q * D:(q + 1) * D], zeros16[:, 0:P], zeros16[:, :], start=False, stop=True)
                last.then_inc(S["counts_done"], 1)
                pe.wait_ge(S["h_made"], c + 1)
                job("h", c)
                if c < 8:
                    job(("Wl0", "Wr0")[c // KC], c % KC)

            def product_u(layer, n):
                i = layer * NT + n
                if i >= 2:
                    pe.wait_ge(S["u_out"], i - 1)
                if n < 1 or layer == 0:
                    pe.wait_ge(S["tr_lo"], JOB[(("h", "g")[layer], NT - 1)] + 1)
                product(bank[n % 2], nodes(hT, n), weights(f"Wl{layer}")).then_inc(S["u_done"], 1)

            def product_sv(layer, n):
                i = layer * NT + n
                if n == 0:
                    pe.wait_ge(S["u_out"], (layer + 1) * NT)
                    pe.wait_ge(S["tr_lo"], LAST_JOB[f"Wr{layer}"] + 1)
                if i >= 2:
                    pe.wait_ge(S["z_made"], i - 1)
                for s in range(NT):
                    pe.matmul(bank[2 + n % 2], AT[:, s, n * P:(n + 1) * P], u[:, s, :], start=s == 0, stop=s == NT - 1)
                product(bank[4 + n % 2], nodes(hT, n), weights(f"Wr{layer}")).then_inc(S["sv_done"], 1)

            pe.wait_ge(S["counts_out"], NT)
            for n in range(NT):
                product_u(0, n)
            for n in range(NT):
                if n < KC:
                    job("Wl1", n)
                product_sv(0, n)
                if n:
                    pe.wait_ge(S["g_made"], n)
                    job("g", n - 1)
            pe.wait_ge(S["g_made"], NT)
            job("g", NT - 1)
            for n in range(NT):
                if n < KC:
                    job("Wr1", n)
                product_u(1, n)
            for n in range(NT):
                if n < KC:
                    job("W1a", n)
                if n == KC:
                    job("W1b", 0)
                product_sv(1, n)
            for k in range(KC):
                job("W2", k)
            def job_h2(n):
                pe.wait_ge(S["h2_made"], n + 1)
                job("h2", n)
            job_h2(0)
            for n in range(NT):
                if n + 1 < NT:
                    job_h2(n + 1)
                pe.wait_ge(S["tr_lo"], JOB[("h2", n)] + 1)
                if n >= 2:
                    pe.wait_ge(S["p_made"], n - 1)
                product(bank[n % 2], nodes(hT, n), weights("W1a")).then_inc(S["p_done"], 1)
            for k in range(KC):
                job("ih_r", k)

            def transpose_edges(v):
                for j in range(U):
                    pe.wait_ge(ea_loaded[j], v * 16)
                    if j == 0:
                        pe.wait_ge(S["ea_lo"], v)
                    last = pe.transpose(bank[5][:, j * P:(j + 1) * P], ea[j][:, :], ident[:, :])
                last.then_inc(S["ea_T"], 1)

            def multiply_edges(v):
                pe.wait_ge(S["ea_lo"], v + 1)
                for j in range(U):
                    pe.wait_ge(S["q_used"], v * U + (j + 1))
                    pe.matmul(bank[j], eaT_hi[:, j, :], W1b_hi[:, :], start=True, stop=False)
                    pe.matmul(bank[j], eaT_hi[:, j, :], W1b_lo[:, :], start=False, stop=False)
                    pe.matmul(bank[j], eaT_lo[:, j, :], W1b_hi[:, :], start=False, stop=True)\
                      .then_inc(S["q_done"], 1)

            pe.wait_ge(S["p_made"], NT)
            pe.wait_ge(S["h_stored"], 16)
            pe.wait_ge(S["const"], 3)
            pe.sem_inc(S["ea_T"], 1)
            pe.sem_inc(S["ea_lo"], 1)
            pe.sem_inc(S["q_done"], U)
            pe.sem_inc(S["q_used"], 2 * U)
            pe.sem_inc(S["summed"], 2 * U)
            pe.sem_inc(S["msg_made"], U)
            pe.sem_inc(S["idx_made"], U)
            transpose_edges(1)
            multiply_edges(1)
            transpose_edges(2)
            for c in range(NT):
                if c >= 2:
                    pe.wait_ge(S["R_out"], c - 1)
                R = bank[3 + c % 2]
                pe.matmul(R, zeros[:, 0:P], zeros[:, :], start=True, stop=False)
                base, v0, v1 = chunk_visits(pe, c)
                with pe.Fori(v0, v1) as v:
                    multiply_edges(v + 1)
                    transpose_edges(v + 2)
                    pe.wait_ge(S["hot_made"], v)
                    for j in range(U):
                        pe.wait_ge(S["msg_made"], v * U + (j + 1))
                        pe.matmul(R, hot[j][:, :], msg[j][:, :], start=False, stop=False).then_inc(S["summed"], 1)
                pe.matmul(R, zeros[:, 0:P], zeros[:, :], start=False, stop=True).then_inc(S["R_done"], 1)
                if c:
                    pe.wait_ge(S["R_out"], c)
                    job("R", c - 1)
            pe.wait_ge(S["R_out"], NT)
            job("R", NT - 1)
            for c in range(NT):
                pe.wait_ge(S["diag_made"], c + 2)
                pe.matmul(bank[c // KC][:, (c % KC) * P:(c % KC + 1) * P], hot[2][:, :], hot[c % 2][:, :],
                          start=True, stop=True).then_inc(S["cntb_done"], 1)
            for k in range(KC):
                job("hh_r", k)
            w2 = slot[SLOT["W2"]]
            pe.wait_ge(S["cntb_out"], 1)
            for i in range(3 * KC):
                nb, oc = i // KC, i % KC
                w = min(D, NP - nb * D)
                if i == 0:
                    pe.wait_ge(S["tr_lo"], JOB[("R", NT - 1)] + 1)
                if i >= 6:
                    pe.wait_ge(S["agg_f"], i - 5)
                product(bank[i % 6][:, 0:w], tuple((lambda kc, y=y: y[:, kc, oc * P:(oc + 1) * P]) for y in w2),
                        tuple((lambda kc, y=y: y[:, kc, nb * D:nb * D + w]) for y in RT)).then_inc(S["agg_done"], 1)
            for n in range(NT):
                if n == 0:
                    pe.wait_ge(S["tr_lo"], LAST_JOB["hh_r"] + 1)
                    pe.wait_ge(S["agg_f"], 3 * KC)
                    pe.wait_ge(S["agg_lo"], 3 * KC)
                if n >= 2:
                    pe.wait_ge(S["r_sum"], n - 1)
                product(bank[n % 2], nodes(RT, n), weights("ih_r"), stop=False)
                product(bank[n % 2], nodes(hT, n), weights("hh_r"), start=False).then_inc(S["r_done"], 1)
                if n < KC:
                    job("ih_n", n)
            for k in range(KC):
                job("hh_n", k)
            for n in range(NT):
                if n >= 2:
                    pe.wait_ge(S["n_sum"], n - 1)
                product(bank[2 + n % 2], nodes(RT, n), weights("ih_n"))
                if n == 0:
                    pe.wait_ge(S["tr_lo"], LAST_JOB["hh_n"] + 1)
                product(bank[4 + n % 2], nodes(hT, n), weights("hh_n")).then_inc(S["n_done"], 1)
                if n < KC:
                    job("ih_z", n)
            for k in range(KC):
                job("hh_z", k)
            for n in range(NT):
                if n < 2:
                    pe.wait_ge(S["r_sum"], NT)
                else:
                    pe.wait_ge(S["z_sum"], n - 1)
                product(bank[n % 2], nodes(RT, n), weights("ih_z"), stop=False)
                if n == 0:
                    pe.wait_ge(S["tr_lo"], LAST_JOB["hh_z"] + 1)
                product(bank[n % 2], nodes(hT, n), weights("hh_z"), start=False).then_inc(S["z_done"], 1)


_INS = ['x', 'src', 'dst', 'edge_attr_128', 'L0_gnn_Wl0', 'L0_gnn_bl0', 'L0_gnn_Wr0', 'L0_gnn_Wl1', 'L0_gnn_bl1',
        'L0_gnn_Wr1', 'L1_gnn_W1', 'L1_gnn_b1', 'L1_gnn_W2', 'L1_gnn_b2', 'L1_gnn_W_ih', 'L1_gnn_W_hh',
        'L1_gnn_b_ih', 'L1_gnn_b_hh', 'L1_gnn_gamma', 'L1_gnn_beta', 'L1_gnn_run_mean', 'L1_gnn_run_var']


def kernel(**inputs):
    import numpy as _np
    import concourse.bacc as _bacc
    from concourse import mybir as _mybir
    from concourse.bass_utils import run_bass_kernel_spmd as _run

    nc = _bacc.Bacc("TRN2", target_bir_lowering=False, num_devices=1)
    arrays, args = {}, []
    for name in _INS:
        a = _np.ascontiguousarray(inputs[name])
        arrays[f"in_{name}"] = a
        args.append(nc.dram_tensor(f"in_{name}", a.shape, _mybir.dt.from_np(a.dtype), kind="ExternalInput").ap())
    f32 = _mybir.dt.float32
    args.append(nc.dram_tensor("out_0", (N, D), f32, kind="ExternalOutput").ap())
    args.append(nc.dram_tensor("p_table", (NP, D), f32, kind="Internal").ap())
    args.append(nc.dram_tensor("h_stash", (P, NT, D), f32, kind="Internal").ap())
    args.append(nc.dram_tensor("xh_stash", (P, NT, D), f32, kind="Internal").ap())
    build_gnn(nc, *args)
    r = _run(nc, [arrays], core_ids=[0])
    return r.results[0]["out_0"]
```

```python
import concourse.bass as bass
from concourse import mybir
from contextlib import ExitStack

P = 128
N = 1250
D = 512
ED = 128
E = 21250
NT = -(-N // P)
NP = NT * P
LAST = N - (NT - 1) * P
KC = D // P
ET = -(-E // P)
FULL = E // P
TAIL = E - FULL * P
U = 3
TC = 172
ROWS2 = ET - P
EPS = 1e-5

JOBS = []
for _c in range(NT):
    if _c < 2 * KC:
        JOBS.append((("Wl0", "Wr0")[_c // KC], _c % KC))
    if _c:
        JOBS.append(("h", _c - 1))
JOBS.append(("h", NT - 1))
for _n in range(NT):
    if _n < KC:
        JOBS.append(("Wl1", _n))
    if _n:
        JOBS.append(("g", _n - 1))
JOBS.append(("g", NT - 1))
JOBS += [("Wr1", k) for k in range(KC)]
JOBS += [("W1a", k) for k in range(KC)] + [("W1b", 0)]
JOBS += [("W2", k) for k in range(KC)]
JOBS += [("h2", n) for n in range(NT)]
JOBS += [("ih_r", k) for k in range(KC)]
JOBS += [("R", c) for c in range(NT)]
JOBS += [("hh_r", k) for k in range(KC)]
JOBS += [("ih_n", k) for k in range(KC)]
JOBS += [("hh_n", k) for k in range(KC)]
JOBS += [("ih_z", k) for k in range(KC)]
JOBS += [("hh_z", k) for k in range(KC)]
JOB = {name: i for i, name in enumerate(JOBS)}

STAGED = ["Wl0", "Wr0", "Wl1", "Wr1", "W1a", "W2", "ih_r", "hh_r", "ih_n", "hh_n", "ih_z", "hh_z"]
LAST_JOB = {w: JOB[(w, KC - 1)] for w in STAGED}
LAST_JOB["W1a"] = JOB[("W1b", 0)]
SLOT = {"Wl0": "A", "Wr0": "B", "Wl1": "A", "Wr1": "B", "W1a": "A", "W1b": "E", "W2": "B", "ih_r": "A",
        "hh_r": "C", "ih_n": "B", "hh_n": "A", "ih_z": "C", "hh_z": "B"}


def build_gnn(nc, x, src, dst, edge_attr, Wl0, bl0, Wr0, Wl1, bl1, Wr1, W1, b1, W2, b2, W_ih, W_hh,
              b_ih, b_hh, gamma, beta, run_mean, run_var, out, p_table, h_stash, xh_stash):
    f32, f32r, f16, i32 = mybir.dt.float32, mybir.dt.float32r, mybir.dt.float16, mybir.dt.int32
    ALU, ACT, AX = mybir.AluOpType, mybir.ActivationFunctionType, mybir.AxisListType

    weight_rows = {"Wl0": Wl0, "Wr0": Wr0, "Wl1": Wl1, "Wr1": Wr1, "W1a": W1, "W2": W2}
    for g, gate in enumerate("rzn"):
        weight_rows["ih_" + gate] = W_ih[g * D:(g + 1) * D, :]
        weight_rows["hh_" + gate] = W_hh[g * D:(g + 1) * D, :]

    with ExitStack() as ctx:
        KB = 1024
        top = [nc.sbuf_base + (-nc.sbuf_base) % 32]

        def region(nbytes):
            at = top[0]
            top[0] += nbytes
            assert top[0] <= nc.sbuf_usable_end, (top[0], nc.sbuf_usable_end)
            return at

        class Part:
            def __init__(self, start, nbytes):
                self.at, self.end = start, start + nbytes

            def __call__(self, name, shape, dt):
                size = mybir.dt.size(dt)
                for s in shape[1:]:
                    size *= s
                size += (-size) % 32
                t = nc.alloc_sbuf_tensor_at(name, shape, dt, offset=self.at)
                self.at += size
                assert self.at <= self.end, (name, self.at - self.end)
                return t

        def part(nbytes):
            return Part(region(nbytes), nbytes)

        misc = part(13 * KB + KB // 4)
        ident = misc("ident", [P, P], f32)
        cntb = Part(misc.at, 5 * KB)("cntb", [P, NP], f32)
        iota = misc("iota", [P, NP], f32)
        srcI = misc("srcI", [P, TC], i32)
        dstF = misc("dstF", [P, TC], f32)
        tab = misc("tab", [1, 32], i32)
        ea_row = misc("ea_row", [1, TC], i32)
        cnt = misc("cnt", [P, NT], f32)
        rcnt = misc("rcnt", [P, NT], f32)
        bn6 = misc("bn6", [P, NT, 6], f32)
        mv = misc("mv", [P, NT, 2], f32)
        ln = misc("ln", [P, 6, NT], f32)
        rstd = misc("rstd", [P, NT], f32)
        shift = misc("shift", [P, NT], f32)
        w1b_at = misc.at
        W1b_hi = misc("W1b_hi", [P, D], f32r)
        W1b_lo = misc("W1b_lo", [P, D], f32r)
        W1b_done = Part(w1b_at, 4 * KB)
        bin_b = W1b_done("bin_b", [P, D], f32)
        bhn_b = W1b_done("bhn_b", [P, D], f32)
        b2col = misc("b2col", [P, KC], f32)
        idx = misc("idx", [P, U], i32)
        sums = misc("sums", [P, 3, NT], f32)

        feat = part(40 * KB)
        feat_at = feat.at
        hT_hi = feat("hT_hi", [P, NT, D], f32r)
        hT_lo = feat("hT_lo", [P, NT, D], f32r)
        x1 = Part(feat_at, 20 * KB)("x1", [P, NT, D], f32)

        slots = part(32 * KB)
        slot = {s: (slots(f"slot{s}_hi", [P, KC, D], f32r), slots(f"slot{s}_lo", [P, KC, D], f32r))
                for s in "AB"}
        slot["E"] = (W1b_hi, W1b_lo)
        stage = part(10 * KB)("stage", [P, KC, D + ED], f32)

        big = region(70 * KB)
        sage = Part(big, 70 * KB)
        at_at = sage.at
        AT = sage("AT", [P, NT, NP], f32)
        AT_r = Part(at_at, 50 * KB)("AT_r", [P, NT, NP], f32r)
        u_at = sage.at
        u_hi = sage("u_hi", [P, NT, D], f32r)
        u_all = Part(u_at, 20 * KB)("u_all", [P, NT, D], f32)
        hots = Part(u_at, 20 * KB)
        hot_src = [hots(f"hot_src{j}", [P, NP], f16) for j in range(U)]
        hot_dst = [hots(f"hot_dst{j}", [P, P], f16) for j in range(U)]
        iota16 = hots("iota16", [P, NP], f16)
        srcF = hots("srcF", [P, TC], f32)
        ones16 = hots("ones16", [P, 1], f16)
        dcol = hots("dcol", [P, U], f32)
        zeros16 = hots("zeros16", [P, D], f16)
        rows = Part(big, 50 * KB)
        dst_i = rows("dst_i", [P, 2, P], i32)
        src_i = rows("src_i", [P, 2, P], i32)
        real_i = rows("real_i", [P, P], i32)
        dst_f = rows("dst_f", [P, 2, P], f32)
        src_f = rows("src_f", [P, 2, P], f32)
        real_f = rows("real_f", [P, P], f32)
        ends = rows("ends", [P, 4], f32)
        ends16 = rows("ends16", [P, 4, 16], f32)
        span = rows("span", [16, 8, ET], f32)
        tile_no = rows("tile_no", [16, ET], f32)
        tile_up = rows("tile_up", [16, ET], f32)
        chunk_lo = rows("chunk_lo", [16, 1], f32)
        chunk_hi = rows("chunk_hi", [16, 1], f32)
        reach = rows("reach", [16, 4], f32)
        line = rows("line", [1, 8, 32], f32)
        line_i = rows("line_i", [1, 2, 32], i32)

        late = Part(big, 70 * KB)
        RT_hi = late("RT_hi", [P, KC, NP], f32r)
        RT_lo = late("RT_lo", [P, KC, NP], f32r)
        late_at = late.at
        edge = Part(late_at, 30 * KB)
        gathered = [edge(f"gathered{j}", [P, D], f32) for j in range(U)]
        msg = [edge(f"msg{j}", [P, D], f32) for j in range(U)]
        msg_hi = edge("msg_hi", [P, D], f32r)
        msg_lo = edge("msg_lo", [P, D], f32r)
        ea = [edge(f"ea{j}", [P, ED], f32) for j in range(U)]
        eaT_hi = edge("eaT_hi", [P, U, P], f32r)
        eaT_lo = edge("eaT_lo", [P, U, P], f32r)
        hot = [edge(f"hot{j}", [P, P], f32r if j == 0 else f32) for j in range(U)]
        Rtmp = [edge(f"Rtmp{j}", [P, D], f32) for j in range(2)]
        zeros = edge("zeros", [P, D], f16)
        before = Part(big, 20 * KB)
        h2 = before("h2", [P, NT, D], f32)
        gru = Part(late_at, 30 * KB)
        slot["C"] = (gru("slotC_hi", [P, KC, D], f32r), gru("slotC_lo", [P, KC, D], f32r))
        ta = [gru(f"ta{j}", [P, D], f32) for j in range(2)]
        tb = [gru(f"tb{j}", [P, D], f32) for j in range(2)]
        tc = [gru(f"tc{j}", [P, D], f32) for j in range(2)]

        xs = part(20 * KB)
        x_at = xs.at
        xt = xs("xt", [P, NT, D], f32)
        u_lo = Part(x_at, 20 * KB)("u_lo", [P, NT, D], f32r)
        rn = Part(x_at, 20 * KB)("rn", [P, NT, D], f32)

        tmps = part(12 * KB)
        tmp_at = tmps.at
        ht = [tmps(f"ht{j}", [P, D], f32) for j in range(2)]
        va = [tmps(f"va{j}", [P, D], f32) for j in range(2)]
        za = [tmps(f"za{j}", [P, D], f32) for j in range(2)]
        gates = Part(tmp_at, 12 * KB)
        td = [gates(f"td{j}", [P, D], f32) for j in range(2)]
        te = [gates(f"te{j}", [P, D], f32) for j in range(2)]
        tf = [gates(f"tf{j}", [P, D], f32) for j in range(2)]

        bias = part(10 * KB)
        bias_at = bias.at
        bl0_b = bias("bl0_b", [P, D], f32)
        bl1_b = bias("bl1_b", [P, D], f32)
        b1_b = bias("b1_b", [P, D], f32)
        G_b = bias("G_b", [P, D], f32)
        B_b = bias("B_b", [P, D], f32)
        sage_done = Part(bias_at, 4 * KB)
        br_b = sage_done("br_b", [P, D], f32)
        bz_b = sage_done("bz_b", [P, D], f32)

        psA = [ctx.enter_context(nc.psum_tensor(f"psA{q}", [P, 3 * D], f32)) for q in range(2)]
        psT = [ctx.enter_context(nc.psum_tensor(f"psT{q}", [P, D], f32)) for q in range(2)]
        bank = [psA[b // 3][:, (b % 3) * D:(b % 3 + 1) * D] for b in range(6)]

        names = """idx_zero idx_loaded x_loaded const rows_f ends_made tables ends_bcast tile_tables
            reach_made reach_T tab_ready hot_ready hot_used counts_done counts_out counts_in ln_stats ln_sqrt ln_ready
            h_made staged tr_pe tr_hi tr_lo u_done u_out sv_done sv_read z_made g_made x1_made
            h2_made p_done p_made xh_made h_stored xh_stored bias_loaded bias_sqrt bias_made
            dst_made dcol_made msg_lo u_lo u_whole sums_made
            ea_T ea_hi ea_lo q_done q_used msg_made hot_made summed gate idx_made
            R_done R_out diag_made cntb_done cntb_out agg_done agg_f agg_hi agg_lo
            r_done r_sum r_made n_done n_hn n_mul n_bias n_sum n_made z_done z_sum z_gate z_diff z_mul
            z_base z_out dve_chain act_chain pool_chain sp_gate gate_bias n_bias_loaded""".split()
        S = {n: ctx.enter_context(nc.semaphore("s_" + n)) for n in names}
        x_again = [ctx.enter_context(nc.semaphore(f"s_x_again{j}")) for j in range(2)]
        p_stored = [ctx.enter_context(nc.semaphore(f"s_p_stored{j}")) for j in range(2)]
        ea_loaded = [ctx.enter_context(nc.semaphore(f"s_ea_loaded{j}")) for j in range(U)]
        p_gathered = [ctx.enter_context(nc.semaphore(f"s_p_gathered{j}")) for j in range(U)]
        h_loaded = [ctx.enter_context(nc.semaphore(f"s_h_loaded{j}")) for j in range(2)]
        xh_loaded = [ctx.enter_context(nc.semaphore(f"s_xh_loaded{j}")) for j in range(2)]
        out_stored = [ctx.enter_context(nc.semaphore(f"s_out_stored{j}")) for j in range(2)]

        block = ctx.enter_context(nc.Block())

        class Visits:
            def __init__(self, eng):
                self.eng, self.base, self.at = eng, [], []

            def load(self, c):
                if not self.at:
                    self.at.append(self.eng.value_load(tab[0:1, 16:17], min_val=1, max_val=700))
                while len(self.base) <= c:
                    k = len(self.base)
                    self.base.append(self.eng.value_load(tab[0:1, k:k + 1], min_val=-U * 700, max_val=ET))
                    self.at.append(self.eng.value_load(tab[0:1, 17 + k:18 + k], min_val=2, max_val=700))

            def of(self, c):
                self.load(c)
                return self.base[c], self.at[c], self.at[c + 1]

        def first_tile(eng, v, base):
            return nc.s_assert_within(eng.snap(v * U + base), 0, TC - U,
                                      skip_runtime_bounds_check_because="the tile tables bound the visits")

        @block.sync
        def _(sp):
            sp.wait_ge(S["idx_zero"], 2)
            for t, a in ((dst_i, dst), (src_i, src)):
                sp.dma_start(t[:, 0, :], a[0:P * P].rearrange("(t p) -> t p", p=P)).then_inc(S["idx_loaded"], 16)
                sp.dma_start(t[0:FULL - P, 1, :], a[P * P:FULL * P].rearrange("(t p) -> t p", p=P))\
                  .then_inc(S["idx_loaded"], 16)
            sp.dma_start(dst_i[FULL - P:FULL - P + 1, 1, P - TAIL:P], dst[FULL * P:E].unsqueeze(0))\
              .then_inc(S["idx_loaded"], 16)
            sp.dma_start(src_i[FULL - P:FULL - P + 1, 1, :], src[E - P:E].unsqueeze(0)).then_inc(S["idx_loaded"], 16)
            sp.dma_start(real_i[0:FULL - P, :], dst[P * P:FULL * P].rearrange("(t p) -> t p", p=P))\
              .then_inc(S["idx_loaded"], 16)
            sp.dma_start(real_i[FULL - P:FULL - P + 1, :], dst[E - P:E].unsqueeze(0)).then_inc(S["idx_loaded"], 16)

            def stage_weights(w):
                if STAGED.index(w):
                    sp.wait_ge(S["tr_pe"], LAST_JOB[STAGED[STAGED.index(w) - 1]] + 1)
                rows_of = weight_rows[w]
                sp.dma_start(stage[:, :, 0:rows_of.shape[1]], rows_of.rearrange("(b p) k -> p b k", p=P))\
                  .then_inc(S["staged"], 16)

            sp.wait_ge(S["idx_loaded"], 16 * 8)
            stage_weights("Wl0")
            sp.wait_ge(S["x_loaded"], 32)
            for t, a in ((bl0_b, bl0), (bl1_b, bl1), (b1_b, b1), (G_b, run_var), (B_b, beta),
                         (za[0], gamma), (za[1], run_mean)):
                sp.dma_start(t[:, :], a.partition_broadcast(P)).then_inc(S["bias_loaded"], 16)
            sp.dma_start(b2col[:, :], b2.rearrange("(k p) -> p k", p=P), allow_slow_non_contiguous=True)\
              .then_inc(S["bias_loaded"], 16)
            for w in STAGED[1:5]:
                stage_weights(w)
            stage_weights("W2")
            sp.wait_ge(S["tab_ready"], 1)
            sp.wait_ge(S["counts_in"], 1)
            visits = Visits(sp)
            visits.load(NT - 1)
            sp.wait_ge(S["x1_made"], NT)
            for t, a in ((br_b, b_ih[0:D]), (bz_b, b_ih[D:2 * D]), (za[0], b_hh[0:D]), (za[1], b_hh[D:2 * D])):
                sp.dma_start(t[:, :], a.partition_broadcast(P)).then_inc(S["gate_bias"], 16)
            stage_weights("ih_r")
            for c in range(NT):
                base, v0, v1 = visits.of(c)
                with sp.Fori(v0, v1) as v:
                    t = first_tile(sp, v, base)
                    row = [sp.value_load(ea_row[0:1, bass.ds(t + j, 1)], min_val=0, max_val=E - P) for j in range(U)]
                    sp.wait_ge(S["ea_T"], v)
                    sp.sem_inc(S["sp_gate"], 1)
                    for j in range(U):
                        sp.dma_start(ea[j][:, :], edge_attr[bass.ds(row[j], P), :]).then_inc(ea_loaded[j], 16)
                if c == 0:
                    stage_weights("hh_r")
            end = visits.at[NT]
            for k in range(2):
                sp.wait_ge(S["ea_T"], end + k)
                sp.sem_inc(S["sp_gate"], 1)
                for j in range(U):
                    sp.dma_start(ea[j][:, :], edge_attr[0:P, :]).then_inc(ea_loaded[j], 16)
            sp.wait_ge(S["R_done"], NT)
            for t, a in ((bin_b, b_ih[2 * D:3 * D]), (bhn_b, b_hh[2 * D:3 * D])):
                sp.dma_start(t[:, :], a.partition_broadcast(P)).then_inc(S["n_bias_loaded"], 16)
            for w in ("ih_n", "hh_n", "ih_z", "hh_z"):
                stage_weights(w)
            for n in range(NT):
                size = P if n < NT - 1 else LAST
                if n >= 2:
                    sp.wait_ge(S["z_diff"], n - 1)
                else:
                    sp.wait_ge(S["n_made"], NT - 1 + n)
                sp.dma_start(te[n % 2][:, :], h_stash[:, n, :]).then_inc(h_loaded[n % 2], 16)
                if n >= 2:
                    sp.wait_ge(S["z_out"], n - 1)
                sp.dma_start(tf[n % 2][:, :], xh_stash[:, n, :]).then_inc(xh_loaded[n % 2], 16)
                if n >= 1:
                    sp.wait_ge(S["z_out"], n)
                    sp.dma_start(out[(n - 1) * P:n * P, :], tc[(n - 1) % 2][:, :])\
                      .then_inc(out_stored[(n - 1) % 2], 16)
            sp.wait_ge(S["z_out"], NT)
            sp.dma_start(out[(NT - 1) * P:N, :], tc[(NT - 1) % 2][0:LAST, :]).then_inc(out_stored[(NT - 1) % 2], 16)
            for j in range(2):
                sp.wait_ge(out_stored[j], 16 * (NT // 2))

        @block.gpsimd
        def _(pool):
            chain = [0]

            def link(ins):
                chain[0] += 1
                ins.then_inc(S["pool_chain"], 1)
                pool.wait_ge(S["pool_chain"], chain[0])

            pool.memset(dst_i[:, 1, :], -1).then_inc(S["idx_zero"], 1)
            pool.memset(src_i[:, 1, :], 0).then_inc(S["idx_zero"], 1)
            link(pool.memset(ident[:, :], 0.0))
            link(pool.affine_select(out=ident[:, :], in_=ident[:, :], compare_op=ALU.not_equal, fill=1.0,
                                    base=0, pattern=[[-1, P]], channel_multiplier=1))
            pool.iota(chunk_lo[:, :], pattern=[[0, 1]], base=0, channel_multiplier=P,
                      allow_small_or_imprecise_dtypes=True)
            pool.iota(chunk_hi[:, :], pattern=[[0, 1]], base=P - 1, channel_multiplier=P,
                      allow_small_or_imprecise_dtypes=True)
            pool.iota(tile_no[:, :], pattern=[[1, ET]], base=-1000, channel_multiplier=0,
                      allow_small_or_imprecise_dtypes=True)
            pool.iota(tile_up[:, :], pattern=[[1, ET]], base=1, channel_multiplier=0,
                      allow_small_or_imprecise_dtypes=True)
            pool.memset(line[:, :, :], 0.0)
            pool.memset(xt[:, NT - 1, :], 0.0).then_inc(S["const"], 1)
            pool.iota(iota16[:, :], pattern=[[1, NP]], base=0, channel_multiplier=0,
                      allow_small_or_imprecise_dtypes=True)
            pool.iota(iota[:, :], pattern=[[1, NP]], base=0, channel_multiplier=0,
                      allow_small_or_imprecise_dtypes=True)
            pool.memset(ones16[:, :], 1.0)
            pool.memset(zeros16[:, :], 0.0).then_inc(S["const"], 1)
            link(pool.iota(ea_row[:, :], pattern=[[P, TC]], base=0, channel_multiplier=0))
            link(pool.tensor_scalar(ea_row[:, :], ea_row[:, :], E - P, None, ALU.min))
            pool.memset(tab[0:1, 28:32], 0).then_inc(S["counts_in"], 1)

            pool.wait_ge(S["tab_ready"], 1)
            visits = Visits(pool)
            pool.wait_ge(S["tile_tables"], 1)
            for c in range(NT):
                base, v0, v1 = visits.of(c)
                with pool.Fori(v0, v1) as v:
                    t = first_tile(pool, v, base)
                    pool.wait_ge(S["dst_made"], v * U)
                    pool.sem_inc(S["gate"], 1)
                    pool.tensor_copy(dcol[:, :], dstF[:, bass.ds(t, U)]).then_inc(S["dcol_made"], 1)
                    pool.wait_ge(S["dcol_made"], v)
                    pool.sem_inc(S["gate"], 1)
                    for j in range(U):
                        pool.wait_ge(S["hot_used"], v * U + (j + 1))
                        pool.sem_inc(S["gate"], 1)
                        pool.tensor_scalar(hot_dst[j][:, :], iota16[:, c * P:(c + 1) * P],
                                           dcol[:, j:j + 1], None, ALU.is_equal)\
                            .then_inc(S["dst_made"], 1)

            for n in range(NT):
                pool.wait_ge(S["h2_made"], n + 1)
                pool.tensor_tensor(xt[:, n, :], x1[:, n, :], h2[:, n, :], ALU.add).then_inc(S["xh_made"], 1)

            pool.memset(zeros[:, :], 0.0).then_inc(S["const"], 1)
            def gather(j, table=p_table):
                pool.indirect_dma_start(
                    out=gathered[j][:, :], out_offset=None, in_=table[:, :],
                    in_offset=bass.IndirectOffsetOnAxis(ap=idx[:, j:j + 1], axis=0)).then_inc(p_gathered[j], 16)

            link(pool.memset(idx[:, :], 0))
            for j in range(U):
                gather(j, x)
            pool.wait_ge(p_stored[0], 16 * (NT // 2))
            pool.wait_ge(p_stored[1], 16 * (NT // 2))
            for c in range(NT):
                base, v0, v1 = visits.of(c)
                with pool.Fori(v0, v1) as v:
                    t = first_tile(pool, v, base)
                    for j in range(U):
                        pool.wait_ge(p_gathered[j], v * 16)
                        pool.sem_inc(S["gate"], 1)
                        pool.tensor_copy(idx[:, j:j + 1], srcI[:, bass.ds(t + j, 1)]).then_inc(S["idx_made"], 1)
                        pool.wait_ge(S["q_used"], v * U + (j + 1))
                        pool.wait_ge(S["idx_made"], v * U + (j + 1))
                        pool.sem_inc(S["gate"], 1)
                        gather(j)
            end = visits.at[NT]
            for j in range(U):
                pool.wait_ge(S["q_used"], end * U + (j + 1))
                pool.sem_inc(S["gate"], 1)
                gather(j)

            pool.wait_ge(S["xh_stored"], 16 * NT)
            pool.wait_ge(S["n_bias_loaded"], 32)
            for n in range(NT):
                pool.wait_ge(S["n_hn"], n + 1)
                pool.tensor_tensor(ta[n % 2][:, :], ta[n % 2][:, :], rn[:, n, :], ALU.mult).then_inc(S["n_mul"], 1)
                pool.wait_ge(S["n_mul"], n + 1)
                pool.tensor_tensor(ta[n % 2][:, :], ta[n % 2][:, :], bin_b[:, :], ALU.add).then_inc(S["n_bias"], 1)
            for n in range(NT):
                pool.wait_ge(S["n_made"], n + 1)
                pool.wait_ge(h_loaded[n % 2], 16 * (n // 2 + 1))
                if n >= 2:
                    pool.wait_ge(S["z_mul"], n - 1)
                pool.tensor_tensor(td[n % 2][:, :], te[n % 2][:, :], rn[:, n, :], ALU.subtract)\
                    .then_inc(S["z_diff"], 1)
                pool.wait_ge(xh_loaded[n % 2], 16 * (n // 2 + 1))
                pool.tensor_tensor(tf[n % 2][:, :], tf[n % 2][:, :], B_b[:, :], ALU.add).then_inc(S["z_base"], 1)

        @block.scalar
        def _(act):
            act.wait_ge(S["const"], 1)
            act.wait_ge(S["idx_loaded"], 16 * 8)
            act.dma_start(xt[:, 0:NT - 1, :], x[0:(NT - 1) * P, :].rearrange("(n p) d -> p n d", p=P))\
               .then_inc(S["x_loaded"], 16)
            act.dma_start(xt[0:LAST, NT - 1, :], x[(NT - 1) * P:N, :]).then_inc(S["x_loaded"], 16)
            def ln_root(k):
                act.wait_ge(S["ln_stats"], k + 1)
                act.activation(ln[:, 1, :], ln[:, 0, :], ACT.Sqrt).then_inc(S["ln_sqrt"], 1)

            def hi_part(name, k):
                j = JOB[(name, k)]
                act.wait_ge(S["tr_pe"], j + 1)
                if name in ("h", "g", "h2"):
                    o = hT_hi[:, k, :]
                elif name == "R":
                    o = RT_hi[:, :, k * P:(k + 1) * P]
                elif name == "W1b":
                    o = W1b_hi[:, :]
                else:
                    o = slot[SLOT[name]][0][:, k, :]
                i = psT[j % 2][:, :]
                if name == "R":
                    i = i.rearrange("p (k n) -> p k n", k=KC)
                act.activation(o, i, ACT.Copy).then_inc(S["tr_hi"], 1)

            act.wait_ge(S["x_loaded"], 32)
            for n in range(NT):
                if n >= 2:
                    act.wait_ge(S["sums_made"], n - 1)
                act.activation(va[n % 2][:, :], xt[:, n, :], ACT.Copy, accum_out=sums[:, 0, n:n + 1])\
                   .then_inc(S["sums_made"], 1)
            act.wait_ge(S["sums_made"], NT)
            act.activation(sums[:, 1, :], sums[:, 0, :], ACT.Copy, scale=-1.0 / D).then_inc(S["sums_made"], 1)
            act.wait_ge(S["sums_made"], NT + 1)
            for n in range(NT):
                if n >= 2:
                    act.wait_ge(S["sums_made"], NT + n)
                act.activation(va[n % 2][:, :], xt[:, n, :], ACT.Square, bias=sums[:, 1, n:n + 1],
                               accum_out=sums[:, 2, n:n + 1]).then_inc(S["sums_made"], 1)

            def make_h(c):
                if c < 2:
                    act.wait_ge(S["ln_ready"], 1)
                else:
                    act.wait_ge(S["tr_pe"], JOB[("h", c - 2)] + 1)
                act.activation(ht[c % 2][:, :], xt[:, c, :], ACT.Relu, bias=shift[:, c:c + 1],
                               scale=rstd[:, c:c + 1]).then_inc(S["h_made"], 1)

            act.wait_ge(S["tab_ready"], 1)
            exact = act.value_load(tab[0:1, 27:28], min_val=0, max_val=1)
            for c in range(NT):
                act.wait_ge(S["counts_done"], c + 1)
                counts = psA[c % 2][:, 0:NP].rearrange("p (s d) -> p s d", s=NT)
                with act.If(exact > 0):
                    act.activation(AT[:, :, c * P:(c + 1) * P], counts, ACT.Copy)
                with act.Else():
                    act.activation(AT_r[:, :, c * P:(c + 1) * P], counts, ACT.Copy)
                act.activation(cnt[:, c:c + 1], psA[c % 2][:, NP:NP + 1], ACT.Copy).then_inc(S["counts_out"], 1)
                if c < 2 * KC:
                    hi_part(("Wl0", "Wr0")[c // KC], c % KC)
                if c == 0:
                    ln_root(0)
                    make_h(0)
                    make_h(1)
                else:
                    hi_part("h", c - 1)
                    if c + 1 < NT:
                        make_h(c + 1)
            hi_part("h", NT - 1)

            def u_out(layer, n):
                act.wait_ge(S["u_done"], layer * NT + n + 1)
                act.activation(u_hi[:, n, :], bank[n % 2], ACT.Copy).then_inc(S["u_out"], 1)

            for n in range(NT):
                u_out(0, n)
            act.wait_ge(S["bias_sqrt"], 1)
            act.activation(G_b[:, :], G_b[:, :], ACT.Sqrt).then_inc(S["bias_sqrt"], 1)
            for n in range(NT):
                if n < KC:
                    hi_part("Wl1", n)
                act.wait_ge(S["z_made"], n + 1)
                if n >= 2:
                    act.wait_ge(S["tr_pe"], JOB[("g", n - 2)] + 1)
                act.activation(ht[n % 2][:, :], za[n % 2][:, :], ACT.Relu).then_inc(S["g_made"], 1)
                if n:
                    hi_part("g", n - 1)
            hi_part("g", NT - 1)
            for n in range(NT):
                if n < KC:
                    hi_part("Wr1", n)
                u_out(1, n)
            def reload_x(n):
                act.dma_start(ht[n % 2][0:P if n < NT - 1 else LAST, :], x[n * P:min((n + 1) * P, N), :])\
                   .then_inc(x_again[n % 2], 16)
            reload_x(0)
            reload_x(1)
            for n in range(NT):
                if n < KC:
                    hi_part("W1a", n)
                if n == KC:
                    hi_part("W1b", 0)
                if n + 2 < NT:
                    act.wait_ge(S["x1_made"], n + 1)
                    reload_x(n + 2)
            ln_root(1)
            for n in range(KC):
                hi_part("W2", n)
            act.wait_ge(S["ln_ready"], 2)

            def make_h2(n):
                act.activation(h2[:, n, :], x1[:, n, :], ACT.Relu, bias=shift[:, n:n + 1],
                               scale=rstd[:, n:n + 1]).then_inc(S["h2_made"], 1)

            def store_p(n):
                act.wait_ge(S["p_made"], n + 1)
                act.dma_start(p_table[n * P:(n + 1) * P, :], va[n % 2][:, :]).then_inc(p_stored[n % 2], 16)

            make_h2(0)
            make_h2(1)
            for n in range(NT):
                if n + 2 < NT:
                    make_h2(n + 2)
                act.wait_ge(S["xh_made"], n + 1)
                hi_part("h2", n)
                act.wait_ge(S["h2_made"], n + 1)
                act.dma_start(h_stash[:, n, :], h2[:, n, :]).then_inc(S["h_stored"], 16)
                if n >= 2:
                    store_p(n - 2)
            store_p(NT - 2)
            store_p(NT - 1)
            for n in range(KC):
                hi_part("ih_r", n)

            def hi_of_edges(v):
                act.wait_ge(S["ea_T"], v + 1)
                act.wait_ge(S["q_done"], U * v)
                act.activation(eaT_hi[:, :, :], bank[5][:, 0:U * P].rearrange("p (j e) -> p j e", j=U),
                               ACT.Copy).then_inc(S["ea_hi"], 1)

            def relu_messages(v):
                for j in range(U):
                    act.wait_ge(S["q_used"], v * U + (U + j + 1))
                    act.activation(msg[j][:, :] if j else msg_hi[:, :], msg[j][:, :], ACT.Relu)\
                       .then_inc(S["msg_made"], 1)

            visits = Visits(act)
            visits.load(NT - 1)
            hi_of_edges(1)
            hi_of_edges(2)
            relu_messages(1)
            for c in range(NT):
                base, v0, v1 = visits.of(c)
                with act.Fori(v0, v1) as v:
                    hi_of_edges(v + 2)
                    relu_messages(v + 1)
                act.dma_start(xh_stash[:, c, :], xt[:, c, :]).then_inc(S["xh_stored"], 16)
                act.wait_ge(S["R_done"], c + 1)
                if c >= 2:
                    act.wait_ge(S["tr_pe"], JOB[("R", c - 2)] + 1)
                act.activation(Rtmp[c % 2][:, :], bank[3 + c % 2], ACT.Copy).then_inc(S["R_out"], 1)
                if c == 1:
                    act.wait_ge(S["h_stored"], 16 * NT)
                if c:
                    hi_part("R", c - 1)
            hi_part("R", NT - 1)
            for n in range(KC):
                hi_part("hh_r", n)
            for i in range(3 * KC):
                nb, oc = i // KC, i % KC
                act.wait_ge(S["agg_f"], i + 1)
                act.wait_ge(S["agg_done"], KC * (nb + 1))
                w = min(D, NP - nb * D)
                act.activation(RT_hi[:, oc, nb * D:nb * D + w], ta[i % 2][:, 0:w], ACT.Copy).then_inc(S["agg_hi"], 1)
            act.wait_ge(S["xh_stored"], 16 * NT)
            for n in range(NT):
                act.wait_ge(S["r_sum"], n + 1)
                act.activation(rn[:, n, :], tb[n % 2][:, :], ACT.Sigmoid).then_inc(S["r_made"], 1)
                if n < KC:
                    hi_part("ih_n", n)
            for k in range(KC):
                hi_part("hh_n", k)
            for n in range(NT):
                act.wait_ge(S["n_sum"], n + 1)
                act.activation(rn[:, n, :], te[n % 2][:, :], ACT.Tanh).then_inc(S["n_made"], 1)
                if n < KC:
                    hi_part("ih_z", n)
            for k in range(KC):
                hi_part("hh_z", k)
            for n in range(NT):
                act.wait_ge(S["z_sum"], n + 1)
                act.activation(tb[n % 2][:, :], tb[n % 2][:, :], ACT.Sigmoid).then_inc(S["z_gate"], 1)

        @block.vector
        def _(dve):
            chain = [0]

            def link(ins):
                chain[0] += 1
                ins.then_inc(S["dve_chain"], 1)
                dve.wait_ge(S["dve_chain"], chain[0])

            dve.wait_ge(S["idx_loaded"], 16 * 8)
            dve.tensor_copy(real_f[0:ROWS2, :], real_i[0:ROWS2, :])
            dve.tensor_copy(src_f[:, :, :], src_i[:, :, :])
            link(dve.tensor_copy(dst_f[:, :, :], dst_i[:, :, :]))
            S_rows = S["rows_f"]
            dve.tensor_reduce(ends[:, 0:1], dst_f[:, 0, :], AX.X, ALU.min)
            dve.tensor_reduce(ends[:, 1:2], dst_f[:, 0, :], AX.X, ALU.max)
            dve.tensor_reduce(ends[0:ROWS2, 2:3], real_f[0:ROWS2, :], AX.X, ALU.min)
            link(dve.tensor_reduce(ends[0:ROWS2, 3:4], real_f[0:ROWS2, :], AX.X, ALU.max))
            dve.tensor_copy(ends16[:, 0:2, :], ends[:, 0:2].unsqueeze(2).to_broadcast([P, 2, 16]))
            dve.tensor_copy(ends16[0:ROWS2, 2:4, :], ends[0:ROWS2, 2:4].unsqueeze(2).to_broadcast([ROWS2, 2, 16]))\
               .then_inc(S["ends_made"], 1)
            dve.wait_ge(S["const"], 1)
            dve.wait_ge(S["ends_bcast"], 1)
            dve.tensor_copy(span[:, 0, :], psT[1][0:16, 0:ET])
            link(dve.tensor_copy(span[:, 1, :], psT[1][0:16, 256:256 + ET]))
            link(dve.tensor_scalar(span[:, 2, :], span[:, 0, :], chunk_hi[:, 0:1], None, ALU.is_le))
            link(dve.scalar_tensor_tensor(span[:, 3, :], span[:, 1, :], chunk_lo[:, 0:1], span[:, 2, :],
                                          ALU.is_ge, ALU.mult))
            dve.tensor_tensor(span[:, 4, :], span[:, 3, :], tile_no[:, :], ALU.mult)
            link(dve.tensor_tensor(span[:, 5, :], span[:, 3, :], tile_up[:, :], ALU.mult))
            dve.tensor_reduce(reach[:, 0:1], span[:, 4, :], AX.X, ALU.min)
            link(dve.tensor_reduce(reach[:, 1:2], span[:, 5, :], AX.X, ALU.max))
            link(dve.tensor_scalar(reach[:, 2:3], reach[:, 0:1], 1000.0, float(ET - 1), ALU.add, ALU.min))
            link(dve.scalar_tensor_tensor(reach[:, 3:4], reach[:, 2:3], 1.0, reach[:, 1:2], ALU.add, ALU.max))
            dve.tensor_copy(reach[:, 0:1], reach[:, 2:3]).then_inc(S["reach_made"], 1)
            dve.wait_ge(S["tables"], 1)
            dve.tensor_copy(dstF[:, :], psT[0][:, 0:TC])
            dve.tensor_copy(srcI[:, :], psT[0][:, 256:256 + TC])
            dve.tensor_copy(srcF[:, :], psT[0][:, 256:256 + TC]).then_inc(S["tile_tables"], 1)
            dve.wait_ge(S["reach_T"], 1)
            dve.tensor_copy(line[0:1, 0, 0:NT], psT[1][0:1, 0:NT])
            link(dve.tensor_copy(line[0:1, 1, 0:NT], psT[1][0:1, 16:16 + NT]))
            link(dve.tensor_tensor(line[0:1, 2, 0:NT], line[0:1, 1, 0:NT], line[0:1, 0, 0:NT], ALU.subtract))
            link(dve.tensor_reduce(line[0:1, 5, 0:1], line[0:1, 2, 0:NT], AX.X, ALU.max))
            link(dve.tensor_scalar(line[0:1, 6, 0:1], line[0:1, 5, 0:1], float(4096 // P), None, ALU.is_gt))
            dve.tensor_copy(tab[0:1, 27:28], line[0:1, 6, 0:1])
            link(dve.tensor_scalar(line_i[0:1, 0, 0:NT], line[0:1, 2, 0:NT], float(U - 1), 43691.0, ALU.add, ALU.mult))
            link(dve.tensor_scalar(line_i[0:1, 1, 0:NT], line_i[0:1, 0, 0:NT], 17, None, ALU.logical_shift_right))
            link(dve.tensor_copy(line[0:1, 3, 16:16 + NT], line_i[0:1, 1, 0:NT]))
            for k in range(4):
                s = 1 << k
                link(dve.tensor_tensor(line[0:1, 4 + k, 16:16 + NT], line[0:1, 3 + k, 16:16 + NT],
                                       line[0:1, 3 + k, 16 - s:16 + NT - s], ALU.add))
            link(dve.tensor_scalar(line[0:1, 4, 15:16 + NT], line[0:1, 7, 15:16 + NT], 1.0, None, ALU.add))
            dve.tensor_copy(tab[0:1, 16:17 + NT], line[0:1, 4, 15:16 + NT])
            dve.scalar_tensor_tensor(tab[0:1, 0:NT], line[0:1, 4, 15:15 + NT], -float(U), line[0:1, 0, 0:NT],
                                     ALU.mult, ALU.add).then_inc(S["tab_ready"], 1)

            def ln_finish(k):
                dve.tensor_scalar(ln[:, 0, :], mv[:, :, 1], EPS, None, ALU.add).then_inc(S["ln_stats"], 1)
                dve.wait_ge(S["ln_sqrt"], k + 1)
                link(dve.reciprocal(ln[:, 2, :], ln[:, 1, :]))
                link(dve.tensor_tensor(ln[:, 3, :], ln[:, 2, :], ln[:, 2, :], ALU.mult))
                link(dve.tensor_tensor(ln[:, 4, :], ln[:, 3, :], ln[:, 0, :], ALU.mult))
                link(dve.tensor_scalar(ln[:, 5, :], ln[:, 4, :], -0.5, 1.5, ALU.mult, ALU.add))
                link(dve.tensor_tensor(rstd[:, :], ln[:, 5, :], ln[:, 2, :], ALU.mult))
                dve.scalar_tensor_tensor(shift[:, :], mv[:, :, 0], -1.0, rstd[:, :], ALU.mult, ALU.mult)\
                   .then_inc(S["ln_ready"], 1)

            def lo_part(name, k):
                j = JOB[(name, k)]
                dve.wait_ge(S["tr_hi"], j + 1)
                if name in ("h", "g", "h2"):
                    hi, lo = (t[:, k, :] for t in (hT_hi, hT_lo))
                elif name == "R":
                    hi, lo = (t[:, :, k * P:(k + 1) * P] for t in (RT_hi, RT_lo))
                elif name == "W1b":
                    hi, lo = W1b_hi[:, :], W1b_lo[:, :]
                else:
                    hi, lo = (t[:, k, :] for t in slot[SLOT[name]])
                i = psT[j % 2][:, :]
                if name == "R":
                    i = i.rearrange("p (k n) -> p k n", k=KC)
                dve.tensor_tensor(lo, i, hi.bitcast(f32), ALU.subtract).then_inc(S["tr_lo"], 1)

            dve.wait_ge(S["const"], 2)
            dve.wait_ge(S["tab_ready"], 1)
            visits = Visits(dve)
            dve.wait_ge(S["tile_tables"], 1)
            for c in range(NT):
                base, v0, v1 = visits.of(c)
                with dve.Fori(v0, v1) as v:
                    t = first_tile(dve, v, base)
                    for j in range(U):
                        dve.wait_ge(S["hot_used"], v * U + (j + 1))
                        dve.tensor_scalar(hot_src[j][:, :], iota16[:, :], srcF[:, bass.ds(t + j, 1)], None,
                                          ALU.is_equal).then_inc(S["hot_ready"], 1)
                if 0 < c <= 2 * KC:
                    lo_part(("Wl0", "Wr0")[(c - 1) // KC], (c - 1) % KC)
                if c == 0:
                    dve.wait_ge(S["sums_made"], 2 * NT + 1)
                    dve.tensor_scalar(mv[:, :, 0], sums[:, 1, :], -1.0, None, ALU.mult)
                    link(dve.tensor_scalar(mv[:, :, 1], sums[:, 2, :], 1.0 / D, None, ALU.mult))
                    ln_finish(0)
                if c >= 2:
                    lo_part("h", c - 2)
            lo_part("h", NT - 2)
            lo_part("h", NT - 1)
            dve.wait_ge(S["counts_out"], NT)
            link(dve.tensor_scalar(rcnt[:, :], cnt[:, :], 1.0, None, ALU.max))
            link(dve.reciprocal(rcnt[:, :], rcnt[:, :]))

            def u_whole(layer):
                dve.wait_ge(S["u_lo"], (layer + 1) * NT)
                with dve.If(exact > 0):
                    for n in range(NT):
                        dve.tensor_tensor(u_all[:, n, :], u_hi[:, n, :].bitcast(f32), u_lo[:, n, :].bitcast(f32),
                                          ALU.add)
                dve.drain().then_inc(S["u_whole"], 1)

            def u_lo_of(layer, n):
                dve.wait_ge(S["u_out"], layer * NT + n + 1)
                dve.tensor_tensor(u_lo[:, n, :], bank[n % 2], u_hi[:, n, :].bitcast(f32), ALU.subtract)\
                   .then_inc(S["u_lo"], 1)

            exact = dve.value_load(tab[0:1, 27:28], min_val=0, max_val=1)
            for n in range(NT):
                u_lo_of(0, n)
            u_whole(0)
            dve.wait_ge(S["bias_loaded"], 16 * 8)
            link(dve.tensor_scalar(G_b[:, :], G_b[:, :], EPS, None, ALU.add))
            dve.tensor_scalar(za[1][:, :], za[1][:, :], -1.0, None, ALU.mult)
            dve.tensor_copy(va[0][:, :], G_b[:, :]).then_inc(S["bias_sqrt"], 1)
            dve.wait_ge(S["bias_sqrt"], 2)
            link(dve.reciprocal(va[1][:, :], G_b[:, :]))
            link(dve.tensor_tensor(G_b[:, :], va[1][:, :], va[1][:, :], ALU.mult))
            link(dve.tensor_tensor(G_b[:, :], G_b[:, :], va[0][:, :], ALU.mult))
            link(dve.tensor_scalar(G_b[:, :], G_b[:, :], -0.5, 1.5, ALU.mult, ALU.add))
            link(dve.tensor_tensor(G_b[:, :], G_b[:, :], va[1][:, :], ALU.mult))
            link(dve.tensor_tensor(G_b[:, :], G_b[:, :], za[0][:, :], ALU.mult))
            link(dve.tensor_tensor(za[1][:, :], za[1][:, :], G_b[:, :], ALU.mult))
            link(dve.tensor_tensor(B_b[:, :], B_b[:, :], za[1][:, :], ALU.add))

            def sage_sum(layer, n):
                dve.wait_ge(S["sv_done"], layer * NT + n + 1)
                if layer == 0 and n >= 2:
                    dve.wait_ge(S["g_made"], n - 1)
                link(dve.tensor_tensor(va[n % 2][:, :], bank[4 + n % 2], (bl0_b, bl1_b)[layer][:, :], ALU.add))
                dve.scalar_tensor_tensor(za[n % 2][:, :], bank[2 + n % 2], rcnt[:, n:n + 1], va[n % 2][:, :],
                                         ALU.mult, ALU.add).then_inc(S["z_made"], 1)

            for n in range(NT):
                if n < KC:
                    lo_part("Wl1", n)
                sage_sum(0, n)
                if n:
                    lo_part("g", n - 1)
            lo_part("g", NT - 1)
            for n in range(NT):
                if n < KC:
                    lo_part("Wr1", n)
                u_lo_of(1, n)
            u_whole(1)
            for n in range(NT):
                sage_sum(1, n)
                dve.wait_ge(S["z_made"], NT + n + 1)
                dve.wait_ge(x_again[n % 2], 16 * (n // 2 + 1))
                dve.scalar_tensor_tensor(x1[:, n, :], za[n % 2][:, :], 0.0, ht[n % 2][:, :], ALU.max, ALU.add)\
                   .then_inc(S["x1_made"], 1)
                dve.wait_ge(S["x1_made"], n + 1)
                if n < KC:
                    lo_part("W1a", n)
                if n == KC:
                    lo_part("W1b", 0)
                link(dve.bn_stats(bn6[:, n, :], x1[:, n, :]))
                last = dve.bn_aggr(mv[:, n, :], bn6[:, n, :])
            link(last)
            ln_finish(1)
            for k in range(KC):
                lo_part("W2", k)
            for n in range(NT + 1):
                if n < NT:
                    lo_part("h2", n)
                if n:
                    m = n - 1
                    dve.wait_ge(S["p_done"], m + 1)
                    if m >= 2:
                        dve.wait_ge(p_stored[m % 2], 16 * (m // 2))
                    dve.tensor_tensor(va[m % 2][:, :], bank[m % 2], b1_b[:, :], ALU.add).then_inc(S["p_made"], 1)
            for k in range(KC):
                lo_part("ih_r", k)

            def lo_of_edges(v):
                dve.wait_ge(S["ea_hi"], v)
                dve.tensor_tensor(eaT_lo[:, :, :], bank[5][:, 0:U * P].rearrange("p (j e) -> p j e", j=U),
                                  eaT_hi[:, :, :].bitcast(f32), ALU.subtract).then_inc(S["ea_lo"], 1)

            def add_gathered(v):
                for j in range(U):
                    if j == U - 1:
                        dve.wait_ge(S["msg_made"], v * U + 1)
                        dve.scalar_tensor_tensor(msg_lo[:, :], msg[0][:, :], 0.0, msg_hi[:, :].bitcast(f32),
                                                 ALU.max, ALU.subtract).then_inc(S["msg_lo"], 1)
                    dve.wait_ge(S["q_done"], v * U + (j + 1))
                    dve.wait_ge(S["summed"], v * U + (j + 1))
                    dve.wait_ge(p_gathered[j], v * 16 + 16)
                    if j == 0:
                        dve.wait_ge(S["msg_lo"], v)
                    dve.tensor_tensor(msg[j][:, :], bank[j], gathered[j][:, :], ALU.add).then_inc(S["q_used"], 1)

            dve.wait_ge(S["gate_bias"], 64)
            dve.tensor_tensor(br_b[:, :], br_b[:, :], za[0][:, :], ALU.add)
            link(dve.tensor_tensor(bz_b[:, :], bz_b[:, :], za[1][:, :], ALU.add))
            lo_of_edges(1)
            lo_of_edges(2)
            add_gathered(1)
            for c in range(NT):
                base, v0, v1 = visits.of(c)
                with dve.Fori(v0, v1) as v:
                    t = first_tile(dve, v, base)
                    dve.wait_ge(S["summed"], v * U + U)
                    for j in range(U):
                        last = dve.tensor_scalar(hot[j][:, :], iota[:, c * P:(c + 1) * P],
                                                 dstF[:, bass.ds(t + j, 1)], None, ALU.is_equal)
                    last.then_inc(S["hot_made"], 1)
                    lo_of_edges(v + 2)
                    add_gathered(v + 1)
                if c:
                    lo_part("R", c - 1)
            lo_part("R", NT - 1)
            for c in range(NT):
                if c >= 2:
                    dve.wait_ge(S["cntb_done"], c - 1)
                dve.tensor_scalar(hot[1 + c % 2][:, :], ident[:, :], cnt[:, c:c + 1], None, ALU.mult)\
                   .then_inc(S["diag_made"], 1)
                if c == 0:
                    dve.memset(Rtmp[0][:, 0:P], 1.0).then_inc(S["diag_made"], 1)
            for q in range(3):
                w = min(D, NP - q * D)
                dve.wait_ge(S["cntb_done"], min(NT, KC * (q + 1)))
                last = dve.tensor_copy(cntb[:, q * D:q * D + w], bank[q][:, 0:w])
            last.then_inc(S["cntb_out"], 1)
            dve.wait_ge(S["cntb_out"], 1)
            for k in range(KC):
                lo_part("hh_r", k)

            def agg_lo(i):
                nb, oc = i // KC, i % KC
                w = min(D, NP - nb * D)
                dve.wait_ge(S["agg_hi"], i + 1)
                dve.tensor_tensor(RT_lo[:, oc, nb * D:nb * D + w], ta[i % 2][:, 0:w],
                                  RT_hi[:, oc, nb * D:nb * D + w].bitcast(f32), ALU.subtract)\
                   .then_inc(S["agg_lo"], 1)

            for i in range(3 * KC):
                nb, oc = i // KC, i % KC
                w = min(D, NP - nb * D)
                dve.wait_ge(S["agg_done"], i + 1)
                if i >= 2:
                    dve.wait_ge(S["agg_lo"], i - 1)
                dve.scalar_tensor_tensor(ta[i % 2][:, 0:w], cntb[:, nb * D:nb * D + w], b2col[:, oc:oc + 1],
                                         bank[i % 6][:, 0:w], ALU.mult, ALU.add).then_inc(S["agg_f"], 1)
                if i:
                    agg_lo(i - 1)
            agg_lo(3 * KC - 1)

            for n in range(NT):
                dve.wait_ge(S["r_done"], n + 1)
                if n >= 2:
                    dve.wait_ge(S["r_made"], n - 1)
                dve.tensor_tensor(tb[n % 2][:, :], bank[n % 2], br_b[:, :], ALU.add).then_inc(S["r_sum"], 1)
                if n < KC:
                    lo_part("ih_n", n)
            for k in range(KC):
                lo_part("hh_n", k)

            dve.wait_ge(S["n_bias_loaded"], 32)
            def n_sum(n):
                dve.wait_ge(S["n_bias"], n + 1)
                if n >= 2:
                    dve.wait_ge(S["n_made"], n - 1)
                dve.tensor_tensor(te[n % 2][:, :], bank[2 + n % 2], ta[n % 2][:, :], ALU.add).then_inc(S["n_sum"], 1)

            for n in range(NT):
                dve.wait_ge(S["n_done"], n + 1)
                if n >= 2:
                    dve.wait_ge(S["n_sum"], n - 1)
                dve.tensor_tensor(ta[n % 2][:, :], bank[4 + n % 2], bhn_b[:, :], ALU.add).then_inc(S["n_hn"], 1)
                if n:
                    n_sum(n - 1)
                if 1 <= n <= KC:
                    lo_part("ih_z", n - 1)
            n_sum(NT - 1)
            for k in range(KC):
                lo_part("hh_z", k)

            def z_finish(n):
                dve.wait_ge(S["z_gate"], n + 1)
                dve.wait_ge(S["z_diff"], n + 1)
                dve.tensor_tensor(tb[n % 2][:, :], tb[n % 2][:, :], td[n % 2][:, :], ALU.mult)\
                   .then_inc(S["z_mul"], 1)
                dve.wait_ge(S["z_mul"], n + 1)
                link(dve.tensor_tensor(tb[n % 2][:, :], tb[n % 2][:, :], rn[:, n, :], ALU.add))
                link(dve.tensor_tensor(tb[n % 2][:, :], tb[n % 2][:, :], G_b[:, :], ALU.mult))
                dve.wait_ge(S["z_base"], n + 1)
                if n >= 2:
                    dve.wait_ge(out_stored[n % 2], 16 * (n // 2))
                dve.tensor_tensor(tc[n % 2][:, :], tb[n % 2][:, :], tf[n % 2][:, :], ALU.add)\
                   .then_inc(S["z_out"], 1)

            for n in range(NT):
                dve.wait_ge(S["z_done"], n + 1)
                if n >= 2:
                    dve.wait_ge(S["z_out"], n - 1)
                dve.tensor_tensor(tb[n % 2][:, :], bank[n % 2], bz_b[:, :], ALU.add).then_inc(S["z_sum"], 1)
                if n:
                    z_finish(n - 1)
            z_finish(NT - 1)

        @block.tensor
        def _(pe):
            pe.wait_ge(S["pool_chain"], 2)
            pe.wait_ge(S["ends_made"], 1)
            two = TC - P
            for q, (lo, hi) in enumerate(((0, 2), (1, 3))):
                pe.matmul(psT[1][0:16, q * 256:q * 256 + P], ends16[:, lo, :], ident[:, :], start=True, stop=True)
                last = pe.matmul(psT[1][0:16, q * 256 + P:q * 256 + ET], ends16[0:ROWS2, hi, :],
                                 ident[0:ROWS2, 0:ROWS2], start=True, stop=True)
            last.then_inc(S["ends_bcast"], 1)
            for q, rows_f in enumerate((dst_f, src_f)):
                pe.transpose(psT[0][:, q * 256:q * 256 + P], rows_f[:, 0, :], ident[:, :])
                last = pe.transpose(psT[0][:, q * 256 + P:q * 256 + TC], rows_f[0:two, 1, :], ident[0:two, 0:two])
            last.then_inc(S["tables"], 1)
            pe.wait_ge(S["reach_made"], 1)
            pe.transpose(psT[1][0:1, 0:16], reach[:, 0:1], ident[0:16, 0:16])
            pe.transpose(psT[1][0:1, 16:32], reach[:, 3:4], ident[0:16, 0:16]).then_inc(S["reach_T"], 1)

            def job(name, k):
                j = JOB[(name, k)]
                if j >= 2:
                    pe.wait_ge(S["tr_lo"], j - 1)
                if name in STAGED and k == 0:
                    pe.wait_ge(S["staged"], 16 * (STAGED.index(name) + 1))
                for b in range(KC):
                    if name == "h" or name == "g":
                        i = ht[k % 2][:, b * P:(b + 1) * P]
                    elif name == "h2":
                        i = h2[:, k, b * P:(b + 1) * P]
                    elif name == "R":
                        i = Rtmp[k % 2][:, b * P:(b + 1) * P]
                    elif name == "W1b":
                        i = stage[:, b, D:D + ED]
                    else:
                        i = stage[:, b, k * P:(k + 1) * P]
                    last = pe.transpose(psT[j % 2][:, b * P:(b + 1) * P], i, ident[:, :])
                last.then_inc(S["tr_pe"], 1)

            def product(o, lhs, rhs, start=True, stop=True):
                for kc in range(KC):
                    for p, (a, b) in enumerate(((0, 0), (0, 1), (1, 0))):
                        last = pe.matmul(o, lhs[a](kc), rhs[b](kc), start=start and kc == 0 and p == 0,
                                         stop=stop and kc == KC - 1 and p == 2)
                return last

            def nodes(t, n):
                if t is RT:
                    return tuple((lambda kc, y=y: y[:, kc, n * P:(n + 1) * P]) for y in t)
                return tuple((lambda kc, y=y: y[:, n, kc * P:(kc + 1) * P]) for y in t)

            def weights(name):
                return tuple((lambda kc, y=y: y[:, kc, :]) for y in slot[SLOT[name]])

            hT, RT = (hT_hi, hT_lo), (RT_hi, RT_lo)

            pe.wait_ge(S["tab_ready"], 1)
            visits = Visits(pe)
            pe.wait_ge(S["const"], 2)
            pe.wait_ge(S["tile_tables"], 1)
            pe.sem_inc(S["hot_used"], 2 * U)
            pe.sem_inc(S["hot_ready"], U)
            pe.sem_inc(S["dst_made"], U)
            for c in range(NT):
                if c >= 2:
                    pe.wait_ge(S["counts_out"], c - 1)
                A = psA[c % 2]
                for q in range(3):
                    pe.matmul(A[:, q * D:(q + 1) * D], zeros16[:, 0:P], zeros16[:, :], start=True, stop=False)
                base, v0, v1 = visits.of(c)
                with pe.Fori(v0, v1) as v:
                    for j in range(U):
                        pe.wait_ge(S["hot_ready"], v * U + (j + 1))
                        pe.wait_ge(S["dst_made"], v * U + (j + 1))
                        for s in range(NT):
                            pe.matmul(A[:, s * P:(s + 1) * P], hot_src[j][:, s * P:(s + 1) * P], hot_dst[j][:, :],
                                      start=False, stop=False)
                        pe.matmul(A[:, NP:NP + 1], hot_dst[j][:, :], ones16[:, :], start=False, stop=False)\
                          .then_inc(S["hot_used"], 1)
                for q in range(3):
                    last = pe.matmul(A[:, q * D:(q + 1) * D], zeros16[:, 0:P], zeros16[:, :], start=False, stop=True)
                last.then_inc(S["counts_done"], 1)
                if c < 2 * KC:
                    job(("Wl0", "Wr0")[c // KC], c % KC)
                if c:
                    pe.wait_ge(S["h_made"], c)
                    job("h", c - 1)
            pe.wait_ge(S["h_made"], NT)
            job("h", NT - 1)

            def product_u(layer, n):
                i = layer * NT + n
                if i >= 2:
                    pe.wait_ge(S["u_lo"], i - 1)
                if n < 1 or layer == 0:
                    pe.wait_ge(S["tr_lo"], JOB[(("h", "g")[layer], NT - 1)] + 1)
                product(bank[n % 2], nodes(hT, n), weights(f"Wl{layer}")).then_inc(S["u_done"], 1)

            def product_sv(layer, n):
                i = layer * NT + n
                if n == 0:
                    pe.wait_ge(S["u_whole"], layer + 1)
                    pe.wait_ge(S["tr_lo"], LAST_JOB[f"Wr{layer}"] + 1)
                if i >= 2:
                    pe.wait_ge(S["z_made"], i - 1)
                o = bank[2 + n % 2]
                with pe.If(exact > 0):
                    for s in range(NT):
                        pe.matmul(o, AT[:, s, n * P:(n + 1) * P], u_all[:, s, :], start=s == 0, stop=s == NT - 1)
                with pe.Else():
                    for s in range(NT):
                        pe.matmul(o, AT_r[:, s, n * P:(n + 1) * P], u_hi[:, s, :], start=s == 0, stop=False)
                        pe.matmul(o, AT_r[:, s, n * P:(n + 1) * P], u_lo[:, s, :], start=False, stop=s == NT - 1)
                product(bank[4 + n % 2], nodes(hT, n), weights(f"Wr{layer}")).then_inc(S["sv_done"], 1)

            pe.wait_ge(S["counts_out"], NT)
            for n in range(NT):
                product_u(0, n)
            exact = pe.value_load(tab[0:1, 27:28], min_val=0, max_val=1)
            for n in range(NT):
                if n < KC:
                    job("Wl1", n)
                product_sv(0, n)
                if n:
                    pe.wait_ge(S["g_made"], n)
                    job("g", n - 1)
            pe.wait_ge(S["g_made"], NT)
            job("g", NT - 1)
            for n in range(NT):
                if n < KC:
                    job("Wr1", n)
                product_u(1, n)
            for n in range(NT):
                if n < KC:
                    job("W1a", n)
                if n == KC:
                    job("W1b", 0)
                product_sv(1, n)
            pe.sem_inc(S["ea_T"], 1)
            for k in range(KC):
                job("W2", k)
            def job_h2(n):
                pe.wait_ge(S["h2_made"], n + 1)
                job("h2", n)
            job_h2(0)
            for n in range(NT):
                if n + 1 < NT:
                    job_h2(n + 1)
                pe.wait_ge(S["tr_lo"], JOB[("h2", n)] + 1)
                if n >= 2:
                    pe.wait_ge(S["p_made"], n - 1)
                product(bank[n % 2], nodes(hT, n), weights("W1a")).then_inc(S["p_done"], 1)
            for k in range(KC):
                job("ih_r", k)

            def transpose_edges(v):
                for j in range(U):
                    pe.wait_ge(ea_loaded[j], v * 16)
                    if j == 0:
                        pe.wait_ge(S["ea_lo"], v)
                    last = pe.transpose(bank[5][:, j * P:(j + 1) * P], ea[j][:, :], ident[:, :])
                last.then_inc(S["ea_T"], 1)

            def multiply_edges(v, tiles=range(U)):
                if 0 in tiles:
                    pe.wait_ge(S["ea_lo"], v + 1)
                for j in tiles:
                    pe.wait_ge(S["q_used"], v * U + (j + 1))
                    pe.matmul(bank[j], eaT_hi[:, j, :], W1b_hi[:, :], start=True, stop=False)
                    pe.matmul(bank[j], eaT_hi[:, j, :], W1b_lo[:, :], start=False, stop=False)
                    pe.matmul(bank[j], eaT_lo[:, j, :], W1b_hi[:, :], start=False, stop=True)\
                      .then_inc(S["q_done"], 1)

            pe.wait_ge(S["p_made"], NT)
            pe.wait_ge(S["const"], 3)
            pe.sem_inc(S["ea_lo"], 1)
            pe.sem_inc(S["q_done"], U)
            pe.sem_inc(S["q_used"], 2 * U)
            pe.sem_inc(S["summed"], 2 * U)
            pe.sem_inc(S["msg_made"], U)
            pe.sem_inc(S["idx_made"], U)
            pe.sem_inc(S["msg_lo"], 1)
            transpose_edges(1)
            multiply_edges(1)
            transpose_edges(2)
            for c in range(NT):
                if c >= 2:
                    pe.wait_ge(S["R_out"], c - 1)
                R = bank[3 + c % 2]
                pe.matmul(R, zeros[:, 0:P], zeros[:, :], start=True, stop=False)
                base, v0, v1 = visits.of(c)
                with pe.Fori(v0, v1) as v:
                    multiply_edges(v + 1, range(U - 1))
                    transpose_edges(v + 2)
                    multiply_edges(v + 1, range(U - 1, U))
                    pe.wait_ge(S["hot_made"], v)
                    for j in range(U):
                        pe.wait_ge(S["msg_made"], v * U + (j + 1))
                        if j == 0:
                            pe.wait_ge(S["msg_lo"], v + 1)
                            pe.matmul(R, hot[0][:, :], msg_hi[:, :], start=False, stop=False)
                            last = pe.matmul(R, hot[0][:, :], msg_lo[:, :], start=False, stop=False)
                        else:
                            last = pe.matmul(R, hot[j][:, :], msg[j][:, :], start=False, stop=False)
                        last.then_inc(S["summed"], 1)
                pe.matmul(R, zeros[:, 0:P], zeros[:, :], start=False, stop=True).then_inc(S["R_done"], 1)
                if c:
                    pe.wait_ge(S["R_out"], c)
                    job("R", c - 1)
            pe.wait_ge(S["R_out"], NT)
            job("R", NT - 1)
            for c in range(NT):
                pe.wait_ge(S["diag_made"], c + 2)
                pe.matmul(bank[c // KC][:, (c % KC) * P:(c % KC + 1) * P], Rtmp[0][:, 0:P], hot[1 + c % 2][:, :],
                          start=True, stop=True).then_inc(S["cntb_done"], 1)
            for k in range(KC):
                job("hh_r", k)
            w2 = slot[SLOT["W2"]]
            pe.wait_ge(S["cntb_out"], 1)
            for i in range(3 * KC):
                nb, oc = i // KC, i % KC
                w = min(D, NP - nb * D)
                if i == 0:
                    pe.wait_ge(S["tr_lo"], JOB[("R", NT - 1)] + 1)
                if i >= 6:
                    pe.wait_ge(S["agg_f"], i - 5)
                product(bank[i % 6][:, 0:w], tuple((lambda kc, y=y: y[:, kc, oc * P:(oc + 1) * P]) for y in w2),
                        tuple((lambda kc, y=y: y[:, kc, nb * D:nb * D + w]) for y in RT)).then_inc(S["agg_done"], 1)
            for n in range(NT):
                if n == 0:
                    pe.wait_ge(S["tr_lo"], LAST_JOB["hh_r"] + 1)
                    pe.wait_ge(S["agg_f"], 3 * KC)
                    pe.wait_ge(S["agg_lo"], 3 * KC)
                if n >= 2:
                    pe.wait_ge(S["r_sum"], n - 1)
                product(bank[n % 2], nodes(RT, n), weights("ih_r"), stop=False)
                product(bank[n % 2], nodes(hT, n), weights("hh_r"), start=False).then_inc(S["r_done"], 1)
                if n < KC:
                    job("ih_n", n)
            for k in range(KC):
                job("hh_n", k)
            for n in range(NT):
                if n >= 2:
                    pe.wait_ge(S["n_sum"], n - 1)
                product(bank[2 + n % 2], nodes(RT, n), weights("ih_n"))
                if n == 0:
                    pe.wait_ge(S["tr_lo"], LAST_JOB["hh_n"] + 1)
                product(bank[4 + n % 2], nodes(hT, n), weights("hh_n")).then_inc(S["n_done"], 1)
                if n < KC:
                    job("ih_z", n)
            for k in range(KC):
                job("hh_z", k)
            for n in range(NT):
                if n < 2:
                    pe.wait_ge(S["r_sum"], NT)
                else:
                    pe.wait_ge(S["z_sum"], n - 1)
                product(bank[n % 2], nodes(RT, n), weights("ih_z"), stop=False)
                if n == 0:
                    pe.wait_ge(S["tr_lo"], LAST_JOB["hh_z"] + 1)
                product(bank[n % 2], nodes(hT, n), weights("hh_z"), start=False).then_inc(S["z_done"], 1)


_INS = ['x', 'src', 'dst', 'edge_attr_128', 'L0_gnn_Wl0', 'L0_gnn_bl0', 'L0_gnn_Wr0', 'L0_gnn_Wl1', 'L0_gnn_bl1',
        'L0_gnn_Wr1', 'L1_gnn_W1', 'L1_gnn_b1', 'L1_gnn_W2', 'L1_gnn_b2', 'L1_gnn_W_ih', 'L1_gnn_W_hh',
        'L1_gnn_b_ih', 'L1_gnn_b_hh', 'L1_gnn_gamma', 'L1_gnn_beta', 'L1_gnn_run_mean', 'L1_gnn_run_var']


def kernel(**inputs):
    import numpy as _np
    import concourse.bacc as _bacc
    from concourse import mybir as _mybir
    from concourse.bass_utils import run_bass_kernel_spmd as _run

    nc = _bacc.Bacc("TRN2", target_bir_lowering=False, num_devices=1)
    arrays, args = {}, []
    for name in _INS:
        a = _np.ascontiguousarray(inputs[name])
        arrays[f"in_{name}"] = a
        args.append(nc.dram_tensor(f"in_{name}", a.shape, _mybir.dt.from_np(a.dtype), kind="ExternalInput").ap())
    f32 = _mybir.dt.float32
    args.append(nc.dram_tensor("out_0", (N, D), f32, kind="ExternalOutput").ap())
    args.append(nc.dram_tensor("p_table", (NP, D), f32, kind="Internal").ap())
    args.append(nc.dram_tensor("h_stash", (P, NT, D), f32, kind="Internal").ap())
    args.append(nc.dram_tensor("xh_stash", (P, NT, D), f32, kind="Internal").ap())
    build_gnn(nc, *args)
    r = _run(nc, [arrays], core_ids=[0])
    return r.results[0]["out_0"]
```

```python
import concourse.bass as bass
from concourse import mybir
from contextlib import ExitStack

P = 128
N = 1250
D = 512
ED = 128
E = 21250
NT = -(-N // P)
NP = NT * P
LAST = N - (NT - 1) * P
KC = D // P
ET = -(-E // P)
FULL = E // P
TAIL = E - FULL * P
U = 3
TC = 172
ROWS2 = ET - P
EPS = 1e-5

JOBS = []
for _c in range(NT):
    if _c < 2 * KC:
        JOBS.append((("Wl0", "Wr0")[_c // KC], _c % KC))
    if _c >= 2:
        JOBS.append(("h", _c - 2))
JOBS += [("h", NT - 2), ("h", NT - 1)]
for _n in range(NT):
    if _n < KC:
        JOBS.append(("Wl1", _n))
    if _n:
        JOBS.append(("g", _n - 1))
JOBS.append(("g", NT - 1))
JOBS += [("Wr1", k) for k in range(KC)]
JOBS += [("W1a", k) for k in range(KC)] + [("W1b", 0)]
JOBS += [("h2", 0)]
for _n in range(NT):
    if _n + 1 < NT:
        JOBS.append(("h2", _n + 1))
    if _n < KC:
        JOBS.append(("W2", _n))
JOBS += [("ih_r", k) for k in range(KC)]
JOBS += [("R", c) for c in range(NT)]
JOBS += [("hh_r", k) for k in range(KC)]
JOBS += [("ih_n", k) for k in range(KC)]
JOBS += [("hh_n", k) for k in range(KC)]
JOBS += [("ih_z", k) for k in range(KC)]
JOBS += [("hh_z", k) for k in range(KC)]
JOB = {name: i for i, name in enumerate(JOBS)}

LN_CHUNKS = [(0, NT), (0, NT - 2), (NT - 2, NT)]

STAGED = ["Wl0", "Wr0", "Wl1", "Wr1", "W1a", "W2", "ih_r", "hh_r", "ih_n", "hh_n", "ih_z", "hh_z"]
LAST_JOB = {w: JOB[(w, KC - 1)] for w in STAGED}
LAST_JOB["W1a"] = JOB[("W1b", 0)]
SLOT = {"Wl0": "A", "Wr0": "B", "Wl1": "A", "Wr1": "B", "W1a": "A", "W1b": "E", "W2": "B", "ih_r": "A",
        "hh_r": "C", "ih_n": "B", "hh_n": "A", "ih_z": "C", "hh_z": "B"}


def build_gnn(nc, x, src, dst, edge_attr, Wl0, bl0, Wr0, Wl1, bl1, Wr1, W1, b1, W2, b2, W_ih, W_hh,
              b_ih, b_hh, gamma, beta, run_mean, run_var, out, p_table, h_stash, xh_stash):
    f32, f32r, f16, i32 = mybir.dt.float32, mybir.dt.float32r, mybir.dt.float16, mybir.dt.int32
    ALU, ACT, AX = mybir.AluOpType, mybir.ActivationFunctionType, mybir.AxisListType

    weight_rows = {"Wl0": Wl0, "Wr0": Wr0, "Wl1": Wl1, "Wr1": Wr1, "W1a": W1, "W2": W2}
    for g, gate in enumerate("rzn"):
        weight_rows["ih_" + gate] = W_ih[g * D:(g + 1) * D, :]
        weight_rows["hh_" + gate] = W_hh[g * D:(g + 1) * D, :]

    with ExitStack() as ctx:
        KB = 1024
        top = [nc.sbuf_base + (-nc.sbuf_base) % 32]

        def region(nbytes):
            at = top[0]
            top[0] += nbytes
            assert top[0] <= nc.sbuf_usable_end, (top[0], nc.sbuf_usable_end)
            return at

        class Part:
            def __init__(self, start, nbytes):
                self.at, self.end = start, start + nbytes

            def __call__(self, name, shape, dt):
                size = mybir.dt.size(dt)
                for s in shape[1:]:
                    size *= s
                size += (-size) % 32
                t = nc.alloc_sbuf_tensor_at(name, shape, dt, offset=self.at)
                self.at += size
                assert self.at <= self.end, (name, self.at - self.end)
                return t

        def part(nbytes):
            return Part(region(nbytes), nbytes)

        misc = part(13 * KB + KB // 4)
        ident = misc("ident", [P, P], f32)
        iota = misc("iota", [P, NP], f32)
        srcI = misc("srcI", [P, TC], i32)
        dstF = misc("dstF", [P, TC], f32)
        tab = misc("tab", [1, 32], i32)
        ea_row = misc("ea_row", [1, TC], i32)
        cnt = misc("cnt", [P, NT], f32)
        rcnt = misc("rcnt", [P, NT], f32)
        bn6 = misc("bn6", [P, NT, 6], f32)
        mv = misc("mv", [P, NT, 2], f32)
        ln = misc("ln", [P, 6, NT], f32)
        rstd = misc("rstd", [P, NT], f32)
        shift = misc("shift", [P, NT], f32)
        w1b_at = misc.at
        W1b_hi = misc("W1b_hi", [P, D], f32r)
        W1b_lo = misc("W1b_lo", [P, D], f32r)
        W1b_done = Part(w1b_at, 4 * KB)
        bin_b = W1b_done("bin_b", [P, D], f32)
        bhn_b = W1b_done("bhn_b", [P, D], f32)
        b2col = misc("b2col", [P, KC], f32)
        idx = misc("idx", [P, U], i32)
        sums = misc("sums", [P, 3, NT], f32)

        feat = part(40 * KB)
        feat_at = feat.at
        hT_hi = feat("hT_hi", [P, NT, D], f32r)
        hT_lo = feat("hT_lo", [P, NT, D], f32r)
        x1 = Part(feat_at, 20 * KB)("x1", [P, NT, D], f32)

        slots = part(32 * KB)
        slot = {s: (slots(f"slot{s}_hi", [P, KC, D], f32r), slots(f"slot{s}_lo", [P, KC, D], f32r))
                for s in "AB"}
        slot["E"] = (W1b_hi, W1b_lo)
        stage = part(10 * KB)("stage", [P, KC, D + ED], f32)

        big = region(70 * KB)
        sage = Part(big, 70 * KB)
        at_at = sage.at
        AT = sage("AT", [P, NT, NP], f32)
        AT_r = Part(at_at, 50 * KB)("AT_r", [P, NT, NP], f32r)
        u_at = sage.at
        u_hi = sage("u_hi", [P, NT, D], f32r)
        u_all = Part(u_at, 20 * KB)("u_all", [P, NT, D], f32)
        hots = Part(u_at, 20 * KB)
        hot_src = [hots(f"hot_src{j}", [P, NP], f16) for j in range(U)]
        hot_dst = [hots(f"hot_dst{j}", [P, P], f16) for j in range(U)]
        iota16 = hots("iota16", [P, NP], f16)
        srcF = hots("srcF", [P, TC], f32)
        ones16 = hots("ones16", [P, 1], f16)
        zeros16 = hots("zeros16", [P, D], f16)
        rows = Part(big, 50 * KB)
        dst_i = rows("dst_i", [P, 2, P], i32)
        src_i = rows("src_i", [P, 2, P], i32)
        real_i = rows("real_i", [P, P], i32)
        dst_f = rows("dst_f", [P, 2, P], f32)
        src_f = rows("src_f", [P, 2, P], f32)
        real_f = rows("real_f", [P, P], f32)
        ends = rows("ends", [P, 4], f32)
        ends16 = rows("ends16", [P, 4, 16], f32)
        span = rows("span", [16, 8, ET], f32)
        tile_no = rows("tile_no", [16, ET], f32)
        tile_up = rows("tile_up", [16, ET], f32)
        chunk_lo = rows("chunk_lo", [16, 1], f32)
        chunk_hi = rows("chunk_hi", [16, 1], f32)
        reach = rows("reach", [16, 4], f32)
        line = rows("line", [1, 8, 32], f32)
        line_i = rows("line_i", [1, 2, 32], i32)

        late = Part(big, 70 * KB)
        RT_hi = late("RT_hi", [P, KC, NP], f32r)
        RT_lo = late("RT_lo", [P, KC, NP], f32r)
        late_at = late.at
        edge = Part(late_at, 30 * KB)
        gathered = [edge(f"gathered{j}", [P, D], f32) for j in range(U)]
        msg = [edge(f"msg{j}", [P, D], f32) for j in range(U)]
        msg_hi = edge("msg_hi", [P, D], f32r)
        msg_lo = edge("msg_lo", [P, D], f32r)
        ea = [edge(f"ea{j}", [P, ED], f32) for j in range(U)]
        eaT_hi = edge("eaT_hi", [P, U, P], f32r)
        eaT_lo = edge("eaT_lo", [P, U, P], f32r)
        hot = [edge(f"hot{j}", [P, P], f32r if j == 0 else f32) for j in range(U)]
        Rtmp = [edge(f"Rtmp{j}", [P, D], f32) for j in range(2)]
        zeros = edge("zeros", [P, D], f16)
        before = Part(big, 20 * KB)
        h2 = before("h2", [P, NT, D], f32)
        gru = Part(late_at, 30 * KB)
        slot["C"] = (gru("slotC_hi", [P, KC, D], f32r), gru("slotC_lo", [P, KC, D], f32r))
        ta = [gru(f"ta{j}", [P, D], f32) for j in range(2)]
        tb = [gru(f"tb{j}", [P, D], f32) for j in range(2)]
        tc = [gru(f"tc{j}", [P, D], f32) for j in range(2)]

        xs = part(20 * KB)
        x_at = xs.at
        xt = xs("xt", [P, NT, D], f32)
        u_lo = Part(x_at, 20 * KB)("u_lo", [P, NT, D], f32r)
        rn = Part(x_at, 20 * KB)("rn", [P, NT, D], f32)

        tmps = part(12 * KB)
        tmp_at = tmps.at
        va = [tmps(f"va{j}", [P, D], f32) for j in range(2)]
        ht_at = tmps.at
        ht = [tmps(f"ht{j}", [P, D], f32) for j in range(2)]
        za = [tmps(f"za{j}", [P, D], f32) for j in range(2)]
        cntb = Part(ht_at, 5 * KB)("cntb", [P, NP], f32)
        gates = Part(tmp_at, 12 * KB)
        td = [gates(f"td{j}", [P, D], f32) for j in range(2)]
        te = [gates(f"te{j}", [P, D], f32) for j in range(2)]
        tf = [gates(f"tf{j}", [P, D], f32) for j in range(2)]

        bias = part(10 * KB)
        bias_at = bias.at
        bl0_b = bias("bl0_b", [P, D], f32)
        bl1_b = bias("bl1_b", [P, D], f32)
        b1_b = bias("b1_b", [P, D], f32)
        G_b = bias("G_b", [P, D], f32)
        B_b = bias("B_b", [P, D], f32)
        sage_done = Part(bias_at, 4 * KB)
        br_b = sage_done("br_b", [P, D], f32)
        bz_b = sage_done("bz_b", [P, D], f32)

        psA = [ctx.enter_context(nc.psum_tensor(f"psA{q}", [P, 3 * D], f32)) for q in range(2)]
        psT = [ctx.enter_context(nc.psum_tensor(f"psT{q}", [P, D], f32)) for q in range(2)]
        bank = [psA[b // 3][:, (b % 3) * D:(b % 3 + 1) * D] for b in range(6)]

        names = """idx_zero idx_loaded x_loaded const ends_made tables ends_bcast tile_tables
            reach_made reach_T tab_ready hot_ready hot_used counts_done counts_out counts_in ln_stats ln_sqrt ln_ready
            h_made staged tr_pe tr_hi tr_lo u_done u_out sv_done z_made g_made x1_made
            h2_made p_done p_made xh_made h_stored xh_stored bias_loaded bias_sqrt
            msg_lo u_lo u_whole sums_made
            ea_T ea_hi ea_lo q_done q_used msg_made hot_made summed gate idx_made
            R_done R_out diag_made cntb_done cntb_out agg_done agg_f agg_hi agg_lo
            r_done r_sum r_made n_done n_hn n_mul n_bias n_sum n_made z_done z_sum z_gate z_diff z_mul
            z_base z_out dve_chain pool_chain sp_gate gate_bias n_bias_loaded""".split()
        S = {n: ctx.enter_context(nc.semaphore("s_" + n)) for n in names}
        x_again = [ctx.enter_context(nc.semaphore(f"s_x_again{j}")) for j in range(2)]
        p_stored = [ctx.enter_context(nc.semaphore(f"s_p_stored{j}")) for j in range(2)]
        ea_loaded = [ctx.enter_context(nc.semaphore(f"s_ea_loaded{j}")) for j in range(U)]
        p_gathered = [ctx.enter_context(nc.semaphore(f"s_p_gathered{j}")) for j in range(U)]
        h_loaded = [ctx.enter_context(nc.semaphore(f"s_h_loaded{j}")) for j in range(2)]
        xh_loaded = [ctx.enter_context(nc.semaphore(f"s_xh_loaded{j}")) for j in range(2)]
        out_stored = [ctx.enter_context(nc.semaphore(f"s_out_stored{j}")) for j in range(2)]

        block = ctx.enter_context(nc.Block())

        class Visits:
            def __init__(self, eng):
                self.eng, self.base, self.at = eng, [], []

            def load(self, c):
                if not self.at:
                    self.at.append(self.eng.value_load(tab[0:1, 16:17], min_val=1, max_val=700))
                while len(self.base) <= c:
                    k = len(self.base)
                    self.base.append(self.eng.value_load(tab[0:1, k:k + 1], min_val=-U * 700, max_val=ET))
                    self.at.append(self.eng.value_load(tab[0:1, 17 + k:18 + k], min_val=2, max_val=700))

            def of(self, c):
                self.load(c)
                return self.base[c], self.at[c], self.at[c + 1]

        def first_tile(eng, v, base):
            return nc.s_assert_within(eng.snap(v * U + base), 0, TC - U,
                                      skip_runtime_bounds_check_because="the tile tables bound the visits")

        @block.sync
        def _(sp):
            sp.wait_ge(S["idx_zero"], 2)
            for t, a in ((dst_i, dst), (src_i, src)):
                sp.dma_start(t[:, 0, :], a[0:P * P].rearrange("(t p) -> t p", p=P)).then_inc(S["idx_loaded"], 16)
                sp.dma_start(t[0:FULL - P, 1, :], a[P * P:FULL * P].rearrange("(t p) -> t p", p=P))\
                  .then_inc(S["idx_loaded"], 16)
            sp.dma_start(dst_i[FULL - P:FULL - P + 1, 1, P - TAIL:P], dst[FULL * P:E].unsqueeze(0))\
              .then_inc(S["idx_loaded"], 16)
            sp.dma_start(src_i[FULL - P:FULL - P + 1, 1, :], src[E - P:E].unsqueeze(0)).then_inc(S["idx_loaded"], 16)
            sp.dma_start(real_i[0:FULL - P, :], dst[P * P:FULL * P].rearrange("(t p) -> t p", p=P))\
              .then_inc(S["idx_loaded"], 16)
            sp.dma_start(real_i[FULL - P:FULL - P + 1, :], dst[E - P:E].unsqueeze(0)).then_inc(S["idx_loaded"], 16)

            def stage_weights(w):
                if STAGED.index(w):
                    sp.wait_ge(S["tr_pe"], LAST_JOB[STAGED[STAGED.index(w) - 1]] + 1)
                rows_of = weight_rows[w]
                sp.dma_start(stage[:, :, 0:rows_of.shape[1]], rows_of.rearrange("(b p) k -> p b k", p=P))\
                  .then_inc(S["staged"], 16)

            sp.wait_ge(S["idx_loaded"], 16 * 8)
            stage_weights("Wl0")
            sp.wait_ge(S["x_loaded"], 32)
            for t, a in ((bl0_b, bl0), (bl1_b, bl1), (b1_b, b1), (G_b, run_var), (B_b, beta),
                         (za[0], gamma), (za[1], run_mean)):
                sp.dma_start(t[:, :], a.partition_broadcast(P)).then_inc(S["bias_loaded"], 16)
            sp.dma_start(b2col[:, :], b2.rearrange("(k p) -> p k", p=P), allow_slow_non_contiguous=True)\
              .then_inc(S["bias_loaded"], 16)
            for w in STAGED[1:5]:
                stage_weights(w)
            stage_weights("W2")
            sp.wait_ge(S["tab_ready"], 1)
            sp.wait_ge(S["counts_in"], 1)
            visits = Visits(sp)
            visits.load(NT - 1)
            sp.wait_ge(S["x1_made"], NT)
            for t, a in ((br_b, b_ih[0:D]), (bz_b, b_ih[D:2 * D]), (za[0], b_hh[0:D]), (za[1], b_hh[D:2 * D])):
                sp.dma_start(t[:, :], a.partition_broadcast(P)).then_inc(S["gate_bias"], 16)
            stage_weights("ih_r")
            for c in range(NT):
                base, v0, v1 = visits.of(c)
                with sp.Fori(v0, v1) as v:
                    t = first_tile(sp, v, base)
                    row = [sp.value_load(ea_row[0:1, bass.ds(t + j, 1)], min_val=0, max_val=E - P) for j in range(U)]
                    sp.wait_ge(S["ea_T"], v)
                    sp.sem_inc(S["sp_gate"], 1)
                    for j in range(U):
                        sp.dma_start(ea[j][:, :], edge_attr[bass.ds(row[j], P), :]).then_inc(ea_loaded[j], 16)
                if c == 0:
                    stage_weights("hh_r")
            end = visits.at[NT]
            for k in range(2):
                sp.wait_ge(S["ea_T"], end + k)
                sp.sem_inc(S["sp_gate"], 1)
                for j in range(U):
                    sp.dma_start(ea[j][:, :], edge_attr[0:P, :]).then_inc(ea_loaded[j], 16)
            sp.wait_ge(S["R_done"], NT)
            for t, a in ((bin_b, b_ih[2 * D:3 * D]), (bhn_b, b_hh[2 * D:3 * D])):
                sp.dma_start(t[:, :], a.partition_broadcast(P)).then_inc(S["n_bias_loaded"], 16)
            for w in ("ih_n", "hh_n", "ih_z", "hh_z"):
                stage_weights(w)
            for n in range(NT):
                size = P if n < NT - 1 else LAST
                if n >= 2:
                    sp.wait_ge(S["z_diff"], n - 1)
                else:
                    sp.wait_ge(S["n_made"], NT - 1 + n)
                sp.dma_start(te[n % 2][:, :], h_stash[:, n, :]).then_inc(h_loaded[n % 2], 16)
                if n >= 2:
                    sp.wait_ge(S["z_out"], n - 1)
                sp.dma_start(tf[n % 2][:, :], xh_stash[:, n, :]).then_inc(xh_loaded[n % 2], 16)
                if n >= 1:
                    sp.wait_ge(S["z_out"], n)
                    sp.dma_start(out[(n - 1) * P:n * P, :], tc[(n - 1) % 2][:, :])\
                      .then_inc(out_stored[(n - 1) % 2], 16)
            sp.wait_ge(S["z_out"], NT)
            sp.dma_start(out[(NT - 1) * P:N, :], tc[(NT - 1) % 2][0:LAST, :]).then_inc(out_stored[(NT - 1) % 2], 16)
            for j in range(2):
                sp.wait_ge(out_stored[j], 16 * (NT // 2))

        @block.gpsimd
        def _(pool):
            chain = [0]

            def link(ins):
                chain[0] += 1
                ins.then_inc(S["pool_chain"], 1)
                pool.wait_ge(S["pool_chain"], chain[0])

            pool.memset(dst_i[:, 1, :], -1).then_inc(S["idx_zero"], 1)
            pool.memset(src_i[:, 1, :], 0).then_inc(S["idx_zero"], 1)
            link(pool.memset(ident[:, :], 0.0))
            link(pool.affine_select(out=ident[:, :], in_=ident[:, :], compare_op=ALU.not_equal, fill=1.0,
                                    base=0, pattern=[[-1, P]], channel_multiplier=1))
            pool.iota(chunk_lo[:, :], pattern=[[0, 1]], base=0, channel_multiplier=P,
                      allow_small_or_imprecise_dtypes=True)
            pool.iota(chunk_hi[:, :], pattern=[[0, 1]], base=P - 1, channel_multiplier=P,
                      allow_small_or_imprecise_dtypes=True)
            pool.iota(tile_no[:, :], pattern=[[1, ET]], base=-1000, channel_multiplier=0,
                      allow_small_or_imprecise_dtypes=True)
            pool.iota(tile_up[:, :], pattern=[[1, ET]], base=1, channel_multiplier=0,
                      allow_small_or_imprecise_dtypes=True)
            pool.memset(line[:, :, :], 0.0)
            pool.memset(xt[:, NT - 1, :], 0.0).then_inc(S["const"], 1)
            pool.iota(iota16[:, :], pattern=[[1, NP]], base=0, channel_multiplier=0,
                      allow_small_or_imprecise_dtypes=True)
            pool.iota(iota[:, :], pattern=[[1, NP]], base=0, channel_multiplier=0,
                      allow_small_or_imprecise_dtypes=True)
            pool.memset(ones16[:, :], 1.0)
            pool.memset(zeros16[:, :], 0.0).then_inc(S["const"], 1)
            link(pool.iota(ea_row[:, :], pattern=[[P, TC]], base=0, channel_multiplier=0))
            link(pool.tensor_scalar(ea_row[:, :], ea_row[:, :], E - P, None, ALU.min))
            pool.memset(tab[0:1, 28:32], 0).then_inc(S["counts_in"], 1)

            pool.wait_ge(S["tab_ready"], 1)
            visits = Visits(pool)
            visits.load(NT - 1)
            for n in range(NT):
                pool.wait_ge(S["h2_made"], n + 1)
                pool.wait_ge(S["x1_made"], n + 1)
                pool.tensor_tensor(xt[:, n, :], x1[:, n, :], h2[:, n, :], ALU.add).then_inc(S["xh_made"], 1)

            pool.memset(zeros[:, :], 0.0).then_inc(S["const"], 1)
            def gather(j, table=p_table):
                pool.indirect_dma_start(
                    out=gathered[j][:, :], out_offset=None, in_=table[:, :],
                    in_offset=bass.IndirectOffsetOnAxis(ap=idx[:, j:j + 1], axis=0)).then_inc(p_gathered[j], 16)

            link(pool.memset(idx[:, :], 0))
            for j in range(U):
                gather(j, x)
            pool.wait_ge(p_stored[0], 16 * (NT // 2))
            pool.wait_ge(p_stored[1], 16 * (NT // 2))
            for c in range(NT):
                base, v0, v1 = visits.of(c)
                with pool.Fori(v0, v1) as v:
                    t = first_tile(pool, v, base)
                    for j in range(U):
                        pool.wait_ge(p_gathered[j], v * 16)
                        pool.sem_inc(S["gate"], 1)
                        pool.tensor_copy(idx[:, j:j + 1], srcI[:, bass.ds(t + j, 1)]).then_inc(S["idx_made"], 1)
                        pool.wait_ge(S["q_used"], v * U + (j + 1))
                        pool.wait_ge(S["idx_made"], v * U + (j + 1))
                        pool.sem_inc(S["gate"], 1)
                        gather(j)
            end = visits.at[NT]
            for j in range(U):
                pool.wait_ge(S["q_used"], end * U + (j + 1))
                pool.sem_inc(S["gate"], 1)
                gather(j)

            pool.wait_ge(S["xh_stored"], 16 * NT)
            pool.wait_ge(S["n_bias_loaded"], 32)
            for n in range(NT):
                pool.wait_ge(S["n_hn"], n + 1)
                pool.tensor_tensor(ta[n % 2][:, :], ta[n % 2][:, :], rn[:, n, :], ALU.mult).then_inc(S["n_mul"], 1)
                pool.wait_ge(S["n_mul"], n + 1)
                pool.tensor_tensor(ta[n % 2][:, :], ta[n % 2][:, :], bin_b[:, :], ALU.add).then_inc(S["n_bias"], 1)
            for n in range(NT):
                pool.wait_ge(S["n_made"], n + 1)
                pool.wait_ge(h_loaded[n % 2], 16 * (n // 2 + 1))
                if n >= 2:
                    pool.wait_ge(S["z_mul"], n - 1)
                pool.tensor_tensor(td[n % 2][:, :], te[n % 2][:, :], rn[:, n, :], ALU.subtract)\
                    .then_inc(S["z_diff"], 1)
                pool.wait_ge(xh_loaded[n % 2], 16 * (n // 2 + 1))
                pool.tensor_tensor(tf[n % 2][:, :], tf[n % 2][:, :], B_b[:, :], ALU.add).then_inc(S["z_base"], 1)

        @block.scalar
        def _(act):
            act.wait_ge(S["const"], 1)
            act.wait_ge(S["idx_loaded"], 16 * 8)
            act.dma_start(xt[:, 0:NT - 1, :], x[0:(NT - 1) * P, :].rearrange("(n p) d -> p n d", p=P))\
               .then_inc(S["x_loaded"], 16)
            act.dma_start(xt[0:LAST, NT - 1, :], x[(NT - 1) * P:N, :]).then_inc(S["x_loaded"], 16)
            def ln_root(k):
                act.wait_ge(S["ln_stats"], k + 1)
                a, b = LN_CHUNKS[k]
                act.activation(ln[:, 1, a:b], ln[:, 0, a:b], ACT.Sqrt).then_inc(S["ln_sqrt"], 1)

            def hi_part(name, k):
                j = JOB[(name, k)]
                act.wait_ge(S["tr_pe"], j + 1)
                if name in ("h", "g", "h2"):
                    o = hT_hi[:, k, :]
                elif name == "R":
                    o = RT_hi[:, :, k * P:(k + 1) * P]
                elif name == "W1b":
                    o = W1b_hi[:, :]
                else:
                    o = slot[SLOT[name]][0][:, k, :]
                i = psT[j % 2][:, :]
                if name == "R":
                    i = i.rearrange("p (k n) -> p k n", k=KC)
                act.activation(o, i, ACT.Copy).then_inc(S["tr_hi"], 1)

            act.wait_ge(S["x_loaded"], 32)
            for n in range(NT):
                if n >= 2:
                    act.wait_ge(S["sums_made"], n - 1)
                act.activation(va[n % 2][:, :], xt[:, n, :], ACT.Copy, accum_out=sums[:, 0, n:n + 1])\
                   .then_inc(S["sums_made"], 1)
            act.wait_ge(S["sums_made"], NT)
            act.activation(sums[:, 1, :], sums[:, 0, :], ACT.Copy, scale=-1.0 / D).then_inc(S["sums_made"], 1)
            act.wait_ge(S["sums_made"], NT + 1)
            for n in range(NT):
                if n >= 2:
                    act.wait_ge(S["sums_made"], NT + n)
                act.activation(va[n % 2][:, :], xt[:, n, :], ACT.Square, bias=sums[:, 1, n:n + 1],
                               accum_out=sums[:, 2, n:n + 1]).then_inc(S["sums_made"], 1)

            def make_h(c):
                if c < 2:
                    act.wait_ge(S["ln_ready"], 1)
                else:
                    act.wait_ge(S["tr_pe"], JOB[("h", c - 2)] + 1)
                act.activation(ht[c % 2][:, :], xt[:, c, :], ACT.Relu, bias=shift[:, c:c + 1],
                               scale=rstd[:, c:c + 1]).then_inc(S["h_made"], 1)

            act.wait_ge(S["tab_ready"], 1)
            exact = act.value_load(tab[0:1, 27:28], min_val=0, max_val=1)
            visits = Visits(act)
            for c in range(NT):
                visits.load(c)
                act.wait_ge(S["counts_done"], c + 1)
                counts = psA[c % 2][:, 0:NP].rearrange("p (s d) -> p s d", s=NT)
                with act.If(exact > 0):
                    act.activation(AT[:, :, c * P:(c + 1) * P], counts, ACT.Copy)
                with act.Else():
                    act.activation(AT_r[:, :, c * P:(c + 1) * P], counts, ACT.Copy)
                act.activation(cnt[:, c:c + 1], psA[c % 2][:, NP:NP + 1], ACT.Copy).then_inc(S["counts_out"], 1)
                if c < 2 * KC:
                    hi_part(("Wl0", "Wr0")[c // KC], c % KC)
                if c == 0:
                    ln_root(0)
                elif c == 1:
                    make_h(0)
                    make_h(1)
                else:
                    hi_part("h", c - 2)
                    make_h(c)

            def u_out(layer, n):
                act.wait_ge(S["u_done"], layer * NT + n + 1)
                act.activation(u_hi[:, n, :], bank[n % 2], ACT.Copy).then_inc(S["u_out"], 1)

            for n in range(NT):
                u_out(0, n)
                if n < 2:
                    hi_part("h", NT - 2 + n)
            act.wait_ge(S["bias_sqrt"], 1)
            act.activation(G_b[:, :], G_b[:, :], ACT.Sqrt).then_inc(S["bias_sqrt"], 1)
            for n in range(NT):
                if n < KC:
                    hi_part("Wl1", n)
                act.wait_ge(S["z_made"], n + 1)
                if n >= 2:
                    act.wait_ge(S["tr_pe"], JOB[("g", n - 2)] + 1)
                act.activation(ht[n % 2][:, :], za[n % 2][:, :], ACT.Relu).then_inc(S["g_made"], 1)
                if n:
                    hi_part("g", n - 1)
            hi_part("g", NT - 1)
            for n in range(NT):
                u_out(1, n)
                if n < KC:
                    hi_part("Wr1", n)
            def reload_x(n):
                act.dma_start(ht[n % 2][0:P if n < NT - 1 else LAST, :], x[n * P:min((n + 1) * P, N), :])\
                   .then_inc(x_again[n % 2], 16)
            reload_x(0)
            reload_x(1)
            for n in range(NT):
                if n < KC:
                    hi_part("W1a", n)
                if n == KC:
                    hi_part("W1b", 0)
                if n + 2 < NT:
                    act.wait_ge(S["x1_made"], n + 1)
                    reload_x(n + 2)
            ln_root(1)
            act.wait_ge(S["ln_ready"], 2)
            act.wait_ge(S["sv_done"], 2 * NT)

            def make_h2(n):
                act.activation(h2[:, n, :], x1[:, n, :], ACT.Relu, bias=shift[:, n:n + 1],
                               scale=rstd[:, n:n + 1]).then_inc(S["h2_made"], 1)

            def store_p(n):
                act.wait_ge(S["p_made"], n + 1)
                act.dma_start(p_table[n * P:(n + 1) * P, :], va[n % 2][:, :]).then_inc(p_stored[n % 2], 16)

            def hi_of_edges(v):
                act.wait_ge(S["ea_T"], v + 1)
                act.wait_ge(S["q_done"], U * v)
                act.activation(eaT_hi[:, :, :], bank[5][:, 0:U * P].rearrange("p (j e) -> p j e", j=U),
                               ACT.Copy).then_inc(S["ea_hi"], 1)

            def relu_messages(v):
                for j in range(U):
                    act.wait_ge(S["q_used"], v * U + (U + j + 1))
                    act.activation(msg[j][:, :] if j else msg_hi[:, :], msg[j][:, :], ACT.Relu)\
                       .then_inc(S["msg_made"], 1)

            make_h2(0)
            make_h2(1)
            for n in range(NT):
                if n == 2:
                    ln_root(2)
                if n == NT - 4:
                    act.wait_ge(S["ln_ready"], 3)
                if 1 <= n < NT - 1:
                    make_h2(n + 1)
                act.wait_ge(S["xh_made"], n + 1)
                hi_part("h2", n)
                if 1 <= n <= KC:
                    hi_part("W2", n - 1)
                act.wait_ge(S["h2_made"], n + 1)
                act.dma_start(h_stash[:, n, :], h2[:, n, :]).then_inc(S["h_stored"], 16)
                if n >= 2:
                    store_p(n - 2)
            hi_of_edges(1)
            store_p(NT - 2)
            store_p(NT - 1)
            hi_of_edges(2)
            for n in range(KC):
                hi_part("ih_r", n)

            relu_messages(1)
            for c in range(NT):
                base, v0, v1 = visits.of(c)
                with act.Fori(v0, v1) as v:
                    hi_of_edges(v + 2)
                    relu_messages(v + 1)
                act.dma_start(xh_stash[:, c, :], xt[:, c, :]).then_inc(S["xh_stored"], 16)
                act.wait_ge(S["R_done"], c + 1)
                if c >= 2:
                    act.wait_ge(S["tr_pe"], JOB[("R", c - 2)] + 1)
                act.activation(Rtmp[c % 2][:, :], bank[3 + c % 2], ACT.Copy).then_inc(S["R_out"], 1)
                if c == 1:
                    act.wait_ge(S["h_stored"], 16 * NT)
                if c:
                    hi_part("R", c - 1)
            hi_part("R", NT - 1)
            hi_part("hh_r", 0)
            hi_part("hh_r", 1)
            for i in range(3 * KC):
                nb, oc = i // KC, i % KC
                act.wait_ge(S["agg_f"], i + 1)
                act.wait_ge(S["agg_done"], KC * (nb + 1))
                w = min(D, NP - nb * D)
                act.activation(RT_hi[:, oc, nb * D:nb * D + w], ta[i % 2][:, 0:w], ACT.Copy).then_inc(S["agg_hi"], 1)
                if i in (2, 3):
                    hi_part("hh_r", i)
            act.wait_ge(S["xh_stored"], 16 * NT)
            for n in range(NT):
                act.wait_ge(S["r_sum"], n + 1)
                act.activation(rn[:, n, :], tb[n % 2][:, :], ACT.Sigmoid).then_inc(S["r_made"], 1)
                if n < KC:
                    hi_part("ih_n", n)
            for k in range(KC):
                hi_part("hh_n", k)
            for n in range(NT):
                if n == NT - 1:
                    hi_part("hh_z", 0)
                    hi_part("hh_z", 1)
                act.wait_ge(S["n_sum"], n + 1)
                act.activation(rn[:, n, :], te[n % 2][:, :], ACT.Tanh).then_inc(S["n_made"], 1)
                if n < KC:
                    hi_part("ih_z", n)
            hi_part("hh_z", 2)
            hi_part("hh_z", 3)
            for n in range(NT):
                act.wait_ge(S["z_sum"], n + 1)
                act.activation(tb[n % 2][:, :], tb[n % 2][:, :], ACT.Sigmoid).then_inc(S["z_gate"], 1)

        @block.vector
        def _(dve):
            chain = [0]

            def link(ins):
                chain[0] += 1
                ins.then_inc(S["dve_chain"], 1)
                dve.wait_ge(S["dve_chain"], chain[0])

            dve.wait_ge(S["idx_loaded"], 16 * 8)
            dve.tensor_copy(real_f[0:ROWS2, :], real_i[0:ROWS2, :])
            dve.tensor_copy(src_f[:, :, :], src_i[:, :, :])
            link(dve.tensor_copy(dst_f[:, :, :], dst_i[:, :, :]))
            dve.tensor_reduce(ends[:, 0:1], dst_f[:, 0, :], AX.X, ALU.min)
            dve.tensor_reduce(ends[:, 1:2], dst_f[:, 0, :], AX.X, ALU.max)
            dve.tensor_reduce(ends[0:ROWS2, 2:3], real_f[0:ROWS2, :], AX.X, ALU.min)
            link(dve.tensor_reduce(ends[0:ROWS2, 3:4], real_f[0:ROWS2, :], AX.X, ALU.max))
            dve.tensor_copy(ends16[:, 0:2, :], ends[:, 0:2].unsqueeze(2).to_broadcast([P, 2, 16]))
            dve.tensor_copy(ends16[0:ROWS2, 2:4, :], ends[0:ROWS2, 2:4].unsqueeze(2).to_broadcast([ROWS2, 2, 16]))\
               .then_inc(S["ends_made"], 1)
            dve.wait_ge(S["const"], 1)
            dve.wait_ge(S["ends_bcast"], 1)
            dve.tensor_copy(span[:, 0, :], psT[1][0:16, 0:ET])
            link(dve.tensor_copy(span[:, 1, :], psT[1][0:16, 256:256 + ET]))
            link(dve.tensor_scalar(span[:, 2, :], span[:, 0, :], chunk_hi[:, 0:1], None, ALU.is_le))
            link(dve.scalar_tensor_tensor(span[:, 3, :], span[:, 1, :], chunk_lo[:, 0:1], span[:, 2, :],
                                          ALU.is_ge, ALU.mult))
            dve.tensor_tensor(span[:, 4, :], span[:, 3, :], tile_no[:, :], ALU.mult)
            link(dve.tensor_tensor(span[:, 5, :], span[:, 3, :], tile_up[:, :], ALU.mult))
            dve.tensor_reduce(reach[:, 0:1], span[:, 4, :], AX.X, ALU.min)
            link(dve.tensor_reduce(reach[:, 1:2], span[:, 5, :], AX.X, ALU.max))
            link(dve.tensor_scalar(reach[:, 2:3], reach[:, 0:1], 1000.0, float(ET - 1), ALU.add, ALU.min))
            link(dve.scalar_tensor_tensor(reach[:, 3:4], reach[:, 2:3], 1.0, reach[:, 1:2], ALU.add, ALU.max))
            dve.tensor_copy(reach[:, 0:1], reach[:, 2:3]).then_inc(S["reach_made"], 1)
            dve.wait_ge(S["tables"], 1)
            dve.tensor_copy(dstF[:, :], psT[0][:, 0:TC])
            dve.tensor_copy(srcI[:, :], psT[0][:, 256:256 + TC])
            dve.tensor_copy(srcF[:, :], psT[0][:, 256:256 + TC]).then_inc(S["tile_tables"], 1)
            dve.wait_ge(S["reach_T"], 1)
            dve.tensor_copy(line[0:1, 0, 0:NT], psT[1][0:1, 0:NT])
            link(dve.tensor_copy(line[0:1, 1, 0:NT], psT[1][0:1, 16:16 + NT]))
            link(dve.tensor_tensor(line[0:1, 2, 0:NT], line[0:1, 1, 0:NT], line[0:1, 0, 0:NT], ALU.subtract))
            link(dve.tensor_reduce(line[0:1, 5, 0:1], line[0:1, 2, 0:NT], AX.X, ALU.max))
            link(dve.tensor_scalar(line[0:1, 6, 0:1], line[0:1, 5, 0:1], float(4096 // P), None, ALU.is_gt))
            dve.tensor_copy(tab[0:1, 27:28], line[0:1, 6, 0:1])
            link(dve.tensor_scalar(line_i[0:1, 0, 0:NT], line[0:1, 2, 0:NT], float(U - 1), 43691.0, ALU.add, ALU.mult))
            link(dve.tensor_scalar(line_i[0:1, 1, 0:NT], line_i[0:1, 0, 0:NT], 17, None, ALU.logical_shift_right))
            link(dve.tensor_copy(line[0:1, 3, 16:16 + NT], line_i[0:1, 1, 0:NT]))
            for k in range(4):
                s = 1 << k
                link(dve.tensor_tensor(line[0:1, 4 + k, 16:16 + NT], line[0:1, 3 + k, 16:16 + NT],
                                       line[0:1, 3 + k, 16 - s:16 + NT - s], ALU.add))
            link(dve.tensor_scalar(line[0:1, 4, 15:16 + NT], line[0:1, 7, 15:16 + NT], 1.0, None, ALU.add))
            dve.tensor_copy(tab[0:1, 16:17 + NT], line[0:1, 4, 15:16 + NT])
            dve.scalar_tensor_tensor(tab[0:1, 0:NT], line[0:1, 4, 15:15 + NT], -float(U), line[0:1, 0, 0:NT],
                                     ALU.mult, ALU.add).then_inc(S["tab_ready"], 1)

            def ln_begin(k):
                a, b = LN_CHUNKS[k]
                dve.tensor_scalar(ln[:, 0, a:b], mv[:, a:b, 1], EPS, None, ALU.add).then_inc(S["ln_stats"], 1)

            def ln_finish(k):
                a, b = LN_CHUNKS[k]
                dve.wait_ge(S["ln_sqrt"], k + 1)
                link(dve.reciprocal(ln[:, 2, a:b], ln[:, 1, a:b]))
                link(dve.tensor_tensor(ln[:, 3, a:b], ln[:, 2, a:b], ln[:, 2, a:b], ALU.mult))
                link(dve.tensor_tensor(ln[:, 4, a:b], ln[:, 3, a:b], ln[:, 0, a:b], ALU.mult))
                link(dve.tensor_scalar(ln[:, 5, a:b], ln[:, 4, a:b], -0.5, 1.5, ALU.mult, ALU.add))
                link(dve.tensor_tensor(rstd[:, a:b], ln[:, 5, a:b], ln[:, 2, a:b], ALU.mult))
                dve.scalar_tensor_tensor(shift[:, a:b], mv[:, a:b, 0], -1.0, rstd[:, a:b], ALU.mult, ALU.mult)\
                   .then_inc(S["ln_ready"], 1)

            def lo_part(name, k):
                j = JOB[(name, k)]
                dve.wait_ge(S["tr_hi"], j + 1)
                if name in ("h", "g", "h2"):
                    hi, lo = (t[:, k, :] for t in (hT_hi, hT_lo))
                elif name == "R":
                    hi, lo = (t[:, :, k * P:(k + 1) * P] for t in (RT_hi, RT_lo))
                elif name == "W1b":
                    hi, lo = W1b_hi[:, :], W1b_lo[:, :]
                else:
                    hi, lo = (t[:, k, :] for t in slot[SLOT[name]])
                i = psT[j % 2][:, :]
                if name == "R":
                    i = i.rearrange("p (k n) -> p k n", k=KC)
                dve.tensor_tensor(lo, i, hi.bitcast(f32), ALU.subtract).then_inc(S["tr_lo"], 1)

            dve.wait_ge(S["const"], 2)
            dve.wait_ge(S["tab_ready"], 1)
            visits = Visits(dve)
            dve.wait_ge(S["tile_tables"], 1)
            for c in range(NT):
                base, v0, v1 = visits.of(c)
                with dve.Fori(v0, v1) as v:
                    t = first_tile(dve, v, base)
                    for j in range(U):
                        dve.wait_ge(S["hot_used"], v * U + (j + 1))
                        dve.tensor_scalar(hot_dst[j][:, :], iota16[:, c * P:(c + 1) * P],
                                          dstF[:, bass.ds(t + j, 1)], None, ALU.is_equal)
                        dve.tensor_scalar(hot_src[j][:, :], iota16[:, :], srcF[:, bass.ds(t + j, 1)], None,
                                          ALU.is_equal).then_inc(S["hot_ready"], 1)
                if 0 < c <= 2 * KC:
                    lo_part(("Wl0", "Wr0")[(c - 1) // KC], (c - 1) % KC)
                if c == 0:
                    dve.wait_ge(S["sums_made"], 2 * NT + 1)
                    dve.tensor_scalar(mv[:, :, 0], sums[:, 1, :], -1.0, None, ALU.mult)
                    link(dve.tensor_scalar(mv[:, :, 1], sums[:, 2, :], 1.0 / D, None, ALU.mult))
                    ln_begin(0)
                if c == 1:
                    ln_finish(0)
                if c >= 3:
                    lo_part("h", c - 3)
            lo_part("h", NT - 3)
            dve.wait_ge(S["counts_out"], NT)
            link(dve.tensor_scalar(rcnt[:, :], cnt[:, :], 1.0, None, ALU.max))
            link(dve.reciprocal(rcnt[:, :], rcnt[:, :]))

            def u_whole(layer):
                dve.wait_ge(S["u_lo"], (layer + 1) * NT)
                with dve.If(exact > 0):
                    for n in range(NT):
                        dve.tensor_tensor(u_all[:, n, :], u_hi[:, n, :].bitcast(f32), u_lo[:, n, :].bitcast(f32),
                                          ALU.add)
                dve.drain().then_inc(S["u_whole"], 1)

            def u_lo_of(layer, n):
                dve.wait_ge(S["u_out"], layer * NT + n + 1)
                dve.tensor_tensor(u_lo[:, n, :], bank[n % 2], u_hi[:, n, :].bitcast(f32), ALU.subtract)\
                   .then_inc(S["u_lo"], 1)

            exact = dve.value_load(tab[0:1, 27:28], min_val=0, max_val=1)
            for n in range(NT):
                u_lo_of(0, n)
                if n < 2:
                    lo_part("h", NT - 2 + n)
            u_whole(0)
            dve.wait_ge(S["bias_loaded"], 16 * 8)
            link(dve.tensor_scalar(G_b[:, :], G_b[:, :], EPS, None, ALU.add))
            dve.tensor_scalar(za[1][:, :], za[1][:, :], -1.0, None, ALU.mult)
            dve.tensor_copy(va[0][:, :], G_b[:, :]).then_inc(S["bias_sqrt"], 1)
            dve.wait_ge(S["bias_sqrt"], 2)
            link(dve.reciprocal(va[1][:, :], G_b[:, :]))
            link(dve.tensor_tensor(G_b[:, :], va[1][:, :], va[1][:, :], ALU.mult))
            link(dve.tensor_tensor(G_b[:, :], G_b[:, :], va[0][:, :], ALU.mult))
            link(dve.tensor_scalar(G_b[:, :], G_b[:, :], -0.5, 1.5, ALU.mult, ALU.add))
            link(dve.tensor_tensor(G_b[:, :], G_b[:, :], va[1][:, :], ALU.mult))
            link(dve.tensor_tensor(G_b[:, :], G_b[:, :], za[0][:, :], ALU.mult))
            link(dve.tensor_tensor(za[1][:, :], za[1][:, :], G_b[:, :], ALU.mult))
            link(dve.tensor_tensor(B_b[:, :], B_b[:, :], za[1][:, :], ALU.add))

            def sage_sum(layer, n):
                dve.wait_ge(S["sv_done"], layer * NT + n + 1)
                if layer == 0 and n >= 2:
                    dve.wait_ge(S["g_made"], n - 1)
                link(dve.tensor_tensor(va[n % 2][:, :], bank[4 + n % 2], (bl0_b, bl1_b)[layer][:, :], ALU.add))
                dve.scalar_tensor_tensor(za[n % 2][:, :], bank[2 + n % 2], rcnt[:, n:n + 1], va[n % 2][:, :],
                                         ALU.mult, ALU.add).then_inc(S["z_made"], 1)

            for n in range(NT):
                if n < KC:
                    lo_part("Wl1", n)
                sage_sum(0, n)
                if n:
                    lo_part("g", n - 1)
            lo_part("g", NT - 1)
            for n in range(NT):
                u_lo_of(1, n)
                if n < KC:
                    lo_part("Wr1", n)
            u_whole(1)
            def stats(n):
                dve.wait_ge(S["x1_made"], n + 1)
                link(dve.bn_stats(bn6[:, n, :], x1[:, n, :]))
                return dve.bn_aggr(mv[:, n, :], bn6[:, n, :])

            for n in range(NT):
                sage_sum(1, n)
                dve.wait_ge(S["z_made"], NT + n + 1)
                dve.wait_ge(x_again[n % 2], 16 * (n // 2 + 1))
                dve.scalar_tensor_tensor(x1[:, n, :], za[n % 2][:, :], 0.0, ht[n % 2][:, :], ALU.max, ALU.add)\
                   .then_inc(S["x1_made"], 1)
                if n < NT - 1:
                    last = stats(n)
                if n < KC:
                    lo_part("W1a", n)
                if n == KC:
                    lo_part("W1b", 0)
                if n == NT - 3:
                    link(last)
                    ln_begin(1)
                    ln_finish(1)
            def lo_of_edges(v):
                dve.wait_ge(S["ea_hi"], v)
                dve.tensor_tensor(eaT_lo[:, :, :], bank[5][:, 0:U * P].rearrange("p (j e) -> p j e", j=U),
                                  eaT_hi[:, :, :].bitcast(f32), ALU.subtract).then_inc(S["ea_lo"], 1)

            def add_gathered(v, next_edges=None):
                for j in range(U):
                    if j == 1 and next_edges is not None:
                        lo_of_edges(next_edges)
                    if j == U - 1:
                        dve.wait_ge(S["msg_made"], v * U + 1)
                        dve.scalar_tensor_tensor(msg_lo[:, :], msg[0][:, :], 0.0, msg_hi[:, :].bitcast(f32),
                                                 ALU.max, ALU.subtract).then_inc(S["msg_lo"], 1)
                    dve.wait_ge(S["q_done"], v * U + (j + 1))
                    dve.wait_ge(S["summed"], v * U + (j + 1))
                    dve.wait_ge(p_gathered[j], v * 16 + 16)
                    if j == 0:
                        dve.wait_ge(S["msg_lo"], v)
                    dve.tensor_tensor(msg[j][:, :], bank[j], gathered[j][:, :], ALU.add).then_inc(S["q_used"], 1)

            def diagonal(c):
                if c >= 2:
                    dve.wait_ge(S["cntb_done"], c - 1)
                dve.tensor_scalar(hot[1 + c % 2][:, :], ident[:, :], cnt[:, c:c + 1], None, ALU.mult)\
                   .then_inc(S["diag_made"], 1)

            def cntb_copy(q):
                w = min(D, NP - q * D)
                dve.wait_ge(S["cntb_done"], min(NT, KC * (q + 1)))
                dve.tensor_copy(cntb[:, q * D:q * D + w], bank[(3, 4, 2)[q]][:, 0:w]).then_inc(S["cntb_out"], 1)

            lo_part("h2", 0)
            lo_part("h2", 1)
            dve.memset(Rtmp[0][:, 0:P], 1.0).then_inc(S["diag_made"], 1)
            diagonal(0)
            link(stats(NT - 1))
            ln_begin(2)
            ln_finish(2)
            for n in range(NT):
                if n >= 1 and n + 1 < NT:
                    lo_part("h2", n + 1)
                if n < KC:
                    lo_part("W2", n)
                if n + 1 < NT:
                    diagonal(n + 1)
                if n == NT - 1:
                    lo_of_edges(1)
                dve.wait_ge(S["p_done"], n + 1)
                if n >= 2:
                    dve.wait_ge(p_stored[n % 2], 16 * (n // 2))
                dve.tensor_tensor(va[n % 2][:, :], bank[n % 2], b1_b[:, :], ALU.add).then_inc(S["p_made"], 1)
                if n == KC:
                    dve.wait_ge(S["gate_bias"], 64)
                    dve.tensor_tensor(br_b[:, :], br_b[:, :], za[0][:, :], ALU.add)
                    link(dve.tensor_tensor(bz_b[:, :], bz_b[:, :], za[1][:, :], ALU.add))
                    cntb_copy(0)
                if n == 2 * KC:
                    cntb_copy(1)
            cntb_copy(2)
            lo_of_edges(2)
            for k in range(KC):
                lo_part("ih_r", k)


            add_gathered(1)
            for c in range(NT):
                base, v0, v1 = visits.of(c)
                with dve.Fori(v0, v1) as v:
                    t = first_tile(dve, v, base)
                    dve.wait_ge(S["summed"], v * U + U)
                    for j in range(U):
                        last = dve.tensor_scalar(hot[j][:, :], iota[:, c * P:(c + 1) * P],
                                                 dstF[:, bass.ds(t + j, 1)], None, ALU.is_equal)
                    last.then_inc(S["hot_made"], 1)
                    add_gathered(v + 1, next_edges=v + 2)
                if c >= 2:
                    lo_part("R", c - 2)
            lo_part("R", NT - 2)
            def agg_lo(i):
                nb, oc = i // KC, i % KC
                w = min(D, NP - nb * D)
                dve.wait_ge(S["agg_hi"], i + 1)
                dve.tensor_tensor(RT_lo[:, oc, nb * D:nb * D + w], ta[i % 2][:, 0:w],
                                  RT_hi[:, oc, nb * D:nb * D + w].bitcast(f32), ALU.subtract)\
                   .then_inc(S["agg_lo"], 1)

            for i in range(3 * KC):
                nb, oc = i // KC, i % KC
                w = min(D, NP - nb * D)
                dve.wait_ge(S["agg_done"], i + 1)
                if i >= 2:
                    dve.wait_ge(S["agg_lo"], i - 1)
                dve.scalar_tensor_tensor(ta[i % 2][:, 0:w], cntb[:, nb * D:nb * D + w], b2col[:, oc:oc + 1],
                                         bank[i % 6][:, 0:w], ALU.mult, ALU.add).then_inc(S["agg_f"], 1)
                if i == 1:
                    lo_part("R", NT - 1)
                    lo_part("hh_r", 0)
                    lo_part("hh_r", 1)
                if i:
                    agg_lo(i - 1)
                if i in (3, 4):
                    lo_part("hh_r", i - 1)
            agg_lo(3 * KC - 1)

            for n in range(NT):
                dve.wait_ge(S["r_done"], n + 1)
                if n >= 2:
                    dve.wait_ge(S["r_made"], n - 1)
                dve.tensor_tensor(tb[n % 2][:, :], bank[n % 2], br_b[:, :], ALU.add).then_inc(S["r_sum"], 1)
                if n < KC:
                    lo_part("ih_n", n)
            for k in range(KC):
                lo_part("hh_n", k)

            dve.wait_ge(S["n_bias_loaded"], 32)
            def n_sum(n):
                dve.wait_ge(S["n_bias"], n + 1)
                if n >= 2:
                    dve.wait_ge(S["n_made"], n - 1)
                dve.tensor_tensor(te[n % 2][:, :], bank[2 + n % 2], ta[n % 2][:, :], ALU.add).then_inc(S["n_sum"], 1)

            for n in range(NT):
                if n:
                    n_sum(n - 1)
                dve.wait_ge(S["n_done"], n + 1)
                if n >= 2:
                    dve.wait_ge(S["n_sum"], n - 1)
                dve.tensor_tensor(ta[n % 2][:, :], bank[4 + n % 2], bhn_b[:, :], ALU.add).then_inc(S["n_hn"], 1)
                if 1 <= n <= KC:
                    lo_part("ih_z", n - 1)
            lo_part("hh_z", 0)
            lo_part("hh_z", 1)
            n_sum(NT - 1)
            lo_part("hh_z", 2)
            lo_part("hh_z", 3)

            def z_finish(n):
                dve.wait_ge(S["z_gate"], n + 1)
                dve.wait_ge(S["z_diff"], n + 1)
                dve.tensor_tensor(tb[n % 2][:, :], tb[n % 2][:, :], td[n % 2][:, :], ALU.mult)\
                   .then_inc(S["z_mul"], 1)
                dve.wait_ge(S["z_mul"], n + 1)
                link(dve.tensor_tensor(tb[n % 2][:, :], tb[n % 2][:, :], rn[:, n, :], ALU.add))
                link(dve.tensor_tensor(tb[n % 2][:, :], tb[n % 2][:, :], G_b[:, :], ALU.mult))
                dve.wait_ge(S["z_base"], n + 1)
                if n >= 2:
                    dve.wait_ge(out_stored[n % 2], 16 * (n // 2))
                dve.tensor_tensor(tc[n % 2][:, :], tb[n % 2][:, :], tf[n % 2][:, :], ALU.add)\
                   .then_inc(S["z_out"], 1)

            for n in range(NT):
                dve.wait_ge(S["z_done"], n + 1)
                if n >= 2:
                    dve.wait_ge(S["z_out"], n - 1)
                dve.tensor_tensor(tb[n % 2][:, :], bank[n % 2], bz_b[:, :], ALU.add).then_inc(S["z_sum"], 1)
                if n:
                    z_finish(n - 1)
            z_finish(NT - 1)

        @block.tensor
        def _(pe):
            pe.wait_ge(S["pool_chain"], 2)
            pe.wait_ge(S["ends_made"], 1)
            two = TC - P
            for q, (lo, hi) in enumerate(((0, 2), (1, 3))):
                pe.matmul(psT[1][0:16, q * 256:q * 256 + P], ends16[:, lo, :], ident[:, :], start=True, stop=True)
                last = pe.matmul(psT[1][0:16, q * 256 + P:q * 256 + ET], ends16[0:ROWS2, hi, :],
                                 ident[0:ROWS2, 0:ROWS2], start=True, stop=True)
            last.then_inc(S["ends_bcast"], 1)
            for q, rows_f in enumerate((dst_f, src_f)):
                pe.transpose(psT[0][:, q * 256:q * 256 + P], rows_f[:, 0, :], ident[:, :])
                last = pe.transpose(psT[0][:, q * 256 + P:q * 256 + TC], rows_f[0:two, 1, :], ident[0:two, 0:two])
            last.then_inc(S["tables"], 1)
            pe.wait_ge(S["reach_made"], 1)
            pe.transpose(psT[1][0:1, 0:16], reach[:, 0:1], ident[0:16, 0:16])
            pe.transpose(psT[1][0:1, 16:32], reach[:, 3:4], ident[0:16, 0:16]).then_inc(S["reach_T"], 1)

            def job(name, k):
                j = JOB[(name, k)]
                if j >= 2:
                    pe.wait_ge(S["tr_lo"], j - 1)
                if name in STAGED and k == 0:
                    pe.wait_ge(S["staged"], 16 * (STAGED.index(name) + 1))
                for b in range(KC):
                    if name == "h" or name == "g":
                        i = ht[k % 2][:, b * P:(b + 1) * P]
                    elif name == "h2":
                        i = h2[:, k, b * P:(b + 1) * P]
                    elif name == "R":
                        i = Rtmp[k % 2][:, b * P:(b + 1) * P]
                    elif name == "W1b":
                        i = stage[:, b, D:D + ED]
                    else:
                        i = stage[:, b, k * P:(k + 1) * P]
                    last = pe.transpose(psT[j % 2][:, b * P:(b + 1) * P], i, ident[:, :])
                last.then_inc(S["tr_pe"], 1)

            def product(o, lhs, rhs, start=True, stop=True):
                for kc in range(KC):
                    for p, (a, b) in enumerate(((0, 0), (0, 1), (1, 0))):
                        last = pe.matmul(o, lhs[a](kc), rhs[b](kc), start=start and kc == 0 and p == 0,
                                         stop=stop and kc == KC - 1 and p == 2)
                return last

            def nodes(t, n):
                if t is RT:
                    return tuple((lambda kc, y=y: y[:, kc, n * P:(n + 1) * P]) for y in t)
                return tuple((lambda kc, y=y: y[:, n, kc * P:(kc + 1) * P]) for y in t)

            def weights(name):
                return tuple((lambda kc, y=y: y[:, kc, :]) for y in slot[SLOT[name]])

            hT, RT = (hT_hi, hT_lo), (RT_hi, RT_lo)

            pe.wait_ge(S["tab_ready"], 1)
            visits = Visits(pe)
            pe.wait_ge(S["const"], 2)
            pe.wait_ge(S["tile_tables"], 1)
            pe.sem_inc(S["hot_used"], 2 * U)
            pe.sem_inc(S["hot_ready"], U)
            for c in range(NT):
                if c >= 2:
                    pe.wait_ge(S["counts_out"], c - 1)
                A = psA[c % 2]
                for q in range(3):
                    pe.matmul(A[:, q * D:(q + 1) * D], zeros16[:, 0:P], zeros16[:, :], start=True, stop=False)
                base, v0, v1 = visits.of(c)
                with pe.Fori(v0, v1) as v:
                    for j in range(U):
                        pe.wait_ge(S["hot_ready"], v * U + (j + 1))
                        for s in range(NT):
                            pe.matmul(A[:, s * P:(s + 1) * P], hot_src[j][:, s * P:(s + 1) * P], hot_dst[j][:, :],
                                      start=False, stop=False)
                        pe.matmul(A[:, NP:NP + 1], hot_dst[j][:, :], ones16[:, :], start=False, stop=False)\
                          .then_inc(S["hot_used"], 1)
                for q in range(3):
                    last = pe.matmul(A[:, q * D:(q + 1) * D], zeros16[:, 0:P], zeros16[:, :], start=False, stop=True)
                last.then_inc(S["counts_done"], 1)
                if c < 2 * KC:
                    job(("Wl0", "Wr0")[c // KC], c % KC)
                if c >= 2:
                    pe.wait_ge(S["h_made"], c - 1)
                    job("h", c - 2)

            def product_u(layer, n):
                i = layer * NT + n
                if i >= 2:
                    pe.wait_ge(S["u_lo"], i - 1)
                pe.wait_ge(S["tr_lo"], JOB[(("h", "g")[layer], n)] + 1)
                product(bank[n % 2], nodes(hT, n), weights(f"Wl{layer}")).then_inc(S["u_done"], 1)

            def product_sv(layer, n):
                i = layer * NT + n
                if n == 0:
                    pe.wait_ge(S["tr_lo"], LAST_JOB[f"Wr{layer}"] + 1)
                    pe.wait_ge(S["counts_out"], NT)
                if i >= 2:
                    pe.wait_ge(S["z_made"], i - 1)
                product(bank[4 + n % 2], nodes(hT, n), weights(f"Wr{layer}"))
                if n == 0:
                    pe.wait_ge(S["u_whole"], layer + 1)
                o = bank[2 + n % 2]
                with pe.If(exact > 0):
                    for s in range(NT):
                        last = pe.matmul(o, AT[:, s, n * P:(n + 1) * P], u_all[:, s, :],
                                         start=s == 0, stop=s == NT - 1)
                    last.then_inc(S["sv_done"], 1)
                with pe.Else():
                    for s in range(NT):
                        pe.matmul(o, AT_r[:, s, n * P:(n + 1) * P], u_hi[:, s, :], start=s == 0, stop=False)
                        last = pe.matmul(o, AT_r[:, s, n * P:(n + 1) * P], u_lo[:, s, :],
                                         start=False, stop=s == NT - 1)
                    last.then_inc(S["sv_done"], 1)

            pe.wait_ge(S["counts_out"], NT - 1)
            for n in range(NT):
                product_u(0, n)
                if n < 2:
                    pe.wait_ge(S["h_made"], NT - 1 + n)
                    job("h", NT - 2 + n)
            exact = pe.value_load(tab[0:1, 27:28], min_val=0, max_val=1)
            for n in range(NT):
                if n < KC:
                    job("Wl1", n)
                product_sv(0, n)
                if n:
                    pe.wait_ge(S["g_made"], n)
                    job("g", n - 1)
            for n in range(NT):
                product_u(1, n)
                if n == 0:
                    pe.wait_ge(S["g_made"], NT)
                    job("g", NT - 1)
                if n < KC:
                    job("Wr1", n)
            for n in range(NT):
                if n < KC:
                    job("W1a", n)
                if n == KC:
                    job("W1b", 0)
                product_sv(1, n)
            def transpose_edges(v):
                for j in range(U):
                    pe.wait_ge(ea_loaded[j], v * 16)
                    if j == 0:
                        pe.wait_ge(S["ea_lo"], v)
                    last = pe.transpose(bank[5][:, j * P:(j + 1) * P], ea[j][:, :], ident[:, :])
                last.then_inc(S["ea_T"], 1)

            def multiply_edges(v, tiles=range(U)):
                if 0 in tiles:
                    pe.wait_ge(S["ea_lo"], v + 1)
                for j in tiles:
                    pe.wait_ge(S["q_used"], v * U + (j + 1))
                    pe.matmul(bank[j], eaT_hi[:, j, :], W1b_hi[:, :], start=True, stop=False)
                    pe.matmul(bank[j], eaT_hi[:, j, :], W1b_lo[:, :], start=False, stop=False)
                    pe.matmul(bank[j], eaT_lo[:, j, :], W1b_hi[:, :], start=False, stop=True)\
                      .then_inc(S["q_done"], 1)

            pe.sem_inc(S["ea_T"], 1)
            pe.sem_inc(S["ea_lo"], 1)
            pe.sem_inc(S["q_done"], U)
            pe.sem_inc(S["q_used"], 2 * U)
            pe.sem_inc(S["summed"], 2 * U)
            pe.sem_inc(S["msg_made"], U)
            pe.sem_inc(S["idx_made"], U)
            pe.sem_inc(S["msg_lo"], 1)

            def job_h2(n):
                pe.wait_ge(S["h2_made"], n + 1)
                job("h2", n)
            job_h2(0)
            for n in range(NT):
                if n + 1 < NT:
                    job_h2(n + 1)
                if n < KC:
                    job("W2", n)
                pe.wait_ge(S["tr_lo"], JOB[("h2", n)] + 1)
                if n >= 2:
                    pe.wait_ge(S["p_made"], n - 1)
                product(bank[n % 2], nodes(hT, n), weights("W1a")).then_inc(S["p_done"], 1)
                pe.wait_ge(S["diag_made"], n + 2)
                pe.matmul(bank[(3, 4, 2)[n // KC]][:, (n % KC) * P:(n % KC + 1) * P], Rtmp[0][:, 0:P],
                          hot[1 + n % 2][:, :], start=True, stop=True).then_inc(S["cntb_done"], 1)
                if n == NT - 2:
                    transpose_edges(1)
            pe.wait_ge(S["p_made"], NT)
            pe.wait_ge(S["cntb_out"], 3)
            multiply_edges(1)
            transpose_edges(2)
            for k in range(KC):
                job("ih_r", k)
            pe.wait_ge(S["const"], 3)
            for c in range(NT):
                if c >= 2:
                    pe.wait_ge(S["R_out"], c - 1)
                R = bank[3 + c % 2]
                pe.matmul(R, zeros[:, 0:P], zeros[:, :], start=True, stop=False)
                base, v0, v1 = visits.of(c)
                with pe.Fori(v0, v1) as v:
                    multiply_edges(v + 1, range(U - 1))
                    transpose_edges(v + 2)
                    multiply_edges(v + 1, range(U - 1, U))
                    pe.wait_ge(S["hot_made"], v)
                    for j in range(U):
                        pe.wait_ge(S["msg_made"], v * U + (j + 1))
                        if j == 0:
                            pe.wait_ge(S["msg_lo"], v + 1)
                            pe.matmul(R, hot[0][:, :], msg_hi[:, :], start=False, stop=False)
                            last = pe.matmul(R, hot[0][:, :], msg_lo[:, :], start=False, stop=False)
                        else:
                            last = pe.matmul(R, hot[j][:, :], msg[j][:, :], start=False, stop=False)
                        last.then_inc(S["summed"], 1)
                pe.matmul(R, zeros[:, 0:P], zeros[:, :], start=False, stop=True).then_inc(S["R_done"], 1)
                if c:
                    pe.wait_ge(S["R_out"], c)
                    job("R", c - 1)
            w2 = slot[SLOT["W2"]]
            pe.wait_ge(S["q_used"], visits.at[NT] * U + 2 * U)
            for i in range(3 * KC):
                nb, oc = i // KC, i % KC
                w = min(D, NP - nb * D)
                if i == 0:
                    pe.wait_ge(S["tr_lo"], JOB[("R", KC - 1)] + 1)
                if i == KC:
                    pe.wait_ge(S["tr_lo"], JOB[("R", NT - 2)] + 1)
                if i == 2 * KC:
                    pe.wait_ge(S["tr_lo"], JOB[("R", NT - 1)] + 1)
                if i >= 6:
                    pe.wait_ge(S["agg_f"], i - 5)
                product(bank[i % 6][:, 0:w], tuple((lambda kc, y=y: y[:, kc, oc * P:(oc + 1) * P]) for y in w2),
                        tuple((lambda kc, y=y: y[:, kc, nb * D:nb * D + w]) for y in RT)).then_inc(S["agg_done"], 1)
                if i == 1:
                    pe.wait_ge(S["R_out"], NT)
                    job("R", NT - 1)
                if 2 <= i < 2 + KC:
                    job("hh_r", i - 2)
            def r_state(n):
                if n >= 2:
                    pe.wait_ge(S["r_sum"], n - 1)
                product(bank[n % 2], nodes(hT, n), weights("hh_r"), stop=False)

            pe.wait_ge(S["tr_lo"], LAST_JOB["hh_r"] + 1)
            pe.wait_ge(S["agg_f"], 8)
            r_state(0)
            r_state(1)
            pe.wait_ge(S["agg_f"], 3 * KC)
            pe.wait_ge(S["agg_lo"], 3 * KC)
            for n in range(NT):
                if n >= 2:
                    r_state(n)
                product(bank[n % 2], nodes(RT, n), weights("ih_r"), start=False).then_inc(S["r_done"], 1)
                if n < KC:
                    job("ih_n", n)
            def n_input(n):
                if n >= 2:
                    pe.wait_ge(S["n_sum"], n - 1)
                product(bank[2 + n % 2], nodes(RT, n), weights("ih_n"))

            for n in range(2):
                job("hh_n", 2 * n)
                job("hh_n", 2 * n + 1)
                n_input(n)
            pe.wait_ge(S["tr_lo"], LAST_JOB["hh_n"] + 1)
            for n in range(NT):
                if n >= 2:
                    n_input(n)
                product(bank[4 + n % 2], nodes(hT, n), weights("hh_n")).then_inc(S["n_done"], 1)
                if n < KC:
                    job("ih_z", n)

            def z_input(n):
                if n >= 2:
                    pe.wait_ge(S["z_sum"], n - 1)
                product(bank[n % 2], nodes(RT, n), weights("ih_z"), stop=False)

            pe.wait_ge(S["r_sum"], NT)
            for n in range(2):
                job("hh_z", 2 * n)
                job("hh_z", 2 * n + 1)
                z_input(n)
            pe.wait_ge(S["tr_lo"], LAST_JOB["hh_z"] + 1)
            for n in range(NT):
                if n >= 2:
                    z_input(n)
                product(bank[n % 2], nodes(hT, n), weights("hh_z"), start=False).then_inc(S["z_done"], 1)


_INS = ['x', 'src', 'dst', 'edge_attr_128', 'L0_gnn_Wl0', 'L0_gnn_bl0', 'L0_gnn_Wr0', 'L0_gnn_Wl1', 'L0_gnn_bl1',
        'L0_gnn_Wr1', 'L1_gnn_W1', 'L1_gnn_b1', 'L1_gnn_W2', 'L1_gnn_b2', 'L1_gnn_W_ih', 'L1_gnn_W_hh',
        'L1_gnn_b_ih', 'L1_gnn_b_hh', 'L1_gnn_gamma', 'L1_gnn_beta', 'L1_gnn_run_mean', 'L1_gnn_run_var']


def kernel(**inputs):
    import numpy as _np
    import concourse.bacc as _bacc
    from concourse import mybir as _mybir
    from concourse.bass_utils import run_bass_kernel_spmd as _run

    nc = _bacc.Bacc("TRN2", target_bir_lowering=False, num_devices=1)
    arrays, args = {}, []
    for name in _INS:
        a = _np.ascontiguousarray(inputs[name])
        arrays[f"in_{name}"] = a
        args.append(nc.dram_tensor(f"in_{name}", a.shape, _mybir.dt.from_np(a.dtype), kind="ExternalInput").ap())
    f32 = _mybir.dt.float32
    args.append(nc.dram_tensor("out_0", (N, D), f32, kind="ExternalOutput").ap())
    args.append(nc.dram_tensor("p_table", (NP, D), f32, kind="Internal").ap())
    args.append(nc.dram_tensor("h_stash", (P, NT, D), f32, kind="Internal").ap())
    args.append(nc.dram_tensor("xh_stash", (P, NT, D), f32, kind="Internal").ap())
    build_gnn(nc, *args)
    r = _run(nc, [arrays], core_ids=[0])
    return r.results[0]["out_0"]
```
